# Optimizing a Trainium2 kernel written in Bass

```python
import numpy as np
import jax
import jax.numpy as jnp

def _softmax(x, axis=-1):
    return jax.nn.softmax(x, axis=axis)

def _gelu(x):
    return jax.nn.gelu(x, approximate=True)

def _silu(x):
    return jax.nn.silu(x)

def _sigmoid(x):
    return jax.nn.sigmoid(x)

def _layernorm(x, axis=-1, eps=1e-05):
    m = jnp.mean(x, axis=axis, keepdims=True)
    v = jnp.var(x, axis=axis, keepdims=True)
    return (x - m) / jnp.sqrt(v + eps)

def _scatter_add(tgt, idx, src, axis=0):
    return tgt.at[idx].add(src)

def _segment_sum(src, seg, n):
    return jax.ops.segment_sum(src, seg, n)
kernel_name = 'mk_vit_tower_cls_d1_tok_img512_r4_04ffef'

def setup_inputs(seed: int=0):
    np.random.seed(seed)
    _w = jnp.asarray

    def _rec_inputs():
        import jax
        import jax.numpy as jnp
        _rk = jax.random.key(seed)
        x = -0.000190493 + 0.999948 * jax.random.normal(jax.random.fold_in(_rk, 1), (64, 2, 104, 104), jnp.float32)
        cls_tok = 0.02 * jax.random.normal(jax.random.fold_in(_rk, 5), (1, 1, 128), jnp.float32)
        return (x, cls_tok)
    x, cls_tok = _rec_inputs()

    def _L0_tok_setup():
        import jax, jax.numpy as jnp
        import numpy as np
        HP = 4
        PATCH = 8
        EPS = 1e-07

        def _shifts(x):
            h, w = (x.shape[2], x.shape[3])
            pad2 = ((0, 0), (0, 0))
            left_up = jnp.pad(x[:, :, HP:, :w - HP], pad2 + ((0, HP), (HP, 0)))
            right_up = jnp.pad(x[:, :, HP:, HP:], pad2 + ((0, HP), (0, HP)))
            left_down = jnp.pad(x[:, :, :h - HP, :w - HP], pad2 + ((HP, 0), (HP, 0)))
            right_down = jnp.pad(x[:, :, :h - HP, HP:], pad2 + ((HP, 0), (0, HP)))
            return (left_up, right_up, left_down, right_down)
        key = jax.random.key(seed)
        k1, k2, k3, k4 = jax.random.split(key, 4)
        B, C, S = (128, 2, 104)
        embed_dim = 128
        x = jax.random.normal(k1, (B, C, S, S), dtype=jnp.float32)
        gamma = 1.0 + 0.05 * jax.random.normal(k2, (10, S, S), dtype=jnp.float32)
        beta = 0.05 * jax.random.normal(k3, (10, S, S), dtype=jnp.float32)
        W = 0.02 * jax.random.normal(k4, (embed_dim, 10, PATCH, PATCH), dtype=jnp.float32)
        b = jnp.zeros((embed_dim,), dtype=jnp.float32)
        return {'x': x, 'gamma': gamma, 'beta': beta, 'W': W, 'b': b}
    _L0_tok_all = _L0_tok_setup()
    _L0_tok_in = {k: v for k, v in _L0_tok_all.items() if k in ('gamma', 'beta', 'W', 'b')}
    del _L0_tok_all

    def _L0_attn_setup():
        import jax, jax.numpy as jnp
        import numpy as np

        def _gcn_norm(edge_index, n_nodes):
            loops = jnp.arange(n_nodes, dtype=edge_index.dtype)
            src = jnp.concatenate([edge_index[0], loops])
            dst = jnp.concatenate([edge_index[1], loops])
            deg = jnp.zeros((n_nodes,), jnp.float32).at[dst].add(1.0)
            dinv = jnp.where(deg > 0, jax.lax.rsqrt(deg), 0.0)
            norm = dinv[src] * dinv[dst]
            return (src, dst, norm)

        def _gcn_conv(h, W, b, src, dst, norm):
            m = h.shape[0]
            hw = h @ W
            msgs = hw[:, src, :] * norm[None, :, None]
            agg = jnp.zeros((m, h.shape[1], W.shape[1]), hw.dtype).at[:, dst, :].add(msgs)
            return agg + b
        key = jax.random.key(seed)
        ks = jax.random.split(key, 12)
        B, T, N, E, C = (32, 128, 128, 1024, 4)
        pred_len, n_marks = (64, 4)
        return {'x_enc': jax.random.normal(ks[0], (B, T, N), jnp.float32), 'x_mark_enc': jax.random.normal(ks[1], (B, T, n_marks), jnp.float32), 'x_dec': jax.random.normal(ks[2], (B, pred_len, N), jnp.float32), 'x_mark_dec': jax.random.normal(ks[3], (B, pred_len, n_marks), jnp.float32), 'edge_index': jax.random.randint(ks[4], (2, E), 0, N, jnp.int64 if jax.config.jax_enable_x64 else jnp.int32), 'W1': jax.random.normal(ks[5], (1, C), jnp.float32) * 0.1, 'b1': jax.random.normal(ks[6], (C,), jnp.float32) * 0.1, 'W2': jax.random.normal(ks[7], (C, C), jnp.float32) * 0.1, 'b2': jax.random.normal(ks[8], (C,), jnp.float32) * 0.1, 'Wp': jax.random.normal(ks[9], (N, N * (1 + C)), jnp.float32) * 0.02, 'bp': jax.random.normal(ks[10], (N,), jnp.float32) * 0.02}
    _L0_attn_all = _L0_attn_setup()
    _L0_attn_in = {k: v for k, v in _L0_attn_all.items() if k in ('x_mark_enc', 'x_dec', 'x_mark_dec', 'edge_index', 'W1', 'b1', 'W2', 'b2', 'Wp', 'bp')}
    del _L0_attn_all

    def _L0_ffn_setup():
        import jax, jax.numpy as jnp
        import numpy as np
        B, N, DIM = (1, 512, 128)
        DH, H = (64, 8)
        E, FF = (8, 512)

        def _layernorm(x, g, b, eps=1e-05):
            mu = jnp.mean(x, axis=-1, keepdims=True)
            var = jnp.mean(jnp.square(x - mu), axis=-1, keepdims=True)
            return (x - mu) * jax.lax.rsqrt(var + eps) * g + b

        def _l2norm(x, eps=1e-12):
            return x / jnp.sqrt(jnp.sum(jnp.square(x), axis=-1, keepdims=True) + eps)
        key = jax.random.key(seed)
        ks = jax.random.split(key, 12)
        g = lambda k, shape: jax.random.normal(k, shape, jnp.float32) * 0.02
        return {'x': jax.random.normal(ks[0], (B, N, DIM), jnp.float32), 'ln_g': jnp.ones((DIM,), jnp.float32), 'ln_b': jnp.zeros((DIM,), jnp.float32), 'Wq': g(ks[1], (DIM, DIM)), 'Wk': g(ks[2], (DIM, DIM)), 'Wv': g(ks[3], (DIM, DIM)), 'Wo': g(ks[4], (DIM, DIM)), 'qn_g': jnp.ones((DH,), jnp.float32), 'kn_g': jnp.ones((DH,), jnp.float32), 'gate_W': g(ks[5], (DIM, E)), 'gate_b': jnp.zeros((E,), jnp.float32), 'W1': g(ks[6], (E, DIM, FF)), 'b1': jnp.zeros((E, FF), jnp.float32), 'W2': g(ks[7], (E, FF, DIM)), 'b2': jnp.zeros((E, DIM), jnp.float32)}
    _L0_ffn_all = _L0_ffn_setup()
    _L0_ffn_in = {k: v for k, v in _L0_ffn_all.items() if k in ('ln_g', 'ln_b', 'Wq', 'Wk', 'Wv', 'Wo', 'qn_g', 'kn_g', 'gate_W', 'gate_b', 'W1', 'b1', 'W2', 'b2')}
    del _L0_ffn_all
    return {'x': x, 'cls_tok': cls_tok, 'L0_tok_gamma': _L0_tok_in['gamma'], 'L0_tok_beta': _L0_tok_in['beta'], 'L0_tok_W': _L0_tok_in['W'], 'L0_tok_b': _L0_tok_in['b'], 'L0_attn_x_mark_enc': _L0_attn_in['x_mark_enc'], 'L0_attn_x_dec': _L0_attn_in['x_dec'], 'L0_attn_x_mark_dec': _L0_attn_in['x_mark_dec'], 'L0_attn_edge_index': _L0_attn_in['edge_index'], 'L0_attn_W1': _L0_attn_in['W1'], 'L0_attn_b1': _L0_attn_in['b1'], 'L0_attn_W2': _L0_attn_in['W2'], 'L0_attn_b2': _L0_attn_in['b2'], 'L0_attn_Wp': _L0_attn_in['Wp'], 'L0_attn_bp': _L0_attn_in['bp'], 'L0_ffn_ln_g': _L0_ffn_in['ln_g'], 'L0_ffn_ln_b': _L0_ffn_in['ln_b'], 'L0_ffn_Wq': _L0_ffn_in['Wq'], 'L0_ffn_Wk': _L0_ffn_in['Wk'], 'L0_ffn_Wv': _L0_ffn_in['Wv'], 'L0_ffn_Wo': _L0_ffn_in['Wo'], 'L0_ffn_qn_g': _L0_ffn_in['qn_g'], 'L0_ffn_kn_g': _L0_ffn_in['kn_g'], 'L0_ffn_gate_W': _L0_ffn_in['gate_W'], 'L0_ffn_gate_b': _L0_ffn_in['gate_b'], 'L0_ffn_W1': _L0_ffn_in['W1'], 'L0_ffn_b1': _L0_ffn_in['b1'], 'L0_ffn_W2': _L0_ffn_in['W2'], 'L0_ffn_b2': _L0_ffn_in['b2']}

def reference(x, cls_tok, L0_tok_gamma, L0_tok_beta, L0_tok_W, L0_tok_b, L0_attn_x_mark_enc, L0_attn_x_dec, L0_attn_x_mark_dec, L0_attn_edge_index, L0_attn_W1, L0_attn_b1, L0_attn_W2, L0_attn_b2, L0_attn_Wp, L0_attn_bp, L0_ffn_ln_g, L0_ffn_ln_b, L0_ffn_Wq, L0_ffn_Wk, L0_ffn_Wv, L0_ffn_Wo, L0_ffn_qn_g, L0_ffn_kn_g, L0_ffn_gate_W, L0_ffn_gate_b, L0_ffn_W1, L0_ffn_b1, L0_ffn_W2, L0_ffn_b2):
    import jax
    import jax.numpy as jnp

    def _L0_tok_ref(x, gamma, beta, W, b):
        import jax, jax.numpy as jnp
        import numpy as np
        HP = 4
        PATCH = 8
        EPS = 1e-07

        def _shifts(x):
            h, w = (x.shape[2], x.shape[3])
            pad2 = ((0, 0), (0, 0))
            left_up = jnp.pad(x[:, :, HP:, :w - HP], pad2 + ((0, HP), (HP, 0)))
            right_up = jnp.pad(x[:, :, HP:, HP:], pad2 + ((0, HP), (0, HP)))
            left_down = jnp.pad(x[:, :, :h - HP, :w - HP], pad2 + ((HP, 0), (HP, 0)))
            right_down = jnp.pad(x[:, :, :h - HP, HP:], pad2 + ((HP, 0), (0, HP)))
            return (left_up, right_up, left_down, right_down)
        lu, ru, ld, rd = _shifts(x)
        concat = jnp.concatenate((x, lu, ru, ld, rd), axis=1)
        mean = jnp.mean(concat, axis=(1, 2, 3), keepdims=True)
        var = jnp.var(concat, axis=(1, 2, 3), keepdims=True)
        normed = (concat - mean) * jax.lax.rsqrt(var + EPS)
        normed = normed * gamma[None] + beta[None]
        y = jax.lax.conv_general_dilated(normed, W, window_strides=(PATCH, PATCH), padding='VALID', dimension_numbers=('NCHW', 'OIHW', 'NCHW'))
        y = y + b[None, :, None, None]
        B, E = (y.shape[0], y.shape[1])
        y = y.reshape(B, E, -1).transpose(0, 2, 1)
        return y

    def _L0_attn_ref(x_enc, x_mark_enc, x_dec, x_mark_dec, edge_index, W1, b1, W2, b2, Wp, bp):
        import jax, jax.numpy as jnp
        import numpy as np

        def _gcn_norm(edge_index, n_nodes):
            loops = jnp.arange(n_nodes, dtype=edge_index.dtype)
            src = jnp.concatenate([edge_index[0], loops])
            dst = jnp.concatenate([edge_index[1], loops])
            deg = jnp.zeros((n_nodes,), jnp.float32).at[dst].add(1.0)
            dinv = jnp.where(deg > 0, jax.lax.rsqrt(deg), 0.0)
            norm = dinv[src] * dinv[dst]
            return (src, dst, norm)

        def _gcn_conv(h, W, b, src, dst, norm):
            m = h.shape[0]
            hw = h @ W
            msgs = hw[:, src, :] * norm[None, :, None]
            agg = jnp.zeros((m, h.shape[1], W.shape[1]), hw.dtype).at[:, dst, :].add(msgs)
            return agg + b
        B, T, N = x_enc.shape
        src, dst, norm = _gcn_norm(edge_index, N)
        x = x_enc.reshape(B * T, N, 1)
        h = jax.nn.relu(_gcn_conv(x, W1, b1, src, dst, norm))
        h = _gcn_conv(h, W2, b2, src, dst, norm)
        gcn_output = h.reshape(B, T, N, -1)
        x_combined = jnp.concatenate([x_enc[..., None], gcn_output], axis=-1)
        x_combined = x_combined.reshape(B, T, -1)
        x_projected = x_combined @ Wp.T + bp
        return x_projected

    def _L0_ffn_ref(x, ln_g, ln_b, Wq, Wk, Wv, Wo, qn_g, kn_g, gate_W, gate_b, W1, b1, W2, b2):
        import jax, jax.numpy as jnp
        import numpy as np
        B, N, DIM = (1, 512, 128)
        DH, H = (64, 8)
        E, FF = (8, 512)

        def _layernorm(x, g, b, eps=1e-05):
            mu = jnp.mean(x, axis=-1, keepdims=True)
            var = jnp.mean(jnp.square(x - mu), axis=-1, keepdims=True)
            return (x - mu) * jax.lax.rsqrt(var + eps) * g + b

        def _l2norm(x, eps=1e-12):
            return x / jnp.sqrt(jnp.sum(jnp.square(x), axis=-1, keepdims=True) + eps)
        b, n, d = x.shape
        dh = qn_g.shape[0]
        h = d // dh
        hx = _layernorm(x, ln_g, ln_b)
        q = (hx @ Wq).reshape(b, n, h, dh).transpose(0, 2, 1, 3)
        k = (hx @ Wk).reshape(b, n, h, dh).transpose(0, 2, 1, 3)
        v = (hx @ Wv).reshape(b, n, h, dh).transpose(0, 2, 1, 3)
        scale = jnp.sqrt(jnp.float32(dh))
        q = _l2norm(q) * scale * qn_g
        k = _l2norm(k) * scale * kn_g
        scores = jnp.einsum('bhqd,bhkd->bhqk', q, k) * dh ** (-0.5)
        causal = jnp.tril(jnp.ones((n, n), bool))
        scores = jnp.where(causal, scores, jnp.finfo(scores.dtype).min)
        attn = jax.nn.softmax(scores, axis=-1)
        o = jnp.einsum('bhqk,bhkd->bhqd', attn, v)
        y = o.transpose(0, 2, 1, 3).reshape(b, n, d) @ Wo
        gate = jax.nn.softmax(y @ gate_W + gate_b, axis=-1)
        hid = jax.nn.gelu(jnp.einsum('bnd,edf->bnef', y, W1) + b1)
        eo = jnp.einsum('bnef,efd->bned', hid, W2) + b2
        out = jnp.einsum('bned,bne->bnd', eo, gate)
        return out
    h = _L0_tok_ref(x, L0_tok_gamma, L0_tok_beta, L0_tok_W, L0_tok_b)
    h = jnp.concatenate([jnp.broadcast_to(cls_tok, (h.shape[0], 1, h.shape[2])), h], axis=1)
    h = h + _L0_attn_ref(_layernorm(h, axis=-1), L0_attn_x_mark_enc, L0_attn_x_dec, L0_attn_x_mark_dec, L0_attn_edge_index, L0_attn_W1, L0_attn_b1, L0_attn_W2, L0_attn_b2, L0_attn_Wp, L0_attn_bp)
    h = h + _L0_ffn_ref(_layernorm(h, axis=-1), L0_ffn_ln_g, L0_ffn_ln_b, L0_ffn_Wq, L0_ffn_Wk, L0_ffn_Wv, L0_ffn_Wo, L0_ffn_qn_g, L0_ffn_kn_g, L0_ffn_gate_W, L0_ffn_gate_b, L0_ffn_W1, L0_ffn_b1, L0_ffn_W2, L0_ffn_b2)
    return h

_drawn_inputs = setup_inputs


def setup_inputs(seed=0):
    import zlib

    import numpy as np

    out = dict(_drawn_inputs(seed))
    spreads = {'L0_tok_b': (0.0, 0.1),
     'L0_ffn_ln_g': (1.0, 0.6),
     'L0_ffn_ln_b': (0.0, 0.8),
     'L0_ffn_qn_g': (1.0, 0.6),
     'L0_ffn_kn_g': (1.0, 0.6),
     'L0_ffn_gate_b': (0.0, 0.8),
     'L0_ffn_b1': (0.0, 0.603),
     'L0_ffn_b2': (0.0, 0.69)}
    factors = {'L0_attn_W1': 8.0,
     'L0_attn_b1': 8.0,
     'L0_attn_W2': 6.28,
     'L0_ffn_Wq': 8.0,
     'L0_ffn_Wk': 8.0,
     'L0_ffn_Wv': 8.0,
     'L0_ffn_Wo': 8.0,
     'L0_ffn_gate_W': 8.0,
     'L0_ffn_W1': 8.0,
     'L0_ffn_W2': 3.954}
    for name, (base, spread) in spreads.items():
        noise = np.random.default_rng([zlib.crc32(name.encode()), seed]).standard_normal(out[name].shape)
        drawn = base * np.exp(spread * noise) if base else spread * noise
        out[name] = jnp.asarray(drawn.astype(out[name].dtype))
    for name, factor in factors.items():
        out[name] = (out[name] * factor).astype(out[name].dtype)
    return out
```

```python
from contextlib import ExitStack

import concourse.bass as bass
from concourse import mybir

F32 = mybir.dt.float32
F16 = mybir.dt.float16
I32 = mybir.dt.int32
ALU = mybir.AluOpType
ACT = mybir.ActivationFunctionType
AX = mybir.AxisListType

B, C, S = 64, 2, 104
HP, PATCH = 4, 8
NP = S // PATCH
FRAME = S + 2 * HP
NG1 = FRAME // PATCH
SHIFTS = 5
D = 128
TOK = NP * NP + 1
NB = 4
G = B // NB
T = NB * TOK
TH = T // 2
QC = TOK // 2
TILES = T // QC
H, DH = 2, 64
E, FF = 8, 512
CH = FF // D
SLOTS = E * CH
LAG = 2
EPS_TOK, EPS_LN, EPS_L2 = 1e-7, 1e-5, 1e-12
EDGES = 1024
EK = EDGES // 128
NST = 4
AREA = 22444
MASKED = -1e30
COUNT = C * SHIFTS * S * S
KP = C * PATCH * PATCH
CELLS = NG1 * NG1
R1, R0 = 4, 3
COL_B1, COL_TB, COL_BP, COL_LNG, COL_LNB, COL_CLS, COL_QN, COL_KN = 0, 32, 33, 34, 35, 36, 37, 38

PACK_A = {"gamma": SHIFTS * NP * NP, "conv_w": SHIFTS * D}
PACK_B = {"beta": SHIFTS * NP * NP, "cols": 39, "scal": 28, "wp": 5 * D, "wv_t": D, "wo": D, "wq": D,
          "wk": D, "gate_w": E, "gate_b": E, "b2": D}


def vit_tower(nc, cells1, cells0, pack_a, pack_b, edge, w1, w2, out):
    with ExitStack() as ctx:
        def sb(name, shape, dt=F32):
            return ctx.enter_context(nc.sbuf_tensor(name, shape, dt))

        def sem(name):
            return ctx.enter_context(nc.semaphore(name))

        bank = [ctx.enter_context(nc.psum_tensor(f"pair{i}", [128, 2, 512], F32)) for i in range(4)]
        hid_ps = bank[0:2]
        eo_ps = bank[2]
        fr_ps = bank[3]

        def flat(pair):
            return pair[:, :, :].rearrange("p b n -> p (b n)")

        def halves(ps):
            return ps[:, :, 0:TH]

        def two(ap):
            return ap.rearrange("p (b n) -> p b n", b=2)

        ht = sb("ht", [128, B * TOK])
        ws = sb("ws", [128, 4 * SLOTS * D // 2])
        w1h, w1l, w2h, w2l = (ws[:, i * SLOTS * D // 2:(i + 1) * SLOTS * D // 2].bitcast(F16) for i in range(4))
        packs = {}
        for name, layout in (("pack_a", PACK_A), ("pack_b", PACK_B)):
            whole = sb(name + "_sb", [128, sum(layout.values())])
            packs[name] = whole
            o = 0
            for part, n in layout.items():
                packs[part] = whole[:, o:o + n]
                o += n
        gam, conv_w, beta, cols, scal = (packs[n] for n in ("gamma", "conv_w", "beta", "cols", "scal"))
        wp_t, wv_t, wo_s, wq_s, wk_s = (packs[n] for n in ("wp", "wv_t", "wo", "wq", "wk"))
        gate_ws, gate_bs, b2_s = packs["gate_w"], packs["gate_b"][0:QC, :], packs["b2"][0:E, :]
        area = sb("area", [128, AREA])
        stage_all = sb("stage_sb", [128, NST * FF])
        stage = [stage_all[:, i * FF:(i + 1) * FF] for i in range(NST)]

        ident = sb("ident", [128, 128])
        ident16 = sb("ident16", [128, 128], F16)
        mean_m = sb("mean_m", [128, 128])
        count_m = sb("count_m", [128, 128])
        head_m = sb("head_m", [128, 128])
        mask = sb("mask", [QC, QC], mybir.dt.bfloat16)
        identb = sb("identb", [QC, QC], mybir.dt.bfloat16)
        conv_u = sb("conv_u", [128, NP * NP])
        conv_b = sb("conv_b", [128, NP * NP])
        adj_t = sb("adj_t", [128, 128])
        gcn_m = sb("gcn_m", [128, 4 * D])
        gcn_c = sb("gcn_c", [128, 1])
        wvo = sb("wvo", [128, H * D])
        att_b = sb("att_b", [128, 3])
        gq = sb("gq", [128, 2])
        eps = sb("eps", [128, 4])
        edge_i = sb("edge_i", [128, 2 * EK], I32)
        edge_f = sb("edge_f", [128, 2 * EK])
        deg = sb("deg", [128, 4])
        stat = sb("stat", [128, 8 * B])
        img = sb("img", [128, 2 * B])
        rq = sb("rq", [QC, NB * 4])
        qn = sb("qn", [QC, NB * 4])
        mx = sb("mx", [QC, NB * 4])
        nbias = sb("nbias", [QC, NB * 4])
        sm = sb("sm", [QC, NB * 4])
        rs = sb("rs", [QC, NB * 4])
        lg = sb("lg", [QC, TILES * E])
        lge = sb("lge", [QC, TILES * E])
        gts = sb("gts", [QC, TILES * E])
        gm = sb("gm", [QC, TILES * 2])
        gt_t = sb("gt_t", [E, T])
        gate_dram = nc.dram_tensor("gate_scratch", (E, T), F32, kind="Internal").ap()

        at = [0]

        def take(n, whole=area):
            at[0] += n
            return whole[:, at[0] - n:at[0]]

        N1, N0 = NG1 * B, NP * B
        row1 = [take(N1) for _ in range(R1)]
        row0 = [take(N0) for _ in range(R0)]
        sq1 = [take(N1) for _ in range(2)]
        sq0 = [take(N0) for _ in range(2)]
        ax1, as1, ax0, as0 = take(N1), take(N1), take(N0), take(N0)
        xg = [[take(N0) for _ in range(SHIFTS)] for _ in range(2)]
        assert at[0] <= AREA

        at[0] = 0
        oh = take(2 * EK * D // 2, stage_all).bitcast(F16)
        iota_f, adj_n, adj = (take(D, stage_all) for _ in range(3))
        assert at[0] <= NST * FF

        at[0] = 0
        dev, sq, std = take(T), take(T), take(T)
        probs = area[0:QC, 0:NB * 6 * QC]
        h1 = take(4 * T)
        vp = h1[0:QC, 0:NB * 512]
        rst, xh, qs, kb, sqq = (take(T) for _ in range(5))
        fix = sqq[:, 0:NB * NP * NP]
        hid = [take(T) for _ in range(2)]
        hh = [take(T // 2).bitcast(F16) for _ in range(3)]
        hl = [take(T // 2).bitcast(F16) for _ in range(3)]
        gbc = take(E * T)
        tmp = [take(T) for _ in range(2)]
        pt = [take(6 * QC) for _ in range(2)]
        y32, acc = take(T), take(T)
        yh, yl = take(T // 2).bitcast(F16), take(T // 2).bitcast(F16)
        assert at[0] <= AREA, at[0]

        consts_ready, pack_a_in, pack_b_in, edge_in = map(sem, ("consts_ready", "pack_a_in", "pack_b_in", "edge_in"))
        row1_in = [sem(f"row1_in{k}") for k in range(R1)]
        row0_in = [sem(f"row0_in{k}") for k in range(R0)]
        xsum_done, xsq_done, sqsum1_done, sqsum0_done = map(
            sem, ("xsum_done", "xsq_done", "sqsum1_done", "sqsum0_done"))
        fix_step, fixed = map(sem, ("fix_step", "fixed"))
        wstage_in, whi_done, wlo_done = map(sem, ("wstage_in", "whi_done", "wlo_done"))
        pe_prep, act_prep, dve_prep, pool_prep = map(sem, ("pe_prep", "act_prep", "dve_prep", "pool_prep"))
        stat_step, act_stat, pe_stat, mul_done = map(sem, ("stat_step", "act_stat", "pe_stat", "mul_done"))
        conv_done, tok_done = map(sem, ("conv_done", "tok_done"))
        mean_ps, dev_ready, sq_ready, var_ps = map(sem, ("mean_ps", "dev_ready", "sq_ready", "var_ps"))
        std_ready, rst_ready, xh_ready = map(sem, ("std_ready", "rst_ready", "xh_ready"))
        g_ps, h1_ready, gcn_ps, h2_ready = map(sem, ("g_ps", "h1_ready", "gcn_ps", "h2_ready"))
        mean2_ps, dev2_ready, sq2_ready, var2_ps = map(sem, ("mean2_ps", "dev2_ready", "sq2_ready", "var2_ps"))
        std2_ready, rst2_ready, hx_ready = map(sem, ("std2_ready", "rst2_ready", "hx_ready"))
        q_ps, q_ready, k_ps, k_ready = map(sem, ("q_ps", "q_ready", "k_ps", "k_ready"))
        ss_ready, ss_ps, ssd_ready = map(sem, ("ss_ready", "ss_ps", "ssd_ready"))
        krst_ready, qk_ready = map(sem, ("krst_ready", "qk_ready"))
        vp_ps, vp_ready, score_ps, max_ready = map(sem, ("vp_ps", "vp_ready", "score_ps", "max_ready"))
        nb_ready, exp_ready, rs_ready, p_ready = map(sem, ("nb_ready", "exp_ready", "rs_ready", "p_ready"))
        pt_ps, pt_ready, pv_ps, y_ready = map(sem, ("pt_ps", "pt_ready", "pv_ps", "y_ready"))
        yh_ready, yl_ready = map(sem, ("yh_ready", "yl_ready"))
        logit_ps, lg_step, lge_ready, gate_step = map(sem, ("logit_ps", "lg_step", "lge_ready", "gate_step"))
        gt_ps, gt_ready, gate_out = map(sem, ("gt_ps", "gt_ready", "gate_out"))
        gate_in = [sem(f"gate_in{n}") for n in range(2)]
        hid_ps_ready, hid_ready, hhi_act, hhi_dve = map(sem, ("hid_ps_ready", "hid_ready", "hhi_act", "hhi_dve"))
        hlo_ready, chunk_used, tmp_ready, acc_step = map(sem, ("hlo_ready", "chunk_used", "tmp_ready", "acc_step"))
        b2_ps, acc_init, out_done = map(sem, ("b2_ps", "acc_init", "out_done"))
        PREP_PE, PREP_ACT, PREP_POOL, PREP_DVE = 8, 8, 15 + 1 + 2 * EK, 22

        def col(n):
            return cols[:, n:n + 1]

        def tokens(g):
            return two(ht[:, bass.ds(g * T, T)])

        SCORE = H * 3 * QC

        def score_at(h, c):
            return h * 3 * QC + c * QC, (c + 1) * QC

        def score_ps_at(b):
            return hid_ps[b // 2][0:QC, :, (b % 2) * 3 * QC:(b % 2 + 1) * 3 * QC]

        def order1(a):
            return 2 * a - 1 if a else 0

        def order0(p):
            return 2 * p + 2

        block = ctx.enter_context(nc.Block())

        @block.sync
        def _(sp):
            def load1(a):
                if a >= R1:
                    sp.wait_ge(mul_done, a - R1 + 1)
                    sp.wait_ge(xsum_done, order1(a - R1) + 1)
                    sp.wait_ge(xsq_done, order1(a - R1) + 1)
                sp.dma_start(row1[a % R1], cells1[a]).then_inc(row1_in[a % R1], 16)

            def load0(p):
                if p >= R0:
                    sp.wait_ge(mul_done, p - R0 + 1)
                    sp.wait_ge(xsum_done, order0(p - R0) + 1)
                    sp.wait_ge(xsq_done, order0(p - R0) + 1)
                sp.dma_start(row0[p % R0], cells0[p]).then_inc(row0_in[p % R0], 16)

            sp.dma_start(packs["pack_a"][:, :], pack_a).then_inc(pack_a_in, 16)
            load1(0)
            for p in range(NP):
                load1(p + 1)
                load0(p)
            sp.wait_ge(pe_prep, PREP_PE)
            sp.wait_ge(dve_prep, PREP_DVE)
            for i in range(2 * E):
                if i >= NST:
                    sp.wait_ge(wlo_done, i - NST + 1)
                src = w1 if i < E else w2
                sp.dma_start(stage[i % NST], src[:, (i % E) * FF:(i % E + 1) * FF]).then_inc(wstage_in, 16)
                sp.wait_ge(wstage_in, 16 * (i + 1))

            def gates(g, later=True):
                sp.wait_ge(gt_ready, g + 1)
                sp.dma_start(gate_dram, gt_t[:, :]).then_inc(gate_out, 16)
                sp.wait_ge(gate_out, 16 * (g + 1))
                if later:
                    sp.wait_ge(tmp_ready, g * E)
                for n in range(2):
                    e0, e1 = n * (E // 2), (n + 1) * (E // 2)
                    sp.dma_start(gbc[:, e0 * T:e1 * T], gate_dram[e0:e1, :].rearrange("e t -> (e t)")
                                 .partition_broadcast(128)).then_inc(gate_in[n], 16)

            def store(g):
                sp.wait_ge(acc_step, E * (g + 1))
                sp.dma_start(out[:, bass.ds(g * T, T)], acc).then_inc(out_done, 16)

            gates(0, later=False)
            with sp.Fori(1, G) as g:
                store(g - 1)
                gates(g)
            store(G - 1)
            sp.wait_ge(out_done, 16 * G)

        @block.gpsimd
        def _(pool):
            pool.memset(ident[:, :], 0.0).then_inc(pool_prep, 1)
            pool.memset(mask[:, :], 0.0).then_inc(pool_prep, 1)
            pool.memset(head_m[:, :], 0.0).then_inc(pool_prep, 1)
            pool.iota(iota_f, [[1, D]], base=0, channel_multiplier=0,
                      allow_small_or_imprecise_dtypes=True).then_inc(pool_prep, 1)
            pool.memset(mean_m[:, :], 1.0 / D).then_inc(pool_prep, 1)
            pool.memset(count_m[:, :], 1.0 / COUNT).then_inc(pool_prep, 1)
            for n, v in enumerate((EPS_TOK, EPS_LN, EPS_LN * EPS_LN, EPS_L2)):
                pool.memset(eps[:, n:n + 1], v).then_inc(pool_prep, 1)
            pool.wait_ge(pool_prep, 10)
            for h in range(H):
                pool.memset(head_m[h * DH:(h + 1) * DH, h * DH:(h + 1) * DH], 1.0).then_inc(pool_prep, 1)
            pool.wait_ge(pool_prep, 12)
            pool.affine_select(out=ident[:, :], in_=ident[:, :], compare_op=ALU.not_equal, fill=1.0,
                               base=0, pattern=[[-1, 128]], channel_multiplier=1).then_inc(pool_prep, 1)
            pool.affine_select(out=mask[:, :], in_=mask[:, :], compare_op=ALU.is_ge, fill=MASKED,
                               base=0, pattern=[[-1, QC]], channel_multiplier=1).then_inc(pool_prep, 1)
            pool.wait_ge(pool_prep, 14)
            pool.tensor_copy(ident16[:, :], ident[:, :]).then_inc(pool_prep, 1)
            pool.wait_ge(pool_prep, 15)
            pool.tensor_copy(identb[:, :], ident[0:QC, 0:QC]).then_inc(consts_ready, 1)
            pool.wait_ge(edge_in, 16)
            pool.tensor_copy(edge_f[:, :], edge_i[:, :]).then_inc(pool_prep, 1)
            pool.wait_ge(pool_prep, 16)
            for k in range(2 * EK):
                pool.tensor_scalar(oh[:, k * D:(k + 1) * D], iota_f, edge_f[:, k:k + 1], None,
                                   ALU.is_equal).then_inc(pool_prep, 1)
            n = 0
            for p in range(-1, NP):
                a = p + 1
                pool.wait_ge(row1_in[a % R1], 16 * (a // R1 + 1))
                if a == 0:
                    pool.tensor_scalar(ax1, row1[0], 0.5, None, ALU.mult).then_inc(xsum_done, 1)
                    continue
                pool.wait_ge(xsum_done, 2 * a - 1 if a > 1 else 1)
                if a < NP:
                    pool.tensor_tensor(ax1, ax1, row1[a % R1], ALU.add).then_inc(xsum_done, 1)
                else:
                    pool.wait_ge(sqsum1_done, NP)
                    pool.tensor_scalar(sq1[0], row1[a % R1], 0.5, None, ALU.mult).then_inc(xsum_done, 1)
                pool.wait_ge(row0_in[p % R0], 16 * (p // R0 + 1))
                if p == 0:
                    pool.tensor_copy(ax0, row0[0]).then_inc(xsum_done, 1)
                else:
                    pool.tensor_tensor(ax0, ax0, row0[p % R0], ALU.add).then_inc(xsum_done, 1)
                pool.wait_ge(xsq_done, order0(p) + 1)
                if p == 0:
                    pool.tensor_copy(as0, sq0[0]).then_inc(sqsum0_done, 1)
                else:
                    pool.wait_ge(sqsum0_done, p)
                    pool.tensor_tensor(as0, as0, sq0[p % 2], ALU.add).then_inc(sqsum0_done, 1)
            pool.wait_ge(xsum_done, 2 * NP + 1)
            pool.tensor_tensor(ax1, ax1, sq1[0], ALU.add).then_inc(xsum_done, 1)
            for i in range(2 * E):
                pool.wait_ge(whi_done, i + 1)
                hi, lo = (w1h, w1l) if i < E else (w2h, w2l)
                j = i % E
                pool.tensor_tensor(lo[:, j * FF:(j + 1) * FF], stage[i % NST], hi[:, j * FF:(j + 1) * FF],
                                   ALU.subtract).then_inc(wlo_done, 1)
            with pool.Fori(0, G) as g:
                for e in range(E):
                    pool.wait_ge(tmp_ready, g * E + e + 1)
                    if e == 0:
                        pool.wait_ge(acc_init, g + 1)
                    else:
                        pool.wait_ge(acc_step, g * E + e)
                    pool.tensor_tensor(acc, acc, tmp[e % 2], ALU.add).then_inc(acc_step, 1)

        @block.scalar
        def _(act):
            act.dma_start(edge_i[:, :], edge).then_inc(edge_in, 16)
            act.dma_start(packs["pack_b"][:, :], pack_b).then_inc(pack_b_in, 16)

            def prep_evac():
                act.wait_ge(pe_prep, 1)
                nc.scalar.activation(conv_u[:, :], hid_ps[0][:, 0, 0:NP * NP], ACT.Copy).then_inc(act_prep, 1)
                nc.scalar.activation(conv_b[:, :], hid_ps[0][:, 1, 0:NP * NP], ACT.Identity,
                                     bias=col(COL_TB)).then_inc(act_prep, 1)
                act.wait_ge(dve_prep, 1)
                nc.scalar.activation(deg[:, 1:2], deg[:, 0:1], ACT.Sqrt).then_inc(act_prep, 1)
                act.wait_ge(pe_prep, 4)
                nc.scalar.activation(adj, eo_ps[:, 0, 0:128], ACT.Copy).then_inc(act_prep, 1)
                act.wait_ge(pe_prep, 6)
                nc.scalar.activation(gcn_c[:, :], eo_ps[:, 0, 128:129], ACT.Identity,
                                     bias=col(COL_BP)).then_inc(act_prep, 1)
                nc.scalar.activation(wvo[:, 0:D], eo_ps[:, 1, 0:D], ACT.Copy).then_inc(act_prep, 1)
                nc.scalar.activation(wvo[:, D:2 * D], hid_ps[0][:, 0, 0:D], ACT.Copy).then_inc(act_prep, 1)
                act.wait_ge(pe_prep, 8)
                nc.scalar.activation(att_b[:, :], eo_ps[:, 0, 256:259], ACT.Copy).then_inc(act_prep, 1)

            def squares1(a):
                act.wait_ge(row1_in[a % R1], 16 * (a // R1 + 1))
                if a >= 2:
                    act.wait_ge(sqsum1_done, a - 1)
                nc.scalar.activation(sq1[a % 2], row1[a % R1], ACT.Square).then_inc(xsq_done, 1)

            def squares0(p):
                act.wait_ge(row0_in[p % R0], 16 * (p // R0 + 1))
                if p >= 2:
                    act.wait_ge(sqsum0_done, p - 1)
                nc.scalar.activation(sq0[p % 2], row0[p % R0], ACT.Square).then_inc(xsq_done, 1)

            def tokens_out(p):
                act.wait_ge(conv_done, p + 1)
                dst = ht[:, :].rearrange("p (b t) -> p t b", t=TOK)[:, 1 + p * NP:1 + (p + 1) * NP, :]
                nc.scalar.activation(dst, flat(fr_ps)[:, 0:N0].rearrange("p (j b) -> p j b", b=B),
                                     ACT.Copy).then_inc(tok_done, 1)

            squares1(0)
            for p in range(NP):
                squares1(p + 1)
                squares0(p)
                if p:
                    tokens_out(p - 1)
                if p == 2:
                    prep_evac()
            tokens_out(NP - 1)
            act.wait_ge(pack_b_in, 16)
            nc.scalar.activation(ht[:, :].rearrange("p (b t) -> p t b", t=TOK)[:, 0, :],
                                 col(COL_CLS).broadcast_to([128, B]), ACT.Copy).then_inc(tok_done, 1)
            act.wait_ge(stat_step, 14)
            nc.scalar.activation(stat[:, 5 * B:6 * B], stat[:, 4 * B:5 * B], ACT.Sqrt, bias=eps[:, 0:1]).then_inc(act_stat, 1)

            for i in range(2 * E):
                act.wait_ge(wstage_in, 16 * (i + 1))
                hi = w1h if i < E else w2h
                j = i % E
                nc.scalar.activation(hi[:, j * FF:(j + 1) * FF], stage[i % NST], ACT.Copy).then_inc(whi_done, 1)

            def front(g, slot):
                if slot == 2:
                    act.wait_ge(dev_ready, g + 1)
                    nc.scalar.activation(sq, dev, ACT.Square).then_inc(sq_ready, 1)
                if slot == 4:
                    act.wait_ge(var_ps, g + 1)
                    nc.scalar.activation(two(std), halves(fr_ps), ACT.Sqrt, bias=eps[:, 1:2]).then_inc(std_ready, 1)
                if slot in (7, 8):
                    act.wait_ge(g_ps, g + 1)
                    for c in (0, 1) if slot == 7 else (2, 3):
                        nc.scalar.activation(two(h1[:, c * T:(c + 1) * T]), halves(fr_ps), ACT.Relu,
                                             bias=scal[:, 4 + c:5 + c], scale=scal[:, c:c + 1]).then_inc(h1_ready, 1)
                if slot == 16:
                    act.wait_ge(dev2_ready, g + 1)
                    nc.scalar.activation(sq, dev, ACT.Square).then_inc(sq2_ready, 1)
                if slot == 18:
                    act.wait_ge(var2_ps, g + 1)
                    nc.scalar.activation(two(std), halves(fr_ps), ACT.Sqrt, bias=eps[:, 2:3],
                                         scale=1.0 + EPS_LN).then_inc(std2_ready, 1)
                if slot == 21:
                    act.wait_ge(q_ps, g + 1)
                    nc.scalar.activation(two(qs), halves(fr_ps), ACT.Identity, bias=att_b[:, 0:1]).then_inc(q_ready, 1)
                if slot == 23:
                    act.wait_ge(k_ps, g + 1)
                    nc.scalar.activation(two(kb), halves(fr_ps), ACT.Identity, bias=att_b[:, 1:2]).then_inc(k_ready, 1)
                if slot == 24:
                    act.wait_ge(q_ready, g + 1)
                    nc.scalar.activation(sqq, qs, ACT.Square).then_inc(ss_ready, 1)
                    act.wait_ge(k_ready, g + 1)
                    nc.scalar.activation(sq, kb, ACT.Square).then_inc(ss_ready, 1)
                if slot == 26:
                    act.wait_ge(ss_ps, g + 1)
                    nc.scalar.activation(two(std), halves(fr_ps), ACT.Sqrt, bias=eps[:, 3:4]).then_inc(ssd_ready, 1)
                    nc.scalar.activation(qn[:, :], fr_ps[0:QC, 0, TH:TH + NB * 4], ACT.Sqrt,
                                         bias=eps[0:QC, 3:4]).then_inc(ssd_ready, 1)

            def values_evac(g, b):
                act.wait_ge(vp_ps, g * NB + b + 1)
                nc.scalar.activation(vp[:, b * 512:(b + 1) * 512], fr_ps[0:QC, b % 2, :], ACT.Copy).then_inc(vp_ready, 1)

            def exps(g, b):
                act.wait_ge(nb_ready, g * (NB // 2) + b // 2 + 1)
                for c in range(2):
                    for h in range(H):
                        n = 4 * b + 2 * c + h
                        o0, w = score_at(h, c)
                        nc.scalar.activation(probs[:, b * SCORE + o0:b * SCORE + o0 + w],
                                             score_ps_at(b)[:, h, c * QC:c * QC + w], ACT.Exp,
                                             bias=nbias[:, n:n + 1], scale=rq[:, n:n + 1],
                                             accum_out=sm[:, n:n + 1]).then_inc(exp_ready, 1)

            def attention(g):
                values_evac(g, 0)
                values_evac(g, 1)
                exps(g, 0)
                exps(g, 1)
                values_evac(g, 2)
                values_evac(g, 3)
                exps(g, 2)
                exps(g, 3)
                act.wait_ge(pv_ps, NB * (g + 1))
                nc.scalar.activation(two(y32), halves(fr_ps), ACT.Identity, bias=att_b[:, 2:3]).then_inc(y_ready, 1)
                act.wait_ge(lg_step, 3 * (g + 1))
                nc.scalar.activation(lge[:, :], lg[:, :], ACT.Exp).then_inc(lge_ready, 1)

            def experts(g, slot):
                n = g * SLOTS + slot
                act.wait_ge(hid_ps_ready, n + 1)
                if slot >= 2:
                    act.wait_ge(hlo_ready, n - 1)
                nc.scalar.activation(two(hid[slot % 2]), halves(hid_ps[slot % 2]), ACT.Gelu_apprx_tanh,
                                     bias=col(COL_B1 + slot)).then_inc(hid_ready, 1)
                if slot % 2:
                    if slot >= 3:
                        act.wait_ge(chunk_used, n - 2)
                    nc.scalar.activation(two(hh[slot % 3]), halves(hid_ps[slot % 2]), ACT.Gelu_apprx_tanh,
                                         bias=col(COL_B1 + slot)).then_inc(hhi_act, 1)

            for slot in range(SLOTS):
                front(0, slot)
            attention(0)
            with act.Fori(1, G) as g:
                for slot in range(SLOTS):
                    experts(g - 1, slot)
                    front(g, slot)
                attention(g)
            for slot in range(SLOTS):
                experts(G - 1, slot)

        @block.tensor
        def _(pe):
            mm, tr = nc.tensor.matmul, nc.tensor.transpose
            pe.wait_ge(consts_ready, 1)
            pe.wait_ge(pack_a_in, 16)
            pe.wait_ge(pack_b_in, 16)

            def prepare():
                for n, src in enumerate((gam, beta)):
                    for s in range(SHIFTS):
                        last = mm(hid_ps[0][:, n, 0:NP * NP], conv_w[:, s * D:(s + 1) * D],
                                  src[:, s * NP * NP:(s + 1) * NP * NP], start=(s == 0), stop=(s == SHIFTS - 1))
                last.then_inc(pe_prep, 1)
                pe.wait_ge(pool_prep, PREP_POOL)
                for k in range(EK):
                    mm(hid_ps[1][:, 0, 0:D], oh[:, (EK + k) * D:(EK + k + 1) * D], oh[:, k * D:(k + 1) * D],
                       start=(k == 0), stop=False)
                mm(hid_ps[1][:, 0, 0:D], ident16[:, :], ident16[:, :], start=False, stop=True).then_inc(pe_prep, 1)
                pe.wait_ge(dve_prep, 3)
                tr(hid_ps[1][:, 1, 0:D], adj_n, ident[:, :]).then_inc(pe_prep, 1)
                pe.wait_ge(dve_prep, 4)
                tr(eo_ps[:, 0, 0:D], adj_t[:, :], ident[:, :]).then_inc(pe_prep, 1)
                pe.wait_ge(act_prep, 4)
                mm(hid_ps[1][:, 0, :], adj, wp_t[:, D:5 * D], start=True, stop=True).then_inc(pe_prep, 1)
                for k in range(4):
                    mm(eo_ps[:, 0, D:D + 1], wp_t[:, (k + 1) * D:(k + 2) * D], scal[:, 24 + k:25 + k],
                       start=(k == 0), stop=(k == 3))
                for h in range(H):
                    last = mm(eo_ps[:, 1, 0:D] if h == 0 else hid_ps[0][:, 0, 0:D], wv_t[h * DH:(h + 1) * DH, :],
                              wo_s[h * DH:(h + 1) * DH, :], start=True, stop=True)
                last.then_inc(pe_prep, 1)
                pe.wait_ge(act_prep, 7)
                mm(eo_ps[:, 0, 2 * D:2 * D + 1], wq_s, col(COL_LNB), start=True, stop=True)
                mm(eo_ps[:, 0, 2 * D + 1:2 * D + 2], wk_s, col(COL_LNB), start=True, stop=True).then_inc(pe_prep, 1)
                for h in range(H):
                    last = mm(eo_ps[:, 0, 2 * D + 2:2 * D + 3], wvo[:, h * D:(h + 1) * D], col(COL_LNB),
                              start=(h == 0), stop=(h == H - 1))
                last.then_inc(pe_prep, 1)

            def conv(p):
                pe.wait_ge(mul_done, p + 1)
                if p:
                    pe.wait_ge(tok_done, p)
                for s in range(SHIFTS):
                    for a, b in ((0, 512), (512, N0)):
                        last = mm(flat(fr_ps)[:, a:b], conv_w[:, s * D:(s + 1) * D], xg[p % 2][s][:, a:b],
                                  start=(s == 0), stop=(s == SHIFTS - 1))
                last.then_inc(conv_done, 1)

            for p in range(NP):
                conv(p)
                if p == 1:
                    prepare()
            pe.wait_ge(stat_step, 10)
            mm(hid_ps[0][:, 0, 0:2 * B], count_m[:, :], stat[:, 0:2 * B], start=True, stop=True).then_inc(pe_stat, 1)
            pe.wait_ge(tok_done, NP + 1)
            pe.wait_ge(wlo_done, 2 * E)

            def both(lhs, rhs, start=True, stop=True):
                for j in range(2):
                    last = mm(fr_ps[:, j, 0:TH], lhs, rhs[:, j, :], start=start, stop=stop)
                return last

            def front(g, slot, first=False):
                if slot == 1:
                    pe.wait_ge(fixed, g + 1)
                    if not first:
                        pe.wait_ge(acc_init, g)
                    both(mean_m[:, :], tokens(g)).then_inc(mean_ps, 1)
                if slot == 3:
                    pe.wait_ge(sq_ready, g + 1)
                    both(mean_m[:, :], two(sq)).then_inc(var_ps, 1)
                if slot == 6:
                    pe.wait_ge(xh_ready, g + 1)
                    both(adj_t[:, :], two(xh)).then_inc(g_ps, 1)
                if slot == 9:
                    pe.wait_ge(h1_ready, 4 * (g + 1))
                    both(wp_t[:, 0:D], two(xh), stop=False)
                if 10 <= slot < 14:
                    c = slot - 10
                    last = both(gcn_m[:, c * D:(c + 1) * D], two(h1[:, c * T:(c + 1) * T]),
                                start=False, stop=(c == 3))
                    if c == 3:
                        last.then_inc(gcn_ps, 1)
                if slot == 15:
                    pe.wait_ge(h2_ready, g + 1)
                    both(mean_m[:, :], tokens(g)).then_inc(mean2_ps, 1)
                if slot == 17:
                    pe.wait_ge(sq2_ready, g + 1)
                    both(mean_m[:, :], two(sq)).then_inc(var2_ps, 1)
                if slot == 20:
                    pe.wait_ge(hx_ready, g + 1)
                    both(wq_s, two(xh)).then_inc(q_ps, 1)
                if slot == 22:
                    pe.wait_ge(q_ready, g + 1)
                    both(wk_s, two(xh)).then_inc(k_ps, 1)
                if slot == 25:
                    pe.wait_ge(k_ready, g + 1)
                    pe.wait_ge(ss_ready, 2 * (g + 1))
                    both(head_m[:, :], two(sq))
                    for t in range(TILES):
                        last = mm(fr_ps[0:QC, 0, TH + 2 * t:TH + 2 * t + 2], sqq[:, t * QC:(t + 1) * QC],
                                  head_m[:, 0:DH + 1:DH], start=True, stop=True)
                    last.then_inc(ss_ps, 1)

            def values(g, b):
                if b < 2:
                    pe.wait_ge(ssd_ready, 2 * (g + 1))
                else:
                    pe.wait_ge(vp_ready, g * NB + b - 1)
                for k in range(2):
                    t = 2 * b + k
                    last = mm(fr_ps[0:QC, b % 2, k * H * D:(k + 1) * H * D], xh[:, t * QC:(t + 1) * QC], wvo[:, :],
                              start=True, stop=True)
                last.then_inc(vp_ps, 1)

            def scores(g, b):
                if b == 0:
                    pe.wait_ge(qk_ready, 2 * (g + 1))
                ps = score_ps_at(b)
                for h in range(H):
                    p = slice(h * DH, (h + 1) * DH)
                    for c in range(2):
                        w = (c + 1) * QC
                        mm(ps[:, h, c * QC:c * QC + w], qs[p, (2 * b + c) * QC:(2 * b + c + 1) * QC],
                           kb[p, b * TOK:b * TOK + w], start=True, stop=False)
                        last = mm(ps[:, h, c * QC + w - QC:c * QC + w], identb[:, :], mask[:, :], start=False, stop=True)
                last.then_inc(score_ps, 1)

            def turn_probs(g, b, later):
                pe.wait_ge(p_ready, g * NB + b + 1)
                if b >= 2:
                    pe.wait_ge(pt_ready, g * NB + b - 1)
                elif later:
                    pe.wait_ge(tmp_ready, g * E)
                for n in range(3 * H):
                    last = tr(eo_ps[0:QC, b % 2, n * QC:(n + 1) * QC],
                              probs[:, b * SCORE + n * QC:b * SCORE + (n + 1) * QC], ident[0:QC, 0:QC])
                last.then_inc(pt_ps, 1)

            def weigh(g, b):
                pe.wait_ge(pt_ready, g * NB + b + 1)
                if b == 0:
                    pe.wait_ge(vp_ready, NB * (g + 1))
                for k in range(2):
                    for h in range(H):
                        v0 = b * 512 + k * H * D + h * D
                        p0 = h * 3 * QC + k * TOK
                        y0 = (b % 2) * TOK
                        last = mm(fr_ps[:, b // 2, y0 + k * QC:y0 + TOK], vp[:, v0:v0 + D],
                                  pt[b % 2][0:QC, p0:p0 + TOK - k * QC],
                                  start=(k == 0 and h == 0), stop=(k == 1 and h == H - 1))
                last.then_inc(pv_ps, 1)

            def attention(g, later):
                values(g, 0)
                values(g, 1)
                scores(g, 0)
                scores(g, 1)
                scores(g, 2)
                scores(g, 3)
                values(g, 2)
                values(g, 3)
                turn_probs(g, 0, later)
                turn_probs(g, 1, later)
                weigh(g, 0)
                turn_probs(g, 2, later)
                weigh(g, 1)
                turn_probs(g, 3, later)
                weigh(g, 2)
                weigh(g, 3)
                pe.wait_ge(y_ready, g + 1)
                pe.wait_ge(pt_ready, NB * (g + 1))
                for t in range(TILES):
                    last = mm(eo_ps[0:QC, 0, t * E:(t + 1) * E], y32[:, t * QC:(t + 1) * QC], gate_ws,
                              start=True, stop=True)
                last.then_inc(logit_ps, 1)
                pe.wait_ge(gate_step, 3 * (g + 1))
                for t in range(TILES):
                    b, m = t // NB, t % NB
                    last = tr(eo_ps[0:E, b, D + m * QC:D + (m + 1) * QC], gts[:, t * E:(t + 1) * E], ident[0:QC, 0:QC])
                last.then_inc(gt_ps, 1)
                pe.wait_ge(gt_ready, g + 1)
                both(b2_s, two(gt_t[:, :])).then_inc(b2_ps, 1)

            def experts_in(g, slot):
                n = g * SLOTS + slot
                if slot == 0:
                    pe.wait_ge(yl_ready, g + 1)
                elif slot >= 2 and slot % 2 == 0:
                    pe.wait_ge(hid_ready, n - 1)
                elif slot >= 2:
                    pe.wait_ge(hhi_act, g * (SLOTS // 2) + (slot - 1) // 2)
                w = slice(slot * D, (slot + 1) * D)
                for i, (lhs, rhs) in enumerate(((w1h, yh), (w1h, yl), (w1l, yh))):
                    for j in range(2):
                        last = mm(hid_ps[slot % 2][:, j, 0:TH], lhs[:, w], rhs[:, j * TH:(j + 1) * TH],
                                  start=(i == 0), stop=(i == 2))
                last.then_inc(hid_ps_ready, 1)

            def experts_out(g, m):
                n = g * SLOTS + m
                pe.wait_ge(hlo_ready, n + 1)
                if m and m % CH == 0:
                    pe.wait_ge(tmp_ready, g * E + m // CH)
                w = slice(m * D, (m + 1) * D)
                for i, (lhs, rhs) in enumerate(((w2h, hh[m % 3]), (w2h, hl[m % 3]), (w2l, hh[m % 3]))):
                    for j in range(2):
                        last = mm(eo_ps[:, j, 0:TH], lhs[:, w], rhs[:, j * TH:(j + 1) * TH],
                                  start=(m % CH == 0 and i == 0), stop=(m % CH == CH - 1 and i == 2))
                last.then_inc(chunk_used, 1)

            for slot in range(SLOTS):
                front(0, slot, first=True)
            attention(0, False)
            with pe.Fori(1, G) as g:
                for slot in range(SLOTS + LAG):
                    if slot < SLOTS:
                        experts_in(g - 1, slot)
                        front(g, slot)
                    if slot >= LAG:
                        experts_out(g - 1, slot - LAG)
                attention(g, True)
            for slot in range(SLOTS + LAG):
                if slot < SLOTS:
                    experts_in(G - 1, slot)
                if slot >= LAG:
                    experts_out(G - 1, slot - LAG)

        @block.vector
        def _(dve):
            v = nc.vector
            def prepare():
                dve.wait_ge(pe_prep, 2)
                v.tensor_reduce(deg[:, 0:1], hid_ps[1][:, 0, 0:D], AX.X, ALU.add).then_inc(dve_prep, 1)
                dve.wait_ge(act_prep, 3)
                v.reciprocal(deg[:, 2:3], deg[:, 1:2]).then_inc(dve_prep, 1)
                dve.wait_ge(dve_prep, 2)
                v.tensor_scalar(adj_n, hid_ps[1][:, 0, 0:D], deg[:, 2:3], None, ALU.mult).then_inc(dve_prep, 1)
                dve.wait_ge(pe_prep, 3)
                v.tensor_scalar(adj_t[:, :], hid_ps[1][:, 1, 0:D], deg[:, 2:3], None, ALU.mult).then_inc(dve_prep, 1)
                dve.wait_ge(pe_prep, 5)
                for k in range(4):
                    src = hid_ps[1][:, 0, k * D:(k + 1) * D]
                    for c in range(4):
                        dst, w = gcn_m[:, c * D:(c + 1) * D], scal[:, 8 + 4 * c + k:9 + 4 * c + k]
                        if k == 0:
                            v.tensor_scalar(dst, src, w, None, ALU.mult).then_inc(dve_prep, 1)
                        else:
                            dve.wait_ge(dve_prep, 4 + 4 * (k - 1) + c + 1)
                            v.scalar_tensor_tensor(dst, src, w, dst, ALU.mult, ALU.add).then_inc(dve_prep, 1)
                v.tensor_scalar(gq[:, 0:1], col(COL_QN), float(DH) ** 0.5, None, ALU.mult).then_inc(dve_prep, 1)
                dve.wait_ge(dve_prep, 21)
                v.tensor_tensor(gq[:, 1:2], gq[:, 0:1], col(COL_KN), ALU.mult).then_inc(dve_prep, 1)

            dve.wait_ge(pack_a_in, 16)
            gam_v = gam.rearrange("p (s i j) -> p s i j", s=SHIFTS, i=NP)

            def square_sum(a):
                dve.wait_ge(xsq_done, order1(a) + 1)
                if a == 0:
                    v.tensor_scalar(as1, sq1[0], 0.5, None, ALU.mult).then_inc(sqsum1_done, 1)
                else:
                    dve.wait_ge(sqsum1_done, a)
                    v.scalar_tensor_tensor(as1, sq1[a % 2], 0.5 if a == NP else 1.0, as1,
                                           ALU.mult, ALU.add).then_inc(sqsum1_done, 1)

            for p in range(NP):
                if p == 0:
                    dve.wait_ge(row1_in[0], 16)
                dve.wait_ge(row1_in[(p + 1) % R1], 16 * ((p + 1) // R1 + 1))
                dve.wait_ge(row0_in[p % R0], 16 * (p // R0 + 1))
                if p >= 2:
                    dve.wait_ge(conv_done, p - 1)
                upper, lower = row1[p % R1], row1[(p + 1) % R1]
                for s, (src, c0) in enumerate(((row0[p % R0], 0), (lower, 0), (lower, 1), (upper, 0), (upper, 1))):
                    gv = gam_v[:, s, p, :].unsqueeze(2).broadcast_to([128, NP, B])
                    last = v.tensor_tensor(xg[p % 2][s].rearrange("p (j b) -> p j b", b=B),
                                           src[:, c0 * B:(c0 + NP) * B].rearrange("p (j b) -> p j b", b=B),
                                           gv, ALU.mult)
                last.then_inc(mul_done, 1)
                if p == 0:
                    square_sum(0)
                square_sum(p + 1)
                if p == 2:
                    dve.wait_ge(pack_b_in, 16)
                    prepare()
            dve.wait_ge(xsum_done, 2 * NP + 2)
            dve.wait_ge(sqsum0_done, NP)
            dve.wait_ge(sqsum1_done, NG1)
            for n, (a1, a0) in enumerate(((ax1, ax0), (as1, as0))):
                s1, s0, side = (stat[:, k * B:(k + 1) * B] for k in (2 + n, 4 + n, 6 + n))
                v.tensor_reduce(s1, a1.rearrange("p (c b) -> p b c", b=B), AX.X, ALU.add).then_inc(stat_step, 1)
                v.tensor_reduce(s0, a0.rearrange("p (c b) -> p b c", b=B), AX.X, ALU.add).then_inc(stat_step, 1)
                v.tensor_tensor(side, a1[:, 0:B], a1[:, N1 - B:N1], ALU.add).then_inc(stat_step, 1)
            dve.wait_ge(stat_step, 6)
            v.scalar_tensor_tensor(stat[:, 4 * B:6 * B], stat[:, 2 * B:4 * B], 4.0, stat[:, 4 * B:6 * B],
                                   ALU.mult, ALU.add).then_inc(stat_step, 3)
            dve.wait_ge(stat_step, 9)
            v.scalar_tensor_tensor(stat[:, 0:2 * B], stat[:, 6 * B:8 * B], -2.0, stat[:, 4 * B:6 * B],
                                   ALU.mult, ALU.add).then_inc(stat_step, 1)
            dve.wait_ge(pe_stat, 1)
            v.tensor_copy(stat[:, 2 * B:3 * B], hid_ps[0][:, 0, 0:B]).then_inc(stat_step, 1)
            dve.wait_ge(stat_step, 11)
            v.tensor_tensor(stat[:, 3 * B:4 * B], stat[:, 2 * B:3 * B], stat[:, 2 * B:3 * B], ALU.mult).then_inc(stat_step, 1)
            dve.wait_ge(stat_step, 12)
            v.tensor_tensor(stat[:, 4 * B:5 * B], hid_ps[0][:, 0, B:2 * B], stat[:, 3 * B:4 * B],
                            ALU.subtract).then_inc(stat_step, 2)
            dve.wait_ge(act_stat, 1)
            v.reciprocal(img[:, 0:B], stat[:, 5 * B:6 * B]).then_inc(stat_step, 1)
            dve.wait_ge(stat_step, 15)
            v.scalar_tensor_tensor(img[:, B:2 * B], stat[:, 2 * B:3 * B], -1.0, img[:, 0:B],
                                   ALU.mult, ALU.mult).then_inc(stat_step, 1)
            dve.wait_ge(stat_step, 16)
            dve.wait_ge(act_prep, PREP_ACT)
            dve.wait_ge(tok_done, NP + 1)
            dve.wait_ge(conv_done, NP)

            def front(g, slot):
                if slot == 0:
                    for b in range(NB):
                        v.scalar_tensor_tensor(fix[:, b * NP * NP:(b + 1) * NP * NP], conv_u[:, :],
                                               img[:, bass.ds(g * NB + (B + b), 1)], conv_b[:, :],
                                               ALU.mult, ALU.add).then_inc(fix_step, 1)
                    for b in range(NB):
                        dve.wait_ge(fix_step, NB * g + (b + 1))
                        h_b = ht[:, bass.ds(g * T + (b * TOK + 1), NP * NP)]
                        last = v.scalar_tensor_tensor(h_b, h_b, img[:, bass.ds(g * NB + b, 1)],
                                                      fix[:, b * NP * NP:(b + 1) * NP * NP], ALU.mult, ALU.add)
                    last.then_inc(fixed, 1)
                if slot == 1:
                    dve.wait_ge(mean_ps, g + 1)
                    v.tensor_tensor(two(dev), tokens(g), halves(fr_ps), ALU.subtract).then_inc(dev_ready, 1)
                if slot == 5:
                    dve.wait_ge(std_ready, g + 1)
                    v.reciprocal(rst, std).then_inc(rst_ready, 1)
                    dve.wait_ge(rst_ready, g + 1)
                    v.tensor_tensor(xh, dev, rst, ALU.mult).then_inc(xh_ready, 1)
                if slot == 14:
                    dve.wait_ge(gcn_ps, g + 1)
                    v.scalar_tensor_tensor(tokens(g), halves(fr_ps), gcn_c[:, 0:1], tokens(g),
                                           ALU.add, ALU.add).then_inc(h2_ready, 1)
                if slot == 15:
                    dve.wait_ge(mean2_ps, g + 1)
                    dve.wait_ge(h2_ready, g + 1)
                    v.tensor_tensor(two(dev), tokens(g), halves(fr_ps), ALU.subtract).then_inc(dev2_ready, 1)
                if slot == 19:
                    dve.wait_ge(std2_ready, g + 1)
                    v.reciprocal(rst, std).then_inc(rst2_ready, 1)
                    dve.wait_ge(rst2_ready, g + 1)
                    v.scalar_tensor_tensor(xh, dev, col(COL_LNG), rst, ALU.mult, ALU.mult).then_inc(hx_ready, 1)
                if slot == 27:
                    dve.wait_ge(ssd_ready, 2 * (g + 1))
                    v.reciprocal(rst, std).then_inc(krst_ready, 1)
                    v.reciprocal(rq[:, :], qn[:, :]).then_inc(krst_ready, 1)
                    dve.wait_ge(krst_ready, 2 * (g + 1))
                    v.tensor_tensor(kb, kb, rst, ALU.mult).then_inc(qk_ready, 1)
                    v.tensor_scalar(qs, qs, gq[:, 1:2], None, ALU.mult).then_inc(qk_ready, 1)

            def maxima(g, m):
                dve.wait_ge(score_ps, (g * (NB // 2) + m + 1) * 2)
                mx4 = mx[:, 8 * m:8 * m + 8].rearrange("p (i c h) -> p c i h", c=2, h=H)
                ps = hid_ps[m][0:QC, :, 0:2 * 3 * QC].rearrange("p h (i n) -> p i h n", i=2)
                for c in range(2):
                    v.tensor_reduce(mx4[:, c], ps[:, :, :, c * QC:(2 * c + 1) * QC],
                                    AX.X, ALU.max).then_inc(max_ready, 1)
                dve.wait_ge(max_ready, 2 * (g * (NB // 2) + m + 1))
                v.scalar_tensor_tensor(nbias[:, 8 * m:8 * m + 8], mx[:, 8 * m:8 * m + 8], -1.0,
                                       rq[:, 8 * m:8 * m + 8], ALU.mult, ALU.mult).then_inc(nb_ready, 1)

            def normalise(g, b):
                dve.wait_ge(exp_ready, 4 * (g * NB + b + 1))
                v.reciprocal(rs[:, 4 * b:4 * b + 4], sm[:, 4 * b:4 * b + 4]).then_inc(rs_ready, 1)
                dve.wait_ge(rs_ready, g * NB + b + 1)
                for c in range(2):
                    for h in range(H):
                        o0, w = score_at(h, c)
                        p = probs[:, b * SCORE + o0:b * SCORE + o0 + w]
                        n = 4 * b + 2 * c + h
                        last = v.tensor_scalar(p, p, rs[:, n:n + 1], None, ALU.mult)
                last.then_inc(p_ready, 1)

            def turned(g, b):
                dve.wait_ge(pt_ps, g * NB + b + 1)
                if b >= 2:
                    dve.wait_ge(pv_ps, g * NB + b - 1)
                v.tensor_copy(pt[b % 2][0:QC, :], eo_ps[0:QC, b % 2, 0:SCORE]).then_inc(pt_ready, 1)

            def attention(g, later):
                maxima(g, 0)
                maxima(g, 1)
                normalise(g, 0)
                normalise(g, 1)
                turned(g, 0)
                normalise(g, 2)
                turned(g, 1)
                normalise(g, 3)
                turned(g, 2)
                turned(g, 3)
                dve.wait_ge(y_ready, g + 1)
                v.tensor_copy(yh, y32).then_inc(yh_ready, 1)
                dve.wait_ge(yh_ready, g + 1)
                v.tensor_tensor(yl, y32, yh, ALU.subtract).then_inc(yl_ready, 1)
                dve.wait_ge(logit_ps, g + 1)
                lg3 = lg[:, :].rearrange("p (t e) -> p t e", e=E)
                v.tensor_tensor(lg3, eo_ps[0:QC, 0, 0:TILES * E].rearrange("p (t e) -> p t e", e=E),
                                gate_bs.unsqueeze(1).broadcast_to([QC, TILES, E]), ALU.add).then_inc(lg_step, 1)
                dve.wait_ge(lg_step, 3 * g + 1)
                v.tensor_reduce(gm[:, 0:TILES], lg3, AX.X, ALU.max).then_inc(lg_step, 1)
                dve.wait_ge(lg_step, 3 * g + 2)
                v.tensor_tensor(lg3, lg3, gm[:, 0:TILES].unsqueeze(2).broadcast_to([QC, TILES, E]),
                                ALU.subtract).then_inc(lg_step, 1)
                dve.wait_ge(lge_ready, g + 1)
                lge3 = lge[:, :].rearrange("p (t e) -> p t e", e=E)
                v.tensor_reduce(gm[:, TILES:2 * TILES], lge3, AX.X, ALU.add).then_inc(gate_step, 1)
                dve.wait_ge(gate_step, 3 * g + 1)
                v.reciprocal(gm[:, 0:TILES], gm[:, TILES:2 * TILES]).then_inc(gate_step, 1)
                dve.wait_ge(gate_step, 3 * g + 2)
                v.tensor_tensor(gts[:, :].rearrange("p (t e) -> p t e", e=E), lge3,
                                gm[:, 0:TILES].unsqueeze(2).broadcast_to([QC, TILES, E]),
                                ALU.mult).then_inc(gate_step, 1)
                dve.wait_ge(gt_ps, g + 1)
                if later:
                    dve.wait_ge(gate_out, 16 * g)
                v.tensor_copy(two(gt_t[:, :]), eo_ps[0:E, :, D:D + TH]).then_inc(gt_ready, 1)
                dve.wait_ge(b2_ps, g + 1)
                if later:
                    dve.wait_ge(out_done, 16 * g)
                v.tensor_tensor(two(acc), halves(fr_ps), tokens(g), ALU.add).then_inc(acc_init, 1)

            def experts(g, slot):
                n = g * SLOTS + slot
                dve.wait_ge(hid_ready, n + 1)
                if slot >= 3:
                    dve.wait_ge(chunk_used, n - 2)
                if slot % 2:
                    dve.wait_ge(hhi_act, g * (SLOTS // 2) + (slot + 1) // 2)
                else:
                    v.tensor_copy(hh[slot % 3], hid[slot % 2]).then_inc(hhi_dve, 1)
                    dve.wait_ge(hhi_dve, g * (SLOTS // 2) + slot // 2 + 1)
                v.tensor_tensor(hl[slot % 3], hid[slot % 2], hh[slot % 3], ALU.subtract).then_inc(hlo_ready, 1)

            def weigh(g, e):
                dve.wait_ge(chunk_used, g * SLOTS + (e + 1) * CH)
                dve.wait_ge(gate_in[e // (E // 2)], 16 * (g + 1))
                if e >= 2:
                    dve.wait_ge(acc_step, g * E + e - 1)
                v.tensor_tensor(two(tmp[e % 2]), halves(eo_ps), two(gbc[:, e * T:(e + 1) * T]),
                                ALU.mult).then_inc(tmp_ready, 1)

            def expert_slot(g, slot):
                if slot < SLOTS:
                    experts(g, slot)
                if slot >= LAG and (slot - LAG) % CH == CH - 1:
                    weigh(g, (slot - LAG) // CH)

            for slot in range(SLOTS):
                front(0, slot)
            attention(0, False)
            with dve.Fori(1, G) as g:
                for slot in range(SLOTS + LAG):
                    expert_slot(g - 1, slot)
                    if slot < SLOTS:
                        front(g, slot)
                attention(g, True)
            for slot in range(SLOTS + LAG):
                expert_slot(G - 1, slot)


def kernel(**inputs):
    import numpy as np
    import concourse.bacc as bacc
    from concourse.bass_utils import run_bass_kernel_spmd

    def a(name):
        return np.asarray(inputs[name])

    def pack(layout, parts):
        for name, n in layout.items():
            assert parts[name].shape == (128, n), name
        return np.ascontiguousarray(np.concatenate([parts[name] for name in layout], axis=1))

    x = a("x")
    framed = np.pad(x, ((0, 0), (0, 0), (HP, HP), (HP, HP)))
    cells = [np.ascontiguousarray(v.reshape(B, C, n, PATCH, n, PATCH).transpose(2, 1, 3, 5, 4, 0).reshape(n, KP, n * B))
             for v, n in ((framed, NG1), (x, NP))]

    def patches(v):
        return v.reshape(SHIFTS, C, NP, PATCH, NP, PATCH).transpose(1, 3, 5, 0, 2, 4).reshape(KP, -1)

    vectors = [a("L0_ffn_b1").reshape(-1, D), a("L0_tok_b"), a("L0_attn_bp"), a("L0_ffn_ln_g"), a("L0_ffn_ln_b"),
               a("cls_tok").reshape(1, D), np.tile(a("L0_ffn_qn_g"), H), np.tile(a("L0_ffn_kn_g"), H)]
    scalars = [a("L0_attn_W1").ravel(), a("L0_attn_b1"), a("L0_attn_W2").ravel(), a("L0_attn_b2")]
    pack_a = pack(PACK_A, {
        "gamma": patches(a("L0_tok_gamma")),
        "conv_w": a("L0_tok_W").reshape(D, SHIFTS, KP).transpose(2, 1, 0).reshape(KP, -1)})
    pack_b = pack(PACK_B, {
        "beta": patches(a("L0_tok_beta")),
        "cols": np.concatenate([v.reshape(-1, D) for v in vectors]).T,
        "scal": np.tile(np.concatenate(scalars), (128, 1)),
        "wp": a("L0_attn_Wp").reshape(D, D, 5).transpose(1, 2, 0).reshape(D, -1),
        "wv_t": a("L0_ffn_Wv").T, "wo": a("L0_ffn_Wo"), "wq": a("L0_ffn_Wq"), "wk": a("L0_ffn_Wk"),
        "gate_w": a("L0_ffn_gate_W"), "gate_b": np.tile(a("L0_ffn_gate_b"), (128, 1)),
        "b2": np.pad(a("L0_ffn_b2"), ((0, 128 - E), (0, 0)))})
    arrays = {
        "cells1": cells[0], "cells0": cells[1], "pack_a": pack_a, "pack_b": pack_b,
        "edge": np.ascontiguousarray(a("L0_attn_edge_index").reshape(2, 128, EK).transpose(1, 0, 2).reshape(128, -1)),
        "w1": np.ascontiguousarray(a("L0_ffn_W1").transpose(1, 0, 2).reshape(D, -1)),
        "w2": np.ascontiguousarray(a("L0_ffn_W2").reshape(SLOTS, D, D).transpose(1, 0, 2).reshape(D, -1))}

    nc = bacc.Bacc("TRN2", target_bir_lowering=False, num_devices=1)
    args = [nc.dram_tensor(n, v.shape, mybir.dt.from_np(v.dtype), kind="ExternalInput").ap() for n, v in arrays.items()]
    args.append(nc.dram_tensor("tower_out", (D, B * TOK), F32, kind="ExternalOutput").ap())
    vit_tower(nc, *args)
    r = run_bass_kernel_spmd(nc, [arrays], core_ids=[0])
    return np.ascontiguousarray(r.results[0]["tower_out"].reshape(D, B, TOK).transpose(1, 2, 0))
```

```python
from contextlib import ExitStack

import concourse.bass as bass
from concourse import mybir

F32 = mybir.dt.float32
F16 = mybir.dt.float16
I32 = mybir.dt.int32
ALU = mybir.AluOpType
ACT = mybir.ActivationFunctionType
AX = mybir.AxisListType

B, C, S = 64, 2, 104
HP, PATCH = 4, 8
NP = S // PATCH
FRAME = S + 2 * HP
NG1 = FRAME // PATCH
SHIFTS = 5
D = 128
TOK = NP * NP + 1
NB = 4
G = B // NB
T = NB * TOK
TH = T // 2
QC = TOK // 2
TILES = T // QC
H, DH = 2, 64
E, FF = 8, 512
CH = FF // D
SLOTS = E * CH
LAG = 2
EPS_TOK, EPS_LN, EPS_L2 = 1e-7, 1e-5, 1e-12
EDGES = 1024
EK = EDGES // 128
NST = 4
AREA = 22444
LN2_SLOTS = {"row2": 0, "cast2": 1, "hx": 1}
GATE_SLOTS = {"turn": 1, "bias": 3}
QK_SLOTS = {"q": 6, "k": 8, "sums": 10, "root0": 11, "root1": 12, "root2": 13, "krow": 14, "kcast": 15, "kn": 15}
EARLY_SLOTS = {"fix": 11, "mean": 17, "dev": 17, "sq": 18, "var": 19, "root0": 20, "root1": 21, "root2": 22,
               "row": 23, "cast": 25, "xn": 25,
               "edges": 27, "relu0": 28, "relu1": 29, "relu2": 30, "relu3": 31}
RSQRT_SEED = 0x5F3759DF
MASKED = -1e30
COUNT = C * SHIFTS * S * S
KP = C * PATCH * PATCH
CELLS = NG1 * NG1
R1, R0 = 4, 3
COL_B1, COL_TB, COL_BP, COL_LNG, COL_LNB, COL_CLS, COL_QN, COL_KN = 0, 32, 33, 34, 35, 36, 37, 38

PACK_A = {"gamma": SHIFTS * NP * NP, "conv_w": SHIFTS * D}
PACK_B = {"beta": SHIFTS * NP * NP, "cols": 39, "scal": 28, "wp": 5 * D, "wv_t": D, "wo": D, "wq": D,
          "wk": D, "gate_w": E, "gate_b": E, "b2": D}


def vit_tower(nc, cells1, cells0, pack_a, pack_b, edge, w1, w2, out):
    with ExitStack() as ctx:
        def sb(name, shape, dt=F32):
            return ctx.enter_context(nc.sbuf_tensor(name, shape, dt))

        def sem(name):
            return ctx.enter_context(nc.semaphore(name))

        bank = [ctx.enter_context(nc.psum_tensor(f"pair{i}", [128, 2, 512], F32)) for i in range(4)]
        hid_ps = bank[0:2]
        eo_ps = bank[2]
        fr_ps = bank[3]

        def flat(pair):
            return pair[:, :, :].rearrange("p b n -> p (b n)")

        def halves(ps):
            return ps[:, :, 0:TH]

        def two(ap):
            return ap.rearrange("p (b n) -> p b n", b=2)

        ht = sb("ht", [128, B * TOK])
        ws = sb("ws", [128, 4 * SLOTS * D // 2])
        w1h, w1l, w2h, w2l = (ws[:, i * SLOTS * D // 2:(i + 1) * SLOTS * D // 2].bitcast(F16) for i in range(4))
        packs = {}
        for name, layout in (("pack_a", PACK_A), ("pack_b", PACK_B)):
            whole = sb(name + "_sb", [128, sum(layout.values())])
            packs[name] = whole
            o = 0
            for part, n in layout.items():
                packs[part] = whole[:, o:o + n]
                o += n
        gam, conv_w, beta, cols, scal = (packs[n] for n in ("gamma", "conv_w", "beta", "cols", "scal"))
        wp_t, wv_t, wo_s, wq_s, wk_s = (packs[n] for n in ("wp", "wv_t", "wo", "wq", "wk"))
        gate_ws, gate_bs, b2_s = packs["gate_w"], packs["gate_b"][0:QC, :], packs["b2"][0:E, :]
        area = sb("area", [128, AREA])
        stage_all = sb("stage_sb", [128, NST * FF])
        stage = [stage_all[:, i * FF:(i + 1) * FF] for i in range(NST)]

        ident = sb("ident", [128, 128])
        ident16 = sb("ident16", [128, 128], F16)
        mean_m = sb("mean_m", [128, 128])
        count_m = sb("count_m", [128, 128])
        ones_r = sb("ones_r", [1, 128])
        head_m = sb("head_m", [128, 128])
        mask = sb("mask", [QC, QC], mybir.dt.bfloat16)
        identb = sb("identb", [QC, QC], mybir.dt.bfloat16)
        conv_u = sb("conv_u", [128, NP * NP])
        conv_b = sb("conv_b", [128, NP * NP])
        adj_t = sb("adj_t", [128, 128])
        gcn_m = sb("gcn_m", [128, 4 * D])
        gcn_c = sb("gcn_c", [128, 1])
        wvo = sb("wvo", [128, H * D])
        att_b = sb("att_b", [128, 4])
        gq = sb("gq", [128, 2])
        eps = sb("eps", [128, 4])
        edge_i = sb("edge_i", [128, 2 * EK], I32)
        edge_f = sb("edge_f", [128, 2 * EK])
        deg = sb("deg", [128, 4])
        stat = sb("stat", [128, 8 * B])
        img = sb("img", [128, 2 * B])
        root_in, root, root_t = (sb(n, [QC, 6 * TILES]) for n in ("root_in", "root", "root_t"))
        ROOTS = {"qk": slice(0, 4 * TILES), "ln1": slice(4 * TILES, 5 * TILES), "ln2": slice(5 * TILES, 6 * TILES)}
        rq = root[:, 0:2 * TILES]
        fac = sb("fac", [H, T])
        head_sel = sb("head_sel", [H, 128])
        mx = sb("mx", [QC, NB * 4])
        nbias = sb("nbias", [QC, NB * 4])
        sm = sb("sm", [QC, NB * 4])
        rs = sb("rs", [QC, NB * 4])
        lg = sb("lg", [QC, TILES * E])
        lge = sb("lge", [QC, TILES * E])
        gts = sb("gts", [QC, TILES * E])
        gm = sb("gm", [QC, TILES * 2])
        gt_t = sb("gt_t", [E, T])
        gate_dram = nc.dram_tensor("gate_scratch", (E, T), F32, kind="Internal").ap()

        at = [0]

        def take(n, whole=area):
            at[0] += n
            return whole[:, at[0] - n:at[0]]

        N1, N0 = NG1 * B, NP * B
        row1 = [take(N1) for _ in range(R1)]
        row0 = [take(N0) for _ in range(R0)]
        sq1 = [take(N1) for _ in range(2)]
        sq0 = [take(N0) for _ in range(2)]
        ax1, as1, ax0, as0 = take(N1), take(N1), take(N0), take(N0)
        xg = [[take(N0) for _ in range(SHIFTS)] for _ in range(2)]
        assert at[0] <= AREA

        at[0] = 0
        oh = take(2 * EK * D // 2, stage_all).bitcast(F16)
        iota_f, adj_n, adj = (take(D, stage_all) for _ in range(3))
        assert at[0] <= NST * FF

        at[0] = 0
        dev, sq, h1 = take(T), take(T), take(4 * T)
        sqk, fix = h1[:, 0:T], h1[:, T:T + NB * NP * NP]
        xh, qs, kb, sqq = (take(T) for _ in range(4))
        hid = [take(T) for _ in range(2)]
        hh = [take(T // 2).bitcast(F16) for _ in range(3)]
        hl = [take(T // 2).bitcast(F16) for _ in range(3)]
        gbc = take(E * T)
        vp = gbc[0:QC, 0:NB * 512]
        probs = gbc[0:QC, NB * 512:NB * (512 + 6 * QC)]
        assert NB * (512 + 6 * QC) <= (E - 1) * T
        tmp = [take(T) for _ in range(2)]
        pt = [take(6 * QC) for _ in range(2)]
        y32, acc = take(T), take(T)
        yh, yl = take(T // 2).bitcast(F16), take(T // 2).bitcast(F16)
        assert at[0] <= AREA, at[0]

        consts_ready, pack_a_in, pack_b_in, edge_in = map(sem, ("consts_ready", "pack_a_in", "pack_b_in", "edge_in"))
        row1_in = [sem(f"row1_in{k}") for k in range(R1)]
        row0_in = [sem(f"row0_in{k}") for k in range(R0)]
        xsum_done, xsq_done, sqsum1_done, sqsum0_done = map(
            sem, ("xsum_done", "xsq_done", "sqsum1_done", "sqsum0_done"))
        fix_step, fixed = map(sem, ("fix_step", "fixed"))
        wstage_in, whi_done, wlo_done = map(sem, ("wstage_in", "whi_done", "wlo_done"))
        pe_prep, act_prep, dve_prep, pool_prep = map(sem, ("pe_prep", "act_prep", "dve_prep", "pool_prep"))
        stat_step, act_stat, pe_stat, mul_done = map(sem, ("stat_step", "act_stat", "pe_stat", "mul_done"))
        conv_done, tok_done = map(sem, ("conv_done", "tok_done"))
        mean_ps, dev_ready, sq_ready, var_ps = map(sem, ("mean_ps", "dev_ready", "sq_ready", "var_ps"))
        var_out, root_ready, root_step, row_ps, row_out, cast_ps = (
            {kind: sem(f"{n}_{kind}") for kind in ROOTS}
            for n in ("var_out", "root_ready", "root_step", "row_ps", "row_out", "cast_ps"))
        xn_ready = sem("xn_ready")
        g_ps, h1_ready, gcn_ps, h2_ready = map(sem, ("g_ps", "h1_ready", "gcn_ps", "h2_ready"))
        mean2_ps, dev2_ready, sq2_ready, var2_ps = map(sem, ("mean2_ps", "dev2_ready", "sq2_ready", "var2_ps"))
        hx_ready = sem("hx_ready")
        q_ps, q_ready, k_ps, k_ready = map(sem, ("q_ps", "q_ready", "k_ps", "k_ready"))
        ss_ready, ss_ps, kn_ready = map(sem, ("ss_ready", "ss_ps", "kn_ready"))
        vp_ps, vp_ready, score_ps, max_ready = map(sem, ("vp_ps", "vp_ready", "score_ps", "max_ready"))
        nb_ready, exp_ready, rs_ready, p_ready = map(sem, ("nb_ready", "exp_ready", "rs_ready", "p_ready"))
        pt_ps, pt_ready, pv_ps, y_ready = map(sem, ("pt_ps", "pt_ready", "pv_ps", "y_ready"))
        yh_ready, yl_ready = map(sem, ("yh_ready", "yl_ready"))
        logit_ps, lg_step, lge_ready, gate_step = map(sem, ("logit_ps", "lg_step", "lge_ready", "gate_step"))
        gt_ps, gt_ready, gate_out = map(sem, ("gt_ps", "gt_ready", "gate_out"))
        gate_in = [sem(f"gate_in{n}") for n in range(2)]
        hid_ps_ready, hid_ready, hhi_act, hhi_dve = map(sem, ("hid_ps_ready", "hid_ready", "hhi_act", "hhi_dve"))
        hlo_ready, chunk_used, tmp_ready, acc_step = map(sem, ("hlo_ready", "chunk_used", "tmp_ready", "acc_step"))
        b2_ps, acc_init, out_done = map(sem, ("b2_ps", "acc_init", "out_done"))
        PREP_PE, PREP_ACT, PREP_POOL, PREP_DVE = 8, 9, 19 + 1 + 2 * EK, 22

        def col(n):
            return cols[:, n:n + 1]

        def tokens(g):
            return two(ht[:, bass.ds(g * T, T)])

        SCORE = H * 3 * QC

        def score_at(h, c):
            return h * 3 * QC + c * QC, (c + 1) * QC

        def score_ps_at(b):
            return hid_ps[b // 2][0:QC, :, (b % 2) * 3 * QC:(b % 2 + 1) * 3 * QC]

        def steps_in(slots, slot):
            return [step for step, n in slots.items() if n == slot]

        def order1(a):
            return 2 * a - 1 if a else 0

        def order0(p):
            return 2 * p + 2

        block = ctx.enter_context(nc.Block())

        @block.sync
        def _(sp):
            def load1(a):
                if a >= R1:
                    sp.wait_ge(mul_done, a - R1 + 1)
                    sp.wait_ge(xsum_done, order1(a - R1) + 1)
                    sp.wait_ge(xsq_done, order1(a - R1) + 1)
                sp.dma_start(row1[a % R1], cells1[a]).then_inc(row1_in[a % R1], 16)

            def load0(p):
                if p >= R0:
                    sp.wait_ge(mul_done, p - R0 + 1)
                    sp.wait_ge(xsum_done, order0(p - R0) + 1)
                    sp.wait_ge(xsq_done, order0(p - R0) + 1)
                sp.dma_start(row0[p % R0], cells0[p]).then_inc(row0_in[p % R0], 16)

            sp.dma_start(packs["pack_a"][:, :], pack_a).then_inc(pack_a_in, 16)
            load1(0)
            for p in range(NP):
                load1(p + 1)
                load0(p)
            sp.wait_ge(pe_prep, PREP_PE)
            sp.wait_ge(dve_prep, PREP_DVE)
            for i in range(2 * E):
                if i >= NST:
                    sp.wait_ge(wlo_done, i - NST + 1)
                src = w1 if i < E else w2
                sp.dma_start(stage[i % NST], src[:, (i % E) * FF:(i % E + 1) * FF]).then_inc(wstage_in, 16)
                sp.wait_ge(wstage_in, 16 * (i + 1))

            def gates(g, later=True):
                sp.wait_ge(gt_ready, g + 1)
                sp.dma_start(gate_dram, gt_t[:, :]).then_inc(gate_out, 16)
                sp.wait_ge(gate_out, 16 * (g + 1))
                if later:
                    sp.wait_ge(tmp_ready, g * E)
                for n in range(2):
                    e0, e1 = n * (E // 2), (n + 1) * (E // 2)
                    sp.dma_start(gbc[:, e0 * T:e1 * T], gate_dram[e0:e1, :].rearrange("e t -> (e t)")
                                 .partition_broadcast(128)).then_inc(gate_in[n], 16)

            def store(g):
                sp.wait_ge(acc_step, E * (g + 1))
                sp.dma_start(out[:, bass.ds(g * T, T)], acc).then_inc(out_done, 16)

            gates(0, later=False)
            with sp.Fori(1, G) as g:
                store(g - 1)
                gates(g)
            store(G - 1)
            sp.wait_ge(out_done, 16 * G)

        @block.gpsimd
        def _(pool):
            pool.memset(ident[:, :], 0.0).then_inc(pool_prep, 1)
            pool.memset(mask[:, :], 0.0).then_inc(pool_prep, 1)
            pool.memset(head_m[:, :], 0.0).then_inc(pool_prep, 1)
            pool.iota(iota_f, [[1, D]], base=0, channel_multiplier=0,
                      allow_small_or_imprecise_dtypes=True).then_inc(pool_prep, 1)
            pool.memset(mean_m[:, :], 1.0 / D).then_inc(pool_prep, 1)
            pool.memset(count_m[:, :], 1.0 / COUNT).then_inc(pool_prep, 1)
            for n, v in enumerate((EPS_TOK, EPS_LN, EPS_LN * EPS_LN, EPS_L2)):
                pool.memset(eps[:, n:n + 1], v).then_inc(pool_prep, 1)
            pool.wait_ge(pool_prep, 10)
            for h in range(H):
                pool.memset(head_m[h * DH:(h + 1) * DH, h * DH:(h + 1) * DH], 1.0).then_inc(pool_prep, 1)
            pool.wait_ge(pool_prep, 12)
            pool.affine_select(out=ident[:, :], in_=ident[:, :], compare_op=ALU.not_equal, fill=1.0,
                               base=0, pattern=[[-1, 128]], channel_multiplier=1).then_inc(pool_prep, 1)
            pool.affine_select(out=mask[:, :], in_=mask[:, :], compare_op=ALU.is_ge, fill=MASKED,
                               base=0, pattern=[[-1, QC]], channel_multiplier=1).then_inc(pool_prep, 1)
            pool.memset(head_sel[:, :], 1.0).then_inc(pool_prep, 1)
            pool.memset(ones_r[:, :], 1.0).then_inc(pool_prep, 1)
            pool.wait_ge(pool_prep, 16)
            pool.affine_select(out=head_sel[:, :], in_=head_sel[:, :], compare_op=ALU.is_ge, fill=0.0,
                               base=0, pattern=[[1, 128]], channel_multiplier=-DH).then_inc(pool_prep, 1)
            pool.wait_ge(pool_prep, 17)
            pool.affine_select(out=head_sel[:, :], in_=head_sel[:, :], compare_op=ALU.is_ge, fill=0.0,
                               base=DH - 1, pattern=[[-1, 128]], channel_multiplier=DH).then_inc(pool_prep, 1)
            pool.wait_ge(pool_prep, 18)
            pool.tensor_copy(ident16[:, :], ident[:, :]).then_inc(pool_prep, 1)
            pool.wait_ge(pool_prep, 19)
            pool.tensor_copy(identb[:, :], ident[0:QC, 0:QC]).then_inc(consts_ready, 1)
            pool.wait_ge(edge_in, 16)
            pool.tensor_copy(edge_f[:, :], edge_i[:, :]).then_inc(pool_prep, 1)
            pool.wait_ge(pool_prep, 20)
            for k in range(2 * EK):
                pool.tensor_scalar(oh[:, k * D:(k + 1) * D], iota_f, edge_f[:, k:k + 1], None,
                                   ALU.is_equal).then_inc(pool_prep, 1)
            n = 0
            for p in range(-1, NP):
                a = p + 1
                pool.wait_ge(row1_in[a % R1], 16 * (a // R1 + 1))
                if a == 0:
                    pool.tensor_scalar(ax1, row1[0], 0.5, None, ALU.mult).then_inc(xsum_done, 1)
                    continue
                pool.wait_ge(xsum_done, 2 * a - 1 if a > 1 else 1)
                if a < NP:
                    pool.tensor_tensor(ax1, ax1, row1[a % R1], ALU.add).then_inc(xsum_done, 1)
                else:
                    pool.wait_ge(sqsum1_done, NP)
                    pool.tensor_scalar(sq1[0], row1[a % R1], 0.5, None, ALU.mult).then_inc(xsum_done, 1)
                pool.wait_ge(row0_in[p % R0], 16 * (p // R0 + 1))
                if p == 0:
                    pool.tensor_copy(ax0, row0[0]).then_inc(xsum_done, 1)
                else:
                    pool.tensor_tensor(ax0, ax0, row0[p % R0], ALU.add).then_inc(xsum_done, 1)
                pool.wait_ge(xsq_done, order0(p) + 1)
                if p == 0:
                    pool.tensor_copy(as0, sq0[0]).then_inc(sqsum0_done, 1)
                else:
                    pool.wait_ge(sqsum0_done, p)
                    pool.tensor_tensor(as0, as0, sq0[p % 2], ALU.add).then_inc(sqsum0_done, 1)
            pool.wait_ge(xsum_done, 2 * NP + 1)
            pool.tensor_tensor(ax1, ax1, sq1[0], ALU.add).then_inc(xsum_done, 1)
            for i in range(2 * E):
                pool.wait_ge(whi_done, i + 1)
                hi, lo = (w1h, w1l) if i < E else (w2h, w2l)
                j = i % E
                pool.tensor_tensor(lo[:, j * FF:(j + 1) * FF], stage[i % NST], hi[:, j * FF:(j + 1) * FF],
                                   ALU.subtract).then_inc(wlo_done, 1)
            with pool.Fori(0, G) as g:
                for e in range(E):
                    pool.wait_ge(tmp_ready, g * E + e + 1)
                    if e == 0:
                        pool.wait_ge(acc_init, g + 1)
                    else:
                        pool.wait_ge(acc_step, g * E + e)
                    pool.tensor_tensor(acc, acc, tmp[e % 2], ALU.add).then_inc(acc_step, 1)

        @block.scalar
        def _(act):
            act.dma_start(edge_i[:, :], edge).then_inc(edge_in, 16)
            act.dma_start(packs["pack_b"][:, :], pack_b).then_inc(pack_b_in, 16)

            def prep_evac():
                act.wait_ge(pe_prep, 1)
                nc.scalar.activation(conv_u[:, :], hid_ps[0][:, 0, 0:NP * NP], ACT.Copy).then_inc(act_prep, 1)
                nc.scalar.activation(conv_b[:, :], hid_ps[0][:, 1, 0:NP * NP], ACT.Identity,
                                     bias=col(COL_TB)).then_inc(act_prep, 1)
                act.wait_ge(dve_prep, 1)
                nc.scalar.activation(deg[:, 1:2], deg[:, 0:1], ACT.Sqrt).then_inc(act_prep, 1)
                act.wait_ge(pe_prep, 4)
                nc.scalar.activation(adj, eo_ps[:, 0, 0:128], ACT.Copy).then_inc(act_prep, 1)
                act.wait_ge(pe_prep, 6)
                nc.scalar.activation(gcn_c[:, :], eo_ps[:, 0, 128:129], ACT.Identity,
                                     bias=col(COL_BP)).then_inc(act_prep, 1)
                nc.scalar.activation(wvo[:, 0:D], eo_ps[:, 1, 0:D], ACT.Copy).then_inc(act_prep, 1)
                nc.scalar.activation(wvo[:, D:2 * D], hid_ps[0][:, 0, 0:D], ACT.Copy).then_inc(act_prep, 1)
                act.wait_ge(pe_prep, 8)
                nc.scalar.activation(att_b[:, 0:3], eo_ps[:, 0, 256:259], ACT.Copy).then_inc(act_prep, 1)
                act.wait_ge(dve_prep, PREP_DVE)
                nc.scalar.activation(att_b[:, 3:4], eo_ps[:, 0, 256:257], ACT.Identity,
                                     scale=gq[:, 1:2]).then_inc(act_prep, 1)

            def squares1(a):
                act.wait_ge(row1_in[a % R1], 16 * (a // R1 + 1))
                if a >= 2:
                    act.wait_ge(sqsum1_done, a - 1)
                nc.scalar.activation(sq1[a % 2], row1[a % R1], ACT.Square).then_inc(xsq_done, 1)

            def squares0(p):
                act.wait_ge(row0_in[p % R0], 16 * (p // R0 + 1))
                if p >= 2:
                    act.wait_ge(sqsum0_done, p - 1)
                nc.scalar.activation(sq0[p % 2], row0[p % R0], ACT.Square).then_inc(xsq_done, 1)

            def tokens_out(p):
                act.wait_ge(conv_done, p + 1)
                dst = ht[:, :].rearrange("p (b t) -> p t b", t=TOK)[:, 1 + p * NP:1 + (p + 1) * NP, :]
                nc.scalar.activation(dst, flat(fr_ps)[:, 0:N0].rearrange("p (j b) -> p j b", b=B),
                                     ACT.Copy).then_inc(tok_done, 1)

            squares1(0)
            for p in range(NP):
                squares1(p + 1)
                squares0(p)
                if p:
                    tokens_out(p - 1)
                if p == 2:
                    prep_evac()
            tokens_out(NP - 1)
            act.wait_ge(pack_b_in, 16)
            nc.scalar.activation(ht[:, :].rearrange("p (b t) -> p t b", t=TOK)[:, 0, :],
                                 col(COL_CLS).broadcast_to([128, B]), ACT.Copy).then_inc(tok_done, 1)
            act.wait_ge(stat_step, 14)
            nc.scalar.activation(stat[:, 5 * B:6 * B], stat[:, 4 * B:5 * B], ACT.Sqrt, bias=eps[:, 0:1]).then_inc(act_stat, 1)

            for i in range(2 * E):
                act.wait_ge(wstage_in, 16 * (i + 1))
                hi = w1h if i < E else w2h
                j = i % E
                nc.scalar.activation(hi[:, j * FF:(j + 1) * FF], stage[i % NST], ACT.Copy).then_inc(whi_done, 1)

            def var_evac(g, kind, ready, n, scale, at):
                act.wait_ge(ready, g + 1)
                nc.scalar.activation(root_in[:, ROOTS[kind]], fr_ps[0:QC, 0, 0:n], ACT.Identity,
                                     bias=eps[0:QC, at:at + 1], scale=scale).then_inc(var_out[kind], 1)

            def row_evac(g, kind, rows):
                act.wait_ge(row_ps[kind], g + 1)
                nc.scalar.activation(two(fac[0:rows, :]), halves(fr_ps)[0:rows], ACT.Copy).then_inc(row_out[kind], 1)

            def early(g, step):
                if step == "sq":
                    act.wait_ge(dev_ready, g + 1)
                    nc.scalar.activation(sq, dev, ACT.Square).then_inc(sq_ready, 1)
                if step == "var":
                    var_evac(g, "ln1", var_ps, TILES, 1.0, 1)
                if step == "row":
                    row_evac(g, "ln1", 1)
                if step[:4] == "relu":
                    c = int(step[4])
                    act.wait_ge(g_ps, g + 1)
                    nc.scalar.activation(two(h1[:, c * T:(c + 1) * T]), halves(fr_ps), ACT.Relu,
                                         bias=scal[:, 4 + c:5 + c], scale=scal[:, c:c + 1]).then_inc(h1_ready, 1)

            def graph(g, step):
                if step == "sq2":
                    act.wait_ge(dev2_ready, g + 1)
                    nc.scalar.activation(sq, dev, ACT.Square).then_inc(sq2_ready, 1)
                if step == "var2":
                    var_evac(g, "ln2", var2_ps, TILES, 1.0 + EPS_LN, 2)
                if step == "row2":
                    row_evac(g, "ln2", 1)

            def queries_keys(g, step):
                if step == "q":
                    act.wait_ge(q_ps, g + 1)
                    nc.scalar.activation(two(sqq), halves(fr_ps), ACT.Square, bias=att_b[:, 0:1]).then_inc(ss_ready, 1)
                    nc.scalar.activation(two(qs), halves(fr_ps), ACT.Identity, bias=att_b[:, 3:4],
                                         scale=gq[:, 1:2]).then_inc(q_ready, 1)
                if step == "k":
                    act.wait_ge(k_ps, g + 1)
                    nc.scalar.activation(two(sqk), halves(fr_ps), ACT.Square, bias=att_b[:, 1:2]).then_inc(ss_ready, 1)
                    nc.scalar.activation(two(kb), halves(fr_ps), ACT.Identity, bias=att_b[:, 1:2]).then_inc(k_ready, 1)
                if step == "sums":
                    var_evac(g, "qk", ss_ps, 4 * TILES, 1.0, 3)
                if step == "krow":
                    row_evac(g, "qk", H)

            def values_evac(g, b, later):
                act.wait_ge(vp_ps, g * NB + b + 1)
                if b == 0 and later:
                    act.wait_ge(tmp_ready, g * E - 1)
                nc.scalar.activation(vp[:, b * 512:(b + 1) * 512], hid_ps[b // 2][0:QC, b % 2, :],
                                     ACT.Copy).then_inc(vp_ready, 1)

            def exps(g, b):
                act.wait_ge(nb_ready, g * (NB // 2) + b // 2 + 1)
                for c in range(2):
                    for h in range(H):
                        n = 4 * b + 2 * c + h
                        o0, w = score_at(h, c)
                        nc.scalar.activation(probs[:, b * SCORE + o0:b * SCORE + o0 + w],
                                             score_ps_at(b)[:, h, c * QC:c * QC + w], ACT.Exp,
                                             bias=nbias[:, n:n + 1], scale=rq[:, n:n + 1],
                                             accum_out=sm[:, n:n + 1]).then_inc(exp_ready, 1)

            def attention(g, later, ahead):
                for b in range(NB):
                    values_evac(g, b, later)
                for b in range(NB):
                    exps(g, b)
                if ahead:
                    graph(g + 1, "sq2")
                    graph(g + 1, "var2")
                act.wait_ge(pv_ps, NB * (g + 1))
                nc.scalar.activation(two(y32), halves(hid_ps[0]), ACT.Identity, bias=att_b[:, 2:3]).then_inc(y_ready, 1)
                act.wait_ge(lg_step, 3 * (g + 1))
                nc.scalar.activation(lge[:, :], lg[:, :], ACT.Exp).then_inc(lge_ready, 1)

            def experts(g, slot):
                n = g * SLOTS + slot
                act.wait_ge(hid_ps_ready, n + 1)
                if slot >= 2:
                    act.wait_ge(hlo_ready, n - 1)
                nc.scalar.activation(two(hid[slot % 2]), halves(hid_ps[slot % 2]), ACT.Gelu_apprx_tanh,
                                     bias=col(COL_B1 + slot)).then_inc(hid_ready, 1)
                if slot % 2:
                    if slot >= 3:
                        act.wait_ge(chunk_used, n - 2)
                    nc.scalar.activation(two(hh[slot % 3]), halves(hid_ps[slot % 2]), ACT.Gelu_apprx_tanh,
                                         bias=col(COL_B1 + slot)).then_inc(hhi_act, 1)

            def ffn(g, ahead):
                for slot in range(SLOTS):
                    experts(g, slot)
                    for slots, step_of, n in ((LN2_SLOTS, graph, 1), (QK_SLOTS, queries_keys, 1),
                                              (EARLY_SLOTS, early, 2)):
                        if n == 1 or ahead:
                            for step in steps_in(slots, slot):
                                step_of(g + n, step)

            for step in EARLY_SLOTS:
                early(0, step)
            for step in ("sq2", "var2", "row2"):
                graph(0, step)
            for step in QK_SLOTS:
                queries_keys(0, step)
            for step in EARLY_SLOTS:
                early(1, step)
            attention(0, False, True)
            with act.Fori(1, G - 1) as g:
                ffn(g - 1, True)
                attention(g, True, True)
            ffn(G - 2, False)
            attention(G - 1, True, False)
            for slot in range(SLOTS):
                experts(G - 1, slot)

        @block.tensor
        def _(pe):
            mm, tr = nc.tensor.matmul, nc.tensor.transpose
            pe.wait_ge(consts_ready, 1)
            pe.wait_ge(pack_a_in, 16)
            pe.wait_ge(pack_b_in, 16)

            def prepare():
                for n, src in enumerate((gam, beta)):
                    for s in range(SHIFTS):
                        last = mm(hid_ps[0][:, n, 0:NP * NP], conv_w[:, s * D:(s + 1) * D],
                                  src[:, s * NP * NP:(s + 1) * NP * NP], start=(s == 0), stop=(s == SHIFTS - 1))
                last.then_inc(pe_prep, 1)
                pe.wait_ge(pool_prep, PREP_POOL)
                for k in range(EK):
                    mm(hid_ps[1][:, 0, 0:D], oh[:, (EK + k) * D:(EK + k + 1) * D], oh[:, k * D:(k + 1) * D],
                       start=(k == 0), stop=False)
                mm(hid_ps[1][:, 0, 0:D], ident16[:, :], ident16[:, :], start=False, stop=True).then_inc(pe_prep, 1)
                pe.wait_ge(dve_prep, 3)
                tr(hid_ps[1][:, 1, 0:D], adj_n, ident[:, :]).then_inc(pe_prep, 1)
                pe.wait_ge(dve_prep, 4)
                tr(eo_ps[:, 0, 0:D], adj_t[:, :], ident[:, :]).then_inc(pe_prep, 1)
                pe.wait_ge(act_prep, 4)
                mm(hid_ps[1][:, 0, :], adj, wp_t[:, D:5 * D], start=True, stop=True).then_inc(pe_prep, 1)
                for k in range(4):
                    mm(eo_ps[:, 0, D:D + 1], wp_t[:, (k + 1) * D:(k + 2) * D], scal[:, 24 + k:25 + k],
                       start=(k == 0), stop=(k == 3))
                for h in range(H):
                    last = mm(eo_ps[:, 1, 0:D] if h == 0 else hid_ps[0][:, 0, 0:D], wv_t[h * DH:(h + 1) * DH, :],
                              wo_s[h * DH:(h + 1) * DH, :], start=True, stop=True)
                last.then_inc(pe_prep, 1)
                pe.wait_ge(act_prep, 7)
                mm(eo_ps[:, 0, 2 * D:2 * D + 1], wq_s, col(COL_LNB), start=True, stop=True)
                mm(eo_ps[:, 0, 2 * D + 1:2 * D + 2], wk_s, col(COL_LNB), start=True, stop=True).then_inc(pe_prep, 1)
                for h in range(H):
                    last = mm(eo_ps[:, 0, 2 * D + 2:2 * D + 3], wvo[:, h * D:(h + 1) * D], col(COL_LNB),
                              start=(h == 0), stop=(h == H - 1))
                last.then_inc(pe_prep, 1)

            def conv(p):
                pe.wait_ge(mul_done, p + 1)
                if p:
                    pe.wait_ge(tok_done, p)
                for s in range(SHIFTS):
                    for a, b in ((0, 512), (512, N0)):
                        last = mm(flat(fr_ps)[:, a:b], conv_w[:, s * D:(s + 1) * D], xg[p % 2][s][:, a:b],
                                  start=(s == 0), stop=(s == SHIFTS - 1))
                last.then_inc(conv_done, 1)

            for p in range(NP):
                conv(p)
                if p == 1:
                    prepare()
            pe.wait_ge(stat_step, 10)
            mm(hid_ps[0][:, 0, 0:2 * B], count_m[:, :], stat[:, 0:2 * B], start=True, stop=True).then_inc(pe_stat, 1)
            pe.wait_ge(tok_done, NP + 1)
            pe.wait_ge(wlo_done, 2 * E)

            def both(lhs, rhs, start=True, stop=True):
                for j in range(2):
                    last = mm(fr_ps[:, j, 0:TH], lhs, rhs[:, j, :], start=start, stop=stop)
                return last

            def row_of(g, kind, first, rows):
                pe.wait_ge(root_ready[kind], g + 1)
                for t in range(TILES):
                    b, m = t // NB, t % NB
                    last = tr(fr_ps[0:rows, b, m * QC:(m + 1) * QC],
                              root[:, first + t * rows:first + (t + 1) * rows], ident[0:QC, 0:QC])
                last.then_inc(row_ps[kind], 1)

            def cast(g, kind, rows):
                pe.wait_ge(row_out[kind], g + 1)
                both(head_sel[:, :] if rows == H else ones_r[:, :], two(fac[0:rows, :])).then_inc(cast_ps[kind], 1)

            def means(src):
                for t in range(TILES):
                    last = mm(fr_ps[0:QC, 0, t:t + 1], src[:, t * QC:(t + 1) * QC], mean_m[:, 0:1],
                              start=True, stop=True)
                return last

            def early(g, step, later=True):
                if step == "mean":
                    pe.wait_ge(fixed, g + 1)
                    if later:
                        pe.wait_ge(kn_ready, g)
                    both(mean_m[:, :], tokens(g)).then_inc(mean_ps, 1)
                if step == "var":
                    pe.wait_ge(sq_ready, g + 1)
                    means(sq).then_inc(var_ps, 1)
                if step == "row":
                    row_of(g, "ln1", 4 * TILES, 1)
                if step == "cast":
                    cast(g, "ln1", 1)
                if step == "edges":
                    pe.wait_ge(xn_ready, g + 1)
                    both(adj_t[:, :], two(dev)).then_inc(g_ps, 1)

            def graph(g, step):
                if step == "plain":
                    pe.wait_ge(h1_ready, 4 * (g + 1))
                    both(wp_t[:, 0:D], two(dev), stop=False)
                if step in range(4):
                    last = both(gcn_m[:, step * D:(step + 1) * D], two(h1[:, step * T:(step + 1) * T]),
                                start=False, stop=(step == 3))
                    if step == 3:
                        last.then_inc(gcn_ps, 1)
                if step == "mean2":
                    pe.wait_ge(h2_ready, g + 1)
                    both(mean_m[:, :], tokens(g)).then_inc(mean2_ps, 1)
                if step == "var2":
                    pe.wait_ge(sq2_ready, g + 1)
                    means(sq).then_inc(var2_ps, 1)
                if step == "row2":
                    row_of(g, "ln2", 5 * TILES, 1)
                if step == "cast2":
                    cast(g, "ln2", 1)

            def queries_keys(g, step, later=True):
                if step == "q":
                    pe.wait_ge(hx_ready, g + 1)
                    if later:
                        pe.wait_ge(acc_init, g)
                    both(wq_s, two(xh)).then_inc(q_ps, 1)
                if step == "k":
                    pe.wait_ge(q_ready, g + 1)
                    both(wk_s, two(xh)).then_inc(k_ps, 1)
                if step == "sums":
                    pe.wait_ge(k_ready, g + 1)
                    pe.wait_ge(ss_ready, 2 * (g + 1))
                    for n, src in enumerate((sqq, sqk)):
                        for t in range(TILES):
                            c = 2 * (n * TILES + t)
                            last = mm(fr_ps[0:QC, 0, c:c + 2], src[:, t * QC:(t + 1) * QC],
                                      head_m[:, 0:DH + 1:DH], start=True, stop=True)
                    last.then_inc(ss_ps, 1)
                if step == "krow":
                    row_of(g, "qk", 2 * TILES, H)
                if step == "kcast":
                    cast(g, "qk", H)

            def values(g, b, later):
                if b == 0 and later:
                    pe.wait_ge(hid_ready, g * SLOTS - 1)
                if b == 2 and later:
                    pe.wait_ge(hhi_act, g * (SLOTS // 2))
                for k in range(2):
                    t = 2 * b + k
                    last = mm(hid_ps[b // 2][0:QC, b % 2, k * H * D:(k + 1) * H * D], xh[:, t * QC:(t + 1) * QC],
                              wvo[:, :], start=True, stop=True)
                last.then_inc(vp_ps, 1)

            def scores(g, b):
                if b == 0:
                    pe.wait_ge(kn_ready, g + 1)
                pe.wait_ge(vp_ready, g * NB + 2 * (b // 2) + 2)
                ps = score_ps_at(b)
                for h in range(H):
                    p = slice(h * DH, (h + 1) * DH)
                    for c in range(2):
                        w = (c + 1) * QC
                        mm(ps[:, h, c * QC:c * QC + w], qs[p, (2 * b + c) * QC:(2 * b + c + 1) * QC],
                           kb[p, b * TOK:b * TOK + w], start=True, stop=False)
                        last = mm(ps[:, h, c * QC + w - QC:c * QC + w], identb[:, :], mask[:, :], start=False, stop=True)
                last.then_inc(score_ps, 1)

            def turn_probs(g, b, later):
                pe.wait_ge(p_ready, g * NB + b + 1)
                if b >= 2:
                    pe.wait_ge(pt_ready, g * NB + b - 1)
                elif later:
                    pe.wait_ge(tmp_ready, g * E)
                for n in range(3 * H):
                    last = tr(eo_ps[0:QC, b % 2, n * QC:(n + 1) * QC],
                              probs[:, b * SCORE + n * QC:b * SCORE + (n + 1) * QC], ident[0:QC, 0:QC])
                last.then_inc(pt_ps, 1)

            def weigh(g, b):
                pe.wait_ge(pt_ready, g * NB + b + 1)
                for k in range(2):
                    for h in range(H):
                        v0 = b * 512 + k * H * D + h * D
                        p0 = h * 3 * QC + k * TOK
                        y0 = (b % 2) * TOK
                        last = mm(hid_ps[0][:, b // 2, y0 + k * QC:y0 + TOK], vp[:, v0:v0 + D],
                                  pt[b % 2][0:QC, p0:p0 + TOK - k * QC],
                                  start=(k == 0 and h == 0), stop=(k == 1 and h == H - 1))
                last.then_inc(pv_ps, 1)

            def gates(g, step):
                if step == "turn":
                    pe.wait_ge(gate_step, 3 * (g + 1))
                    for t in range(TILES):
                        b, m = t // NB, t % NB
                        last = tr(eo_ps[0:E, b, m * QC:(m + 1) * QC], gts[:, t * E:(t + 1) * E], ident[0:QC, 0:QC])
                    last.then_inc(gt_ps, 1)
                if step == "bias":
                    pe.wait_ge(gt_ready, g + 1)
                    both(b2_s, two(gt_t[:, :])).then_inc(b2_ps, 1)

            def attention(g, later, ahead):
                def graph_of(*steps):
                    if ahead:
                        for step in steps:
                            graph(g + 1, step)

                if not later:
                    values(g, 0, later)
                    values(g, 1, later)
                values(g, 2, later)
                values(g, 3, later)
                scores(g, 0)
                scores(g, 1)
                graph_of("plain", 0)
                scores(g, 2)
                scores(g, 3)
                graph_of(1, 2)
                turn_probs(g, 0, later)
                turn_probs(g, 1, later)
                graph_of(3)
                weigh(g, 0)
                weigh(g, 1)
                graph_of("mean2")
                turn_probs(g, 2, later)
                turn_probs(g, 3, later)
                graph_of("var2")
                weigh(g, 2)
                weigh(g, 3)
                pe.wait_ge(y_ready, g + 1)
                pe.wait_ge(pt_ready, NB * (g + 1))
                for t in range(TILES):
                    last = mm(eo_ps[0:QC, 0, t * E:(t + 1) * E], y32[:, t * QC:(t + 1) * QC], gate_ws,
                              start=True, stop=True)
                last.then_inc(logit_ps, 1)

            def experts_in(g, slot):
                n = g * SLOTS + slot
                if slot == 0:
                    pe.wait_ge(yl_ready, g + 1)
                elif slot >= 2 and slot % 2 == 0:
                    pe.wait_ge(hid_ready, n - 1)
                elif slot >= 2:
                    pe.wait_ge(hhi_act, g * (SLOTS // 2) + (slot - 1) // 2)
                w = slice(slot * D, (slot + 1) * D)
                for i, (lhs, rhs) in enumerate(((w1h, yh), (w1h, yl), (w1l, yh))):
                    for j in range(2):
                        last = mm(hid_ps[slot % 2][:, j, 0:TH], lhs[:, w], rhs[:, j * TH:(j + 1) * TH],
                                  start=(i == 0), stop=(i == 2))
                last.then_inc(hid_ps_ready, 1)

            def experts_out(g, m):
                n = g * SLOTS + m
                pe.wait_ge(hlo_ready, n + 1)
                if m == 0:
                    pe.wait_ge(gt_ready, g + 1)
                if m and m % CH == 0:
                    pe.wait_ge(tmp_ready, g * E + m // CH)
                w = slice(m * D, (m + 1) * D)
                for i, (lhs, rhs) in enumerate(((w2h, hh[m % 3]), (w2h, hl[m % 3]), (w2l, hh[m % 3]))):
                    for j in range(2):
                        last = mm(eo_ps[:, j, 0:TH], lhs[:, w], rhs[:, j * TH:(j + 1) * TH],
                                  start=(m % CH == 0 and i == 0), stop=(m % CH == CH - 1 and i == 2))
                last.then_inc(chunk_used, 1)

            def ffn(g, ahead):
                for slot in range(SLOTS + LAG):
                    if slot < SLOTS:
                        experts_in(g, slot)
                        for slots, step_of, n in ((LN2_SLOTS, graph, 1), (GATE_SLOTS, gates, 0),
                                                  (QK_SLOTS, queries_keys, 1), (EARLY_SLOTS, early, 2)):
                            if n < 2 or ahead:
                                for step in steps_in(slots, slot):
                                    step_of(g + n, step)
                    else:
                        values(g + 1, slot - SLOTS, True)
                    if slot >= LAG:
                        experts_out(g, slot - LAG)

            for step in EARLY_SLOTS:
                early(0, step, later=False)
            for step in ("plain", 0, 1, 2, 3, "mean2", "var2", "row2", "cast2"):
                graph(0, step)
            for step in QK_SLOTS:
                queries_keys(0, step, later=False)
            for step in EARLY_SLOTS:
                early(1, step)
            attention(0, False, True)
            with pe.Fori(1, G - 1) as g:
                ffn(g - 1, True)
                attention(g, True, True)
            ffn(G - 2, False)
            attention(G - 1, True, False)
            for slot in range(SLOTS + LAG):
                if slot < SLOTS:
                    experts_in(G - 1, slot)
                    for step in steps_in(GATE_SLOTS, slot):
                        gates(G - 1, step)
                if slot >= LAG:
                    experts_out(G - 1, slot - LAG)

        @block.vector
        def _(dve):
            v = nc.vector
            def prepare():
                dve.wait_ge(pe_prep, 2)
                v.tensor_reduce(deg[:, 0:1], hid_ps[1][:, 0, 0:D], AX.X, ALU.add).then_inc(dve_prep, 1)
                dve.wait_ge(act_prep, 3)
                v.reciprocal(deg[:, 2:3], deg[:, 1:2]).then_inc(dve_prep, 1)
                dve.wait_ge(dve_prep, 2)
                v.tensor_scalar(adj_n, hid_ps[1][:, 0, 0:D], deg[:, 2:3], None, ALU.mult).then_inc(dve_prep, 1)
                dve.wait_ge(pe_prep, 3)
                v.tensor_scalar(adj_t[:, :], hid_ps[1][:, 1, 0:D], deg[:, 2:3], None, ALU.mult).then_inc(dve_prep, 1)
                dve.wait_ge(pe_prep, 5)
                for k in range(4):
                    src = hid_ps[1][:, 0, k * D:(k + 1) * D]
                    for c in range(4):
                        dst, w = gcn_m[:, c * D:(c + 1) * D], scal[:, 8 + 4 * c + k:9 + 4 * c + k]
                        if k == 0:
                            v.tensor_scalar(dst, src, w, None, ALU.mult).then_inc(dve_prep, 1)
                        else:
                            dve.wait_ge(dve_prep, 4 + 4 * (k - 1) + c + 1)
                            v.scalar_tensor_tensor(dst, src, w, dst, ALU.mult, ALU.add).then_inc(dve_prep, 1)
                v.tensor_scalar(gq[:, 0:1], col(COL_QN), float(DH) ** 0.5, None, ALU.mult).then_inc(dve_prep, 1)
                dve.wait_ge(dve_prep, 21)
                v.tensor_tensor(gq[:, 1:2], gq[:, 0:1], col(COL_KN), ALU.mult).then_inc(dve_prep, 1)

            dve.wait_ge(pack_a_in, 16)
            gam_v = gam.rearrange("p (s i j) -> p s i j", s=SHIFTS, i=NP)

            def square_sum(a):
                dve.wait_ge(xsq_done, order1(a) + 1)
                if a == 0:
                    v.tensor_scalar(as1, sq1[0], 0.5, None, ALU.mult).then_inc(sqsum1_done, 1)
                else:
                    dve.wait_ge(sqsum1_done, a)
                    v.scalar_tensor_tensor(as1, sq1[a % 2], 0.5 if a == NP else 1.0, as1,
                                           ALU.mult, ALU.add).then_inc(sqsum1_done, 1)

            for p in range(NP):
                if p == 0:
                    dve.wait_ge(row1_in[0], 16)
                dve.wait_ge(row1_in[(p + 1) % R1], 16 * ((p + 1) // R1 + 1))
                dve.wait_ge(row0_in[p % R0], 16 * (p // R0 + 1))
                if p >= 2:
                    dve.wait_ge(conv_done, p - 1)
                upper, lower = row1[p % R1], row1[(p + 1) % R1]
                for s, (src, c0) in enumerate(((row0[p % R0], 0), (lower, 0), (lower, 1), (upper, 0), (upper, 1))):
                    gv = gam_v[:, s, p, :].unsqueeze(2).broadcast_to([128, NP, B])
                    last = v.tensor_tensor(xg[p % 2][s].rearrange("p (j b) -> p j b", b=B),
                                           src[:, c0 * B:(c0 + NP) * B].rearrange("p (j b) -> p j b", b=B),
                                           gv, ALU.mult)
                last.then_inc(mul_done, 1)
                if p == 0:
                    square_sum(0)
                square_sum(p + 1)
                if p == 2:
                    dve.wait_ge(pack_b_in, 16)
                    prepare()
            dve.wait_ge(xsum_done, 2 * NP + 2)
            dve.wait_ge(sqsum0_done, NP)
            dve.wait_ge(sqsum1_done, NG1)
            for n, (a1, a0) in enumerate(((ax1, ax0), (as1, as0))):
                s1, s0, side = (stat[:, k * B:(k + 1) * B] for k in (2 + n, 4 + n, 6 + n))
                v.tensor_reduce(s1, a1.rearrange("p (c b) -> p b c", b=B), AX.X, ALU.add).then_inc(stat_step, 1)
                v.tensor_reduce(s0, a0.rearrange("p (c b) -> p b c", b=B), AX.X, ALU.add).then_inc(stat_step, 1)
                v.tensor_tensor(side, a1[:, 0:B], a1[:, N1 - B:N1], ALU.add).then_inc(stat_step, 1)
            dve.wait_ge(stat_step, 6)
            v.scalar_tensor_tensor(stat[:, 4 * B:6 * B], stat[:, 2 * B:4 * B], 4.0, stat[:, 4 * B:6 * B],
                                   ALU.mult, ALU.add).then_inc(stat_step, 3)
            dve.wait_ge(stat_step, 9)
            v.scalar_tensor_tensor(stat[:, 0:2 * B], stat[:, 6 * B:8 * B], -2.0, stat[:, 4 * B:6 * B],
                                   ALU.mult, ALU.add).then_inc(stat_step, 1)
            dve.wait_ge(pe_stat, 1)
            v.tensor_copy(stat[:, 2 * B:3 * B], hid_ps[0][:, 0, 0:B]).then_inc(stat_step, 1)
            dve.wait_ge(stat_step, 11)
            v.tensor_tensor(stat[:, 3 * B:4 * B], stat[:, 2 * B:3 * B], stat[:, 2 * B:3 * B], ALU.mult).then_inc(stat_step, 1)
            dve.wait_ge(stat_step, 12)
            v.tensor_tensor(stat[:, 4 * B:5 * B], hid_ps[0][:, 0, B:2 * B], stat[:, 3 * B:4 * B],
                            ALU.subtract).then_inc(stat_step, 2)
            dve.wait_ge(act_stat, 1)
            v.reciprocal(img[:, 0:B], stat[:, 5 * B:6 * B]).then_inc(stat_step, 1)
            dve.wait_ge(stat_step, 15)
            v.scalar_tensor_tensor(img[:, B:2 * B], stat[:, 2 * B:3 * B], -1.0, img[:, 0:B],
                                   ALU.mult, ALU.mult).then_inc(stat_step, 1)
            dve.wait_ge(stat_step, 16)
            dve.wait_ge(act_prep, PREP_ACT)
            dve.wait_ge(tok_done, NP + 1)
            dve.wait_ge(conv_done, NP)

            def roots(g, kind, n):
                x, y, t = (buf[:, ROOTS[kind]] for buf in (root_in, root, root_t))
                if n == 0:
                    dve.wait_ge(var_out[kind], g + 1)
                    v.tensor_scalar(y.bitcast(I32), x.bitcast(I32), -0.5, float(RSQRT_SEED),
                                    ALU.mult, ALU.add).then_inc(root_step[kind], 1)
                dve.wait_ge(root_step[kind], 9 * g + 3 * n + 1)
                v.scalar_tensor_tensor(t, y, -0.5, y, ALU.mult, ALU.mult).then_inc(root_step[kind], 1)
                dve.wait_ge(root_step[kind], 9 * g + 3 * n + 2)
                v.tensor_tensor(t, t, x, ALU.mult).then_inc(root_step[kind], 1)
                dve.wait_ge(root_step[kind], 9 * g + 3 * n + 3)
                v.scalar_tensor_tensor(y, t, 1.5, y, ALU.add, ALU.mult).then_inc(
                    root_step[kind] if n < 2 else root_ready[kind], 1)

            def early(g, step):
                if step == "fix":
                    for b in range(NB):
                        v.scalar_tensor_tensor(fix[:, b * NP * NP:(b + 1) * NP * NP], conv_u[:, :],
                                               img[:, bass.ds(g * NB + (B + b), 1)], conv_b[:, :],
                                               ALU.mult, ALU.add).then_inc(fix_step, 1)
                    for b in range(NB):
                        dve.wait_ge(fix_step, NB * g + (b + 1))
                        h_b = ht[:, bass.ds(g * T + (b * TOK + 1), NP * NP)]
                        last = v.scalar_tensor_tensor(h_b, h_b, img[:, bass.ds(g * NB + b, 1)],
                                                      fix[:, b * NP * NP:(b + 1) * NP * NP], ALU.mult, ALU.add)
                    last.then_inc(fixed, 1)
                if step == "dev":
                    dve.wait_ge(mean_ps, g + 1)
                    v.tensor_tensor(two(dev), tokens(g), halves(fr_ps), ALU.subtract).then_inc(dev_ready, 1)
                if step[:4] == "root":
                    roots(g, "ln1", int(step[4]))
                if step == "xn":
                    dve.wait_ge(cast_ps["ln1"], g + 1)
                    v.tensor_tensor(two(dev), two(dev), halves(fr_ps), ALU.mult).then_inc(xn_ready, 1)

            def graph(g, step):
                if step == "h2":
                    dve.wait_ge(gcn_ps, g + 1)
                    v.scalar_tensor_tensor(tokens(g), halves(fr_ps), gcn_c[:, 0:1], tokens(g),
                                           ALU.add, ALU.add).then_inc(h2_ready, 1)
                if step == "dev2":
                    dve.wait_ge(mean2_ps, g + 1)
                    dve.wait_ge(h2_ready, g + 1)
                    v.tensor_tensor(two(dev), tokens(g), halves(fr_ps), ALU.subtract).then_inc(dev2_ready, 1)
                if step == "roots2":
                    for n in range(3):
                        roots(g, "ln2", n)
                if step == "hx":
                    dve.wait_ge(cast_ps["ln2"], g + 1)
                    v.scalar_tensor_tensor(two(xh), two(dev), col(COL_LNG), halves(fr_ps),
                                           ALU.mult, ALU.mult).then_inc(hx_ready, 1)

            def queries_keys(g, step):
                if step[:4] == "root":
                    roots(g, "qk", int(step[4]))
                if step == "kn":
                    dve.wait_ge(cast_ps["qk"], g + 1)
                    v.tensor_tensor(two(kb), two(kb), halves(fr_ps), ALU.mult).then_inc(kn_ready, 1)

            def maxima(g, m):
                dve.wait_ge(score_ps, (g * (NB // 2) + m + 1) * 2)
                mx4 = mx[:, 8 * m:8 * m + 8].rearrange("p (i c h) -> p c i h", c=2, h=H)
                ps = hid_ps[m][0:QC, :, 0:2 * 3 * QC].rearrange("p h (i n) -> p i h n", i=2)
                for c in range(2):
                    v.tensor_reduce(mx4[:, c], ps[:, :, :, c * QC:(2 * c + 1) * QC],
                                    AX.X, ALU.max).then_inc(max_ready, 1)
                dve.wait_ge(max_ready, 2 * (g * (NB // 2) + m + 1))
                v.scalar_tensor_tensor(nbias[:, 8 * m:8 * m + 8], mx[:, 8 * m:8 * m + 8], -1.0,
                                       rq[:, 8 * m:8 * m + 8], ALU.mult, ALU.mult).then_inc(nb_ready, 1)

            def normalise(g, b):
                dve.wait_ge(exp_ready, 4 * (g * NB + b + 1))
                v.reciprocal(rs[:, 4 * b:4 * b + 4], sm[:, 4 * b:4 * b + 4]).then_inc(rs_ready, 1)
                dve.wait_ge(rs_ready, g * NB + b + 1)
                for c in range(2):
                    for h in range(H):
                        o0, w = score_at(h, c)
                        p = probs[:, b * SCORE + o0:b * SCORE + o0 + w]
                        n = 4 * b + 2 * c + h
                        last = v.tensor_scalar(p, p, rs[:, n:n + 1], None, ALU.mult)
                last.then_inc(p_ready, 1)

            def turned(g, b):
                dve.wait_ge(pt_ps, g * NB + b + 1)
                if b >= 2:
                    dve.wait_ge(pv_ps, g * NB + b - 1)
                v.tensor_copy(pt[b % 2][0:QC, :], eo_ps[0:QC, b % 2, 0:SCORE]).then_inc(pt_ready, 1)

            def attention(g, later, ahead):
                maxima(g, 0)
                maxima(g, 1)
                normalise(g, 0)
                normalise(g, 1)
                turned(g, 0)
                turned(g, 1)
                if ahead:
                    graph(g + 1, "h2")
                normalise(g, 2)
                normalise(g, 3)
                if ahead:
                    graph(g + 1, "dev2")
                turned(g, 2)
                turned(g, 3)
                dve.wait_ge(y_ready, g + 1)
                v.tensor_copy(yh, y32).then_inc(yh_ready, 1)
                dve.wait_ge(yh_ready, g + 1)
                v.tensor_tensor(yl, y32, yh, ALU.subtract).then_inc(yl_ready, 1)
                if ahead:
                    graph(g + 1, "roots2")
                dve.wait_ge(logit_ps, g + 1)
                lg3 = lg[:, :].rearrange("p (t e) -> p t e", e=E)
                v.tensor_tensor(lg3, eo_ps[0:QC, 0, 0:TILES * E].rearrange("p (t e) -> p t e", e=E),
                                gate_bs.unsqueeze(1).broadcast_to([QC, TILES, E]), ALU.add).then_inc(lg_step, 1)
                dve.wait_ge(lg_step, 3 * g + 1)
                v.tensor_reduce(gm[:, 0:TILES], lg3, AX.X, ALU.max).then_inc(lg_step, 1)
                dve.wait_ge(lg_step, 3 * g + 2)
                v.tensor_tensor(lg3, lg3, gm[:, 0:TILES].unsqueeze(2).broadcast_to([QC, TILES, E]),
                                ALU.subtract).then_inc(lg_step, 1)
                dve.wait_ge(lge_ready, g + 1)
                lge3 = lge[:, :].rearrange("p (t e) -> p t e", e=E)
                v.tensor_reduce(gm[:, TILES:2 * TILES], lge3, AX.X, ALU.add).then_inc(gate_step, 1)
                dve.wait_ge(gate_step, 3 * g + 1)
                v.reciprocal(gm[:, 0:TILES], gm[:, TILES:2 * TILES]).then_inc(gate_step, 1)
                dve.wait_ge(gate_step, 3 * g + 2)
                v.tensor_tensor(gts[:, :].rearrange("p (t e) -> p t e", e=E), lge3,
                                gm[:, 0:TILES].unsqueeze(2).broadcast_to([QC, TILES, E]),
                                ALU.mult).then_inc(gate_step, 1)

            def gates(g, step, later):
                if step == "turn":
                    dve.wait_ge(gt_ps, g + 1)
                    if later:
                        dve.wait_ge(gate_out, 16 * g)
                    v.tensor_copy(two(gt_t[:, :]), halves(eo_ps)[0:E]).then_inc(gt_ready, 1)
                if step == "bias":
                    dve.wait_ge(b2_ps, g + 1)
                    if later:
                        dve.wait_ge(out_done, 16 * g)
                    v.tensor_tensor(two(acc), halves(fr_ps), tokens(g), ALU.add).then_inc(acc_init, 1)

            def experts(g, slot):
                n = g * SLOTS + slot
                dve.wait_ge(hid_ready, n + 1)
                if slot >= 3:
                    dve.wait_ge(chunk_used, n - 2)
                if slot % 2:
                    dve.wait_ge(hhi_act, g * (SLOTS // 2) + (slot + 1) // 2)
                else:
                    v.tensor_copy(hh[slot % 3], hid[slot % 2]).then_inc(hhi_dve, 1)
                    dve.wait_ge(hhi_dve, g * (SLOTS // 2) + slot // 2 + 1)
                v.tensor_tensor(hl[slot % 3], hid[slot % 2], hh[slot % 3], ALU.subtract).then_inc(hlo_ready, 1)

            def weigh(g, e):
                dve.wait_ge(chunk_used, g * SLOTS + (e + 1) * CH)
                dve.wait_ge(gate_in[e // (E // 2)], 16 * (g + 1))
                if e >= 2:
                    dve.wait_ge(acc_step, g * E + e - 1)
                v.tensor_tensor(two(tmp[e % 2]), halves(eo_ps), two(gbc[:, e * T:(e + 1) * T]),
                                ALU.mult).then_inc(tmp_ready, 1)

            def expert_slot(g, slot):
                if slot < SLOTS:
                    experts(g, slot)
                if slot >= LAG and (slot - LAG) % CH == CH - 1:
                    weigh(g, (slot - LAG) // CH)

            def ffn(g, successor=True, ahead=True, later=True):
                for slot in range(SLOTS + LAG):
                    expert_slot(g, slot)
                    if successor:
                        for step in steps_in(LN2_SLOTS, slot):
                            graph(g + 1, step)
                    for step in steps_in(GATE_SLOTS, slot):
                        gates(g, step, later)
                    if successor:
                        for step in steps_in(QK_SLOTS, slot):
                            queries_keys(g + 1, step)
                    if ahead:
                        for step in steps_in(EARLY_SLOTS, slot):
                            early(g + 2, step)

            for step in EARLY_SLOTS:
                early(0, step)
            for step in ("h2", "dev2", "roots2", "hx"):
                graph(0, step)
            for step in QK_SLOTS:
                queries_keys(0, step)
            for step in EARLY_SLOTS:
                early(1, step)
            attention(0, False, True)
            ffn(0, later=False)
            attention(1, True, True)
            with dve.Fori(2, G - 1) as g:
                ffn(g - 1)
                attention(g, True, True)
            ffn(G - 2, ahead=False)
            attention(G - 1, True, False)
            ffn(G - 1, successor=False, ahead=False)


def kernel(**inputs):
    import numpy as np
    import concourse.bacc as bacc
    from concourse.bass_utils import run_bass_kernel_spmd

    def a(name):
        return np.asarray(inputs[name])

    def pack(layout, parts):
        for name, n in layout.items():
            assert parts[name].shape == (128, n), name
        return np.ascontiguousarray(np.concatenate([parts[name] for name in layout], axis=1))

    x = a("x")
    framed = np.pad(x, ((0, 0), (0, 0), (HP, HP), (HP, HP)))
    cells = [np.ascontiguousarray(v.reshape(B, C, n, PATCH, n, PATCH).transpose(2, 1, 3, 5, 4, 0).reshape(n, KP, n * B))
             for v, n in ((framed, NG1), (x, NP))]

    def patches(v):
        return v.reshape(SHIFTS, C, NP, PATCH, NP, PATCH).transpose(1, 3, 5, 0, 2, 4).reshape(KP, -1)

    vectors = [a("L0_ffn_b1").reshape(-1, D), a("L0_tok_b"), a("L0_attn_bp"), a("L0_ffn_ln_g"), a("L0_ffn_ln_b"),
               a("cls_tok").reshape(1, D), np.tile(a("L0_ffn_qn_g"), H), np.tile(a("L0_ffn_kn_g"), H)]
    scalars = [a("L0_attn_W1").ravel(), a("L0_attn_b1"), a("L0_attn_W2").ravel(), a("L0_attn_b2")]
    pack_a = pack(PACK_A, {
        "gamma": patches(a("L0_tok_gamma")),
        "conv_w": a("L0_tok_W").reshape(D, SHIFTS, KP).transpose(2, 1, 0).reshape(KP, -1)})
    pack_b = pack(PACK_B, {
        "beta": patches(a("L0_tok_beta")),
        "cols": np.concatenate([v.reshape(-1, D) for v in vectors]).T,
        "scal": np.tile(np.concatenate(scalars), (128, 1)),
        "wp": a("L0_attn_Wp").reshape(D, D, 5).transpose(1, 2, 0).reshape(D, -1),
        "wv_t": a("L0_ffn_Wv").T, "wo": a("L0_ffn_Wo"), "wq": a("L0_ffn_Wq"), "wk": a("L0_ffn_Wk"),
        "gate_w": a("L0_ffn_gate_W"), "gate_b": np.tile(a("L0_ffn_gate_b"), (128, 1)),
        "b2": np.pad(a("L0_ffn_b2"), ((0, 128 - E), (0, 0)))})
    arrays = {
        "cells1": cells[0], "cells0": cells[1], "pack_a": pack_a, "pack_b": pack_b,
        "edge": np.ascontiguousarray(a("L0_attn_edge_index").reshape(2, 128, EK).transpose(1, 0, 2).reshape(128, -1)),
        "w1": np.ascontiguousarray(a("L0_ffn_W1").transpose(1, 0, 2).reshape(D, -1)),
        "w2": np.ascontiguousarray(a("L0_ffn_W2").reshape(SLOTS, D, D).transpose(1, 0, 2).reshape(D, -1))}

    nc = bacc.Bacc("TRN2", target_bir_lowering=False, num_devices=1)
    args = [nc.dram_tensor(n, v.shape, mybir.dt.from_np(v.dtype), kind="ExternalInput").ap() for n, v in arrays.items()]
    args.append(nc.dram_tensor("tower_out", (D, B * TOK), F32, kind="ExternalOutput").ap())
    vit_tower(nc, *args)
    r = run_bass_kernel_spmd(nc, [arrays], core_ids=[0])
    return np.ascontiguousarray(r.results[0]["tower_out"].reshape(D, B, TOK).transpose(1, 2, 0))
```

```python
from contextlib import ExitStack

import concourse.bass as bass
from concourse import mybir

F32 = mybir.dt.float32
F16 = mybir.dt.float16
I32 = mybir.dt.int32
ALU = mybir.AluOpType
ACT = mybir.ActivationFunctionType
AX = mybir.AxisListType

B, C, S = 64, 2, 104
HP, PATCH = 4, 8
NP = S // PATCH
FRAME = S + 2 * HP
NG1 = FRAME // PATCH
SHIFTS = 5
D = 128
TOK = NP * NP + 1
NB = 4
G = B // NB
T = NB * TOK
TH = T // 2
QC = TOK // 2
TILES = T // QC
H, DH = 2, 64
E, FF = 8, 512
CH = FF // D
SLOTS = E * CH
GATE_PARTS = ((0, 1), (1, 4), (4, E))
LAG = 3
NHID, NPART = 3, 4
EPS_TOK, EPS_LN, EPS_L2 = 1e-7, 1e-5, 1e-12
EDGES = 1024
EK = EDGES // 128
STAGE = E * FF // 2
AREA = 23800

LN2_SLOTS = {"hx": 3, "hx_lo": 3}
GATE_SLOTS = {"turn": 1, "turned": 0}
QK_SLOTS = {"q": 7, "k": 9, "sums": 15, "root0": 15, "root1": 15, "root2": 17, "kn": 22}
EARLY_SLOTS = {"fix0": 7, "fix1": 7, "fix2": 8, "fix3": 8, "tok_hi": 10, "mean": 13, "dev": 13, "sq": 14,
               "var": 17, "root0": 17, "root1": 19, "root2": 19, "xn": 23, "xn_lo": 24, "edges": 27,
               "relu0": 27, "relu1": 28, "relu2": 29, "relu3": 30}

RSQRT_SEED = 0x5F3759DF
W_ROW = 8
MASKED = -1e30
COUNT = C * SHIFTS * S * S
KP = C * PATCH * PATCH
R1, R0 = 4, 3
COL_B1, COL_TB, COL_BP, COL_LNG, COL_LNB, COL_CLS, COL_QN, COL_KN = 0, 32, 33, 34, 35, 36, 37, 38

PACK_A = {"gamma": SHIFTS * NP * NP, "conv_w": SHIFTS * D}
PACK_B = {"beta": SHIFTS * NP * NP, "cols": 39, "scal": 28, "wp": 5 * D, "wv_t": D, "wo": D,
          "wqk": 2 * D, "gate_w": E, "gate_b": E, "b2": E}


def vit_tower(nc, cells1, cells0, pack_a, pack_b, edge, w1, w2, out):
    with ExitStack() as ctx:
        def sb(name, shape, dt=F32):
            return ctx.enter_context(nc.sbuf_tensor(name, shape, dt))

        def sem(name):
            return ctx.enter_context(nc.semaphore(name))

        bank = [ctx.enter_context(nc.psum_tensor(f"pair{i}", [128, 2, 512], F32)) for i in range(4)]
        hid_ps = bank[0:2]
        eo_ps = bank[2]
        fr_ps = bank[3]

        def flat(pair):
            return pair[:, :, :].rearrange("p b n -> p (b n)")

        def halves(ps):
            return ps[:, :, 0:TH]

        def two(ap):
            return ap.rearrange("p (b n) -> p b n", b=2)

        ht = sb("ht", [128, B * TOK])
        ws = sb("ws", [128, 4 * SLOTS * D // 2])
        w1h, w1l, w2h, w2l = (ws[:, i * SLOTS * D // 2:(i + 1) * SLOTS * D // 2].bitcast(F16) for i in range(4))
        packs = {}
        for name, layout in (("pack_a", PACK_A), ("pack_b", PACK_B)):
            whole = sb(name + "_sb", [128, sum(layout.values())])
            packs[name] = whole
            o = 0
            for part, n in layout.items():
                packs[part] = whole[:, o:o + n]
                o += n
        gam, conv_w, beta, cols, scal = (packs[n] for n in ("gamma", "conv_w", "beta", "cols", "scal"))
        wp_t, wv_t, wo_s, wqk_s = (packs[n] for n in ("wp", "wv_t", "wo", "wqk"))
        gate_ws, gate_bs, b2_s = packs["gate_w"], packs["gate_b"][0:QC, :], packs["b2"]
        part_h, part_l = (packs["pack_a"][:, i * T // 2:(i + 1) * T // 2].bitcast(F16) for i in range(2))
        assert T <= PACK_A["gamma"]
        area = sb("area", [128, AREA])
        stage_all = sb("stage_sb", [128, STAGE])

        ident = sb("ident", [128, 128])
        ident16 = sb("ident16", [128, 128], F16)
        mean_m = sb("mean_m", [128, 128])
        mean_16 = sb("mean_16", [128, 128], F16)
        count_m = sb("count_m", [128, 128])
        head_m = sb("head_m", [128, 128])
        mask = sb("mask", [QC, QC], mybir.dt.bfloat16)
        identb = sb("identb", [QC, QC], mybir.dt.bfloat16)
        conv_u = sb("conv_u", [128, NP * NP])
        conv_b = sb("conv_b", [128, NP * NP])
        adj_t = sb("adj_t", [128, 128])
        adj_h, adj_l, plain_h, plain_l = (sb(n, [128, D], F16) for n in ("adj_h", "adj_l", "plain_h", "plain_l"))
        gcn_m = sb("gcn_m", [128, 4 * D])
        gcn_c = sb("gcn_c", [128, 1])
        wvo = sb("wvo", [128, H * D])
        wqk_h, wqk_l, wvo_h, wvo_l = (sb(n, [128, 2 * D], F16) for n in ("wqk_h", "wqk_l", "wvo_h", "wvo_l"))
        att_b = sb("att_b", [128, 4])
        gq = sb("gq", [128, 2])
        eps = sb("eps", [128, 4])
        edge_i = sb("edge_i", [128, 2 * EK], I32)
        edge_f = sb("edge_f", [128, 2 * EK])
        deg = sb("deg", [128, 4])
        stat = sb("stat", [128, 8 * B])
        img = sb("img", [128, 2 * B])
        root_in, root, root_t = (sb(n, [QC, 6 * TILES]) for n in ("root_in", "root", "root_t"))
        ROOTS = {"qk": slice(0, 4 * TILES), "ln1": slice(4 * TILES, 5 * TILES), "ln2": slice(5 * TILES, 6 * TILES)}
        rq = root[:, 0:2 * TILES]
        mx = sb("mx", [QC, NB * 4])
        nbias = sb("nbias", [QC, NB * 4])
        sm = sb("sm", [QC, NB * 4])
        rs = sb("rs", [QC, NB * 4])
        lg = sb("lg", [QC, TILES * E])
        lge = sb("lge", [QC, TILES * E])
        gts = sb("gts", [QC, TILES * E])
        gm = sb("gm", [QC, TILES * 2])
        gt_t = sb("gt_t", [E, T])
        root_dram = {kind: nc.dram_tensor(f"root_{kind}", (rows, T), F32, kind="Internal").ap()
                     for kind, rows in (("qk", H), ("ln1", 1), ("ln2", 1))}
        gate_dram = nc.dram_tensor("gate_scratch", (E, T), F32, kind="Internal").ap()

        at = [0]

        def take(n, whole=area):
            at[0] += n
            return whole[:, at[0] - n:at[0]]

        N1, N0 = NG1 * B, NP * B
        row1 = [take(N1) for _ in range(R1)]
        row0 = [take(N0) for _ in range(R0)]
        sq1 = [take(N1) for _ in range(2)]
        sq0 = [take(N0) for _ in range(2)]
        ax1, as1, ax0, as0 = take(N1), take(N1), take(N0), take(N0)
        xg = [[take(N0) for _ in range(SHIFTS)] for _ in range(2)]
        assert at[0] <= AREA

        at[0] = 0
        oh = take(2 * EK * D // 2, stage_all).bitcast(F16)
        iota_f, adj_n, adj = (take(D, stage_all) for _ in range(3))
        assert at[0] <= STAGE

        at[0] = 0
        dev, sq, h1 = take(T), take(T), take(4 * T)
        sqk, fix = h1[:, 0:T], h1[:, T:T + NB * NP * NP]
        xh, qs, kb, sqq = (take(T) for _ in range(4))
        xh_h, xh_l = take(T // 2).bitcast(F16), take(T // 2).bitcast(F16)
        w_at = at[0]
        hid = [take(T) for _ in range(NHID)]
        hh = [take(T // 2).bitcast(F16) for _ in range(NPART)]
        hl = [take(T // 2).bitcast(F16) for _ in range(NPART)]
        gbc = take(E * T)
        vp = gbc[0:QC, 0:NB * 512]
        probs = gbc[0:QC, NB * 512:NB * (512 + 6 * QC)]
        assert NB * (512 + 6 * QC) <= (E - 1) * T
        tmp = [take(T) for _ in range(2)]
        pt = [take(6 * QC) for _ in range(2)]
        ln_fac, k_fac = take(T), take(T)
        y32, acc = take(T), take(T)
        yh, yl = take(T // 2).bitcast(F16), take(T // 2).bitcast(F16)
        assert at[0] <= AREA, at[0]

        staged = [stage_all[:, :], area[:, w_at:w_at + STAGE], area[:, w_at + STAGE:w_at + 3 * STAGE]]

        consts_ready, pack_a_in, pack_b_in, edge_in = map(sem, ("consts_ready", "pack_a_in", "pack_b_in", "edge_in"))
        row1_in = [sem(f"row1_in{k}") for k in range(R1)]
        row0_in = [sem(f"row0_in{k}") for k in range(R0)]
        xsum_done, xsq_done, sqsum1_done, sqsum0_done = map(
            sem, ("xsum_done", "xsq_done", "sqsum1_done", "sqsum0_done"))
        fix_step, fixed = map(sem, ("fix_step", "fixed"))
        whi_done, wlo_done, oh_step = map(sem, ("whi_done", "wlo_done", "oh_step"))
        w_in = [sem(f"w_in{k}") for k in range(3)]
        pe_prep, act_prep, dve_prep, pool_prep = map(sem, ("pe_prep", "act_prep", "dve_prep", "pool_prep"))
        stat_step, act_stat, pe_stat, mul_done = map(sem, ("stat_step", "act_stat", "pe_stat", "mul_done"))
        conv_done, tok_done = map(sem, ("conv_done", "tok_done"))
        mean_ps, dev_ready, sq_ready, var_ps = map(sem, ("mean_ps", "dev_ready", "sq_ready", "var_ps"))
        var_out, root_ready, root_step, root_out, root_cast = (
            {kind: sem(f"{n}_{kind}") for kind in ROOTS}
            for n in ("var_out", "root_ready", "root_step", "root_out", "root_cast"))
        tokh_ready, tokl_ready, xn_ready, xnh_ready, xnl_ready = map(
            sem, ("tokh_ready", "tokl_ready", "xn_ready", "xnh_ready", "xnl_ready"))
        g_ps, h1_ready, gcn_ps, h2_ready = map(sem, ("g_ps", "h1_ready", "gcn_ps", "h2_ready"))
        mean2_ps, dev2_ready, sq2_ready, var2_ps = map(sem, ("mean2_ps", "dev2_ready", "sq2_ready", "var2_ps"))
        hx_ready, hxh_ready, hxl_ready, split_step = map(sem, ("hx_ready", "hxh_ready", "hxl_ready", "split_step"))
        q_ps, q_ready, k_ps, k_ready = map(sem, ("q_ps", "q_ready", "k_ps", "k_ready"))
        ss_ready, ss_ps, kn_ready = map(sem, ("ss_ready", "ss_ps", "kn_ready"))
        vp_ps, vp_ready, score_ps, max_ready = map(sem, ("vp_ps", "vp_ready", "score_ps", "max_ready"))
        nb_ready, exp_ready, rs_ready, p_ready = map(sem, ("nb_ready", "exp_ready", "rs_ready", "p_ready"))
        pt_ps, pt_ready, pv_ps, y_ready = map(sem, ("pt_ps", "pt_ready", "pv_ps", "y_ready"))
        yh_ready, yl_ready = map(sem, ("yh_ready", "yl_ready"))
        logit_ps, lg_step, lge_ready, gate_step = map(sem, ("logit_ps", "lg_step", "lge_ready", "gate_step"))
        gt_ps, gt_ready, gate_out = map(sem, ("gt_ps", "gt_ready", "gate_out"))
        gate_in = [sem(f"gate_in{n}") for n in range(len(GATE_PARTS))]
        hid_ps_ready, hid_ready, hhi_act, hhi_dve = map(sem, ("hid_ps_ready", "hid_ready", "hhi_act", "hhi_dve"))
        hlo_ready, chunk_used, tmp_ready, acc_step = map(sem, ("hlo_ready", "chunk_used", "tmp_ready", "acc_step"))
        out_done = sem("out_done")
        PREP_PE, PREP_ACT, PREP_DVE = 8, 9, 22

        def col(n):
            return cols[:, n:n + 1]

        def tokens(g):
            return two(ht[:, bass.ds(g * T, T)])

        SCORE = H * 3 * QC

        def score_at(h, c):
            return h * 3 * QC + c * QC, (c + 1) * QC

        def score_ps_at(b):
            return hid_ps[b // 2][0:QC, :, (b % 2) * 3 * QC:(b % 2 + 1) * 3 * QC]

        def hi_on_act(slot):
            return slot % CH > 0

        def his(g, slot):
            return g * (SLOTS - E) + len([n for n in range(slot) if hi_on_act(n)])

        def steps_in(slots, slot):
            return [step for step, n in slots.items() if n == slot]

        def conv_ps(p):
            return (fr_ps, eo_ps)[p % 2]

        def order1(a):
            return 2 * a - 1 if a else 0

        def order0(p):
            return 2 * p + 2

        block = ctx.enter_context(nc.Block())

        @block.sync
        def _(sp):
            def load1(a):
                if a >= R1:
                    sp.wait_ge(mul_done, SHIFTS * (a - R1 + 1))
                    sp.wait_ge(xsum_done, order1(a - R1) + 1)
                    sp.wait_ge(xsq_done, order1(a - R1) + 1)
                sp.dma_start(row1[a % R1], cells1[a]).then_inc(row1_in[a % R1], 16)

            def load0(p):
                if p >= R0:
                    sp.wait_ge(mul_done, SHIFTS * (p - R0 + 1))
                    sp.wait_ge(xsum_done, order0(p - R0) + 1)
                    sp.wait_ge(xsq_done, order0(p - R0) + 1)
                sp.dma_start(row0[p % R0], cells0[p]).then_inc(row0_in[p % R0], 16)

            load0(0)
            load1(1)
            load1(0)
            for p in range(1, NP):
                load1(p + 1)
                load0(p)
                if p == 1:
                    sp.dma_start(packs["pack_b"][:, :], pack_b).then_inc(pack_b_in, 16)
                if p == W_ROW:
                    sp.wait_ge(pe_prep, PREP_PE)
                    sp.wait_ge(dve_prep, PREP_DVE)
                    sp.dma_start(staged[0], w1[:, 0:STAGE]).then_inc(w_in[0], 16)
            sp.wait_ge(stat_step, 9)
            sp.dma_start(staged[1], w1[:, STAGE:2 * STAGE]).then_inc(w_in[1], 16)

            def gates(g, later=True):
                sp.wait_ge(gt_ready, g + 1)
                sp.dma_start(gate_dram, gt_t[:, :]).then_inc(gate_out, 16)
                sp.wait_ge(gate_out, 16 * (g + 1))
                if later:
                    sp.wait_ge(tmp_ready, g * E)
                for n, (e0, e1) in enumerate(GATE_PARTS):
                    sp.dma_start(gbc[:, e0 * T:e1 * T], gate_dram[e0:e1, :].rearrange("e t -> (e t)")
                                 .partition_broadcast(128)).then_inc(gate_in[n], 16)

            def store(g):
                sp.wait_ge(acc_step, E * (g + 1))
                sp.dma_start(out[:, bass.ds(g * T, T)], acc).then_inc(out_done, 16)

            def spread(g, kind, later=True):
                rows, dram = (H if kind == "qk" else 1), root_dram[kind]
                first = {"qk": 2 * TILES, "ln1": 4 * TILES, "ln2": 5 * TILES}[kind]
                sp.wait_ge(root_ready[kind], g + 1)
                for h in range(rows):
                    sp.dma_start(dram[h, :].rearrange("(t p) -> p t", p=QC),
                                 root[:, first + h:first + TILES * rows:rows],
                                 allow_slow_non_contiguous=True).then_inc(root_out[kind], 16)
                sp.wait_ge(root_out[kind], 16 * rows * (g + 1))
                if later:
                    sp.wait_ge({"qk": kn_ready, "ln1": hx_ready, "ln2": xn_ready}[kind], g)
                to, fp = (k_fac, DH) if kind == "qk" else (ln_fac, 128)
                for h in range(rows):
                    sp.dma_start(to[h * fp:(h + 1) * fp, :], dram[h, :].partition_broadcast(fp)
                                 ).then_inc(root_cast[kind], 16)

            spread(0, "ln1", later=False)
            sp.dma_start(staged[2], w2).then_inc(w_in[2], 16)
            spread(0, "ln2", later=False)
            spread(0, "qk", later=False)
            spread(1, "ln1")
            spread(1, "ln2")
            gates(0, later=False)
            with sp.Fori(1, G - 1) as g:
                spread(g, "qk")
                spread(g + 1, "ln1")
                store(g - 1)
                spread(g + 1, "ln2")
                gates(g)
            spread(G - 1, "qk")
            store(G - 2)
            gates(G - 1)
            store(G - 1)
            sp.wait_ge(out_done, 16 * G)

        @block.gpsimd
        def _(pool):
            pool.memset(ident[:, :], 0.0).then_inc(pool_prep, 1)
            pool.memset(mask[:, :], 0.0).then_inc(pool_prep, 1)
            pool.memset(head_m[:, :], 0.0).then_inc(pool_prep, 1)
            pool.iota(iota_f, [[1, D]], base=0, channel_multiplier=0,
                      allow_small_or_imprecise_dtypes=True).then_inc(pool_prep, 1)
            pool.memset(mean_m[:, :], 1.0 / D).then_inc(pool_prep, 1)
            pool.memset(count_m[:, :], 1.0 / COUNT).then_inc(pool_prep, 1)
            for n, v in enumerate((EPS_TOK, EPS_LN, EPS_LN * EPS_LN, EPS_L2)):
                pool.memset(eps[:, n:n + 1], v).then_inc(pool_prep, 1)
            pool.wait_ge(pool_prep, 10)
            for h in range(H):
                pool.memset(head_m[h * DH:(h + 1) * DH, h * DH:(h + 1) * DH], 1.0).then_inc(pool_prep, 1)
            pool.wait_ge(pool_prep, 12)
            pool.affine_select(out=ident[:, :], in_=ident[:, :], compare_op=ALU.not_equal, fill=1.0,
                               base=0, pattern=[[-1, 128]], channel_multiplier=1).then_inc(pool_prep, 1)
            pool.affine_select(out=mask[:, :], in_=mask[:, :], compare_op=ALU.is_ge, fill=MASKED,
                               base=0, pattern=[[-1, QC]], channel_multiplier=1).then_inc(pool_prep, 1)
            pool.memset(mean_16[:, :], 1.0 / D).then_inc(pool_prep, 1)
            pool.wait_ge(pool_prep, 15)
            pool.tensor_copy(ident16[:, :], ident[:, :]).then_inc(pool_prep, 1)
            pool.wait_ge(pool_prep, 16)
            pool.tensor_copy(identb[:, :], ident[0:QC, 0:QC]).then_inc(consts_ready, 1)
            n = 0
            for p in range(-1, NP):
                a = p + 1
                pool.wait_ge(row1_in[a % R1], 16 * (a // R1 + 1))
                if a == 0:
                    pool.tensor_scalar(ax1, row1[0], 0.5, None, ALU.mult).then_inc(xsum_done, 1)
                    continue
                pool.wait_ge(xsum_done, 2 * a - 1 if a > 1 else 1)
                if a < NP:
                    pool.tensor_tensor(ax1, ax1, row1[a % R1], ALU.add).then_inc(xsum_done, 1)
                else:
                    pool.wait_ge(sqsum1_done, NP)
                    pool.tensor_scalar(sq1[0], row1[a % R1], 0.5, None, ALU.mult).then_inc(xsum_done, 1)
                pool.wait_ge(row0_in[p % R0], 16 * (p // R0 + 1))
                if p == 0:
                    pool.tensor_copy(ax0, row0[0]).then_inc(xsum_done, 1)
                else:
                    pool.tensor_tensor(ax0, ax0, row0[p % R0], ALU.add).then_inc(xsum_done, 1)
                pool.wait_ge(xsq_done, order0(p) + 1)
                if p == 0:
                    pool.tensor_copy(as0, sq0[0]).then_inc(sqsum0_done, 1)
                else:
                    pool.wait_ge(sqsum0_done, p)
                    pool.tensor_tensor(as0, as0, sq0[p % 2], ALU.add).then_inc(sqsum0_done, 1)
            pool.wait_ge(xsum_done, 2 * NP + 1)
            pool.tensor_tensor(ax1, ax1, sq1[0], ALU.add).then_inc(xsum_done, 1)
            def tokens_lo(g):
                pool.wait_ge(tokh_ready, g + 1)
                pool.tensor_tensor(two(part_l), tokens(g), two(part_h), ALU.subtract).then_inc(tokl_ready, 1)

            tokens_lo(0)
            for i in range(2 * E):
                part, first = (i * FF // STAGE, i * FF % STAGE) if i < E else (2, (i - E) * FF)
                pool.wait_ge(w_in[part], 16)
                hi, lo = (w1h, w1l) if i < E else (w2h, w2l)
                w, src = slice((i % E) * FF, (i % E + 1) * FF), staged[part][:, first:first + FF]
                pool.tensor_copy(hi[:, w], src).then_inc(whi_done, 1)
                pool.wait_ge(whi_done, i + 1)
                pool.tensor_tensor(lo[:, w], src, hi[:, w], ALU.subtract).then_inc(wlo_done, 1)

            tokens_lo(1)

            def weigh(g, later=True, ahead=True):
                for e in range(E):
                    pool.wait_ge(tmp_ready, g * E + e + 1)
                    if e == 0:
                        if later:
                            pool.wait_ge(out_done, 16 * g)
                        pool.tensor_tensor(two(acc), two(tmp[0]), tokens(g), ALU.add).then_inc(acc_step, 1)
                        if ahead:
                            tokens_lo(g + 2)
                    else:
                        pool.wait_ge(acc_step, g * E + e)
                        pool.tensor_tensor(acc, acc, tmp[e % 2], ALU.add).then_inc(acc_step, 1)

            weigh(0, later=False)
            with pool.Fori(1, G - 2) as g:
                weigh(g)
            weigh(G - 2, ahead=False)
            weigh(G - 1, ahead=False)

        @block.scalar
        def _(act):
            act.dma_start(packs["pack_a"][:, :], pack_a).then_inc(pack_a_in, 16)
            act.dma_start(edge_i[:, :], edge).then_inc(edge_in, 16)

            def prep_evac(p):
                if p == 2:
                    act.wait_ge(pe_prep, 1)
                    nc.scalar.activation(conv_u[:, :], hid_ps[0][:, 0, 0:NP * NP], ACT.Copy).then_inc(act_prep, 1)
                    nc.scalar.activation(conv_b[:, :], hid_ps[0][:, 1, 0:NP * NP], ACT.Identity,
                                         bias=col(COL_TB)).then_inc(act_prep, 1)
                    act.wait_ge(dve_prep, 1)
                    nc.scalar.activation(deg[:, 1:2], deg[:, 0:1], ACT.Sqrt).then_inc(act_prep, 1)
                if p == 4:
                    act.wait_ge(pe_prep, 4)
                    nc.scalar.activation(adj, hid_ps[0][:, 0, 0:128], ACT.Copy).then_inc(act_prep, 1)
                if p == 5:
                    act.wait_ge(pe_prep, 6)
                    nc.scalar.activation(gcn_c[:, :], hid_ps[0][:, 0, 128:129], ACT.Identity,
                                         bias=col(COL_BP)).then_inc(act_prep, 1)
                    nc.scalar.activation(wvo[:, 0:D], hid_ps[0][:, 1, 0:D], ACT.Copy).then_inc(act_prep, 1)
                    nc.scalar.activation(wvo[:, D:2 * D], hid_ps[1][:, 1, 0:D], ACT.Copy).then_inc(act_prep, 1)
                if p == 6:
                    act.wait_ge(pe_prep, 8)
                    nc.scalar.activation(att_b[:, 0:3], hid_ps[0][:, 0, 256:259], ACT.Copy).then_inc(act_prep, 1)
                    act.wait_ge(dve_prep, PREP_DVE)
                    nc.scalar.activation(att_b[:, 3:4], hid_ps[0][:, 0, 256:257], ACT.Identity,
                                         scale=gq[:, 1:2]).then_inc(act_prep, 1)

            def squares1(a):
                act.wait_ge(row1_in[a % R1], 16 * (a // R1 + 1))
                if a >= 2:
                    act.wait_ge(sqsum1_done, a - 1)
                nc.scalar.activation(sq1[a % 2], row1[a % R1], ACT.Square).then_inc(xsq_done, 1)

            def squares0(p):
                act.wait_ge(row0_in[p % R0], 16 * (p // R0 + 1))
                if p >= 2:
                    act.wait_ge(sqsum0_done, p - 1)
                nc.scalar.activation(sq0[p % 2], row0[p % R0], ACT.Square).then_inc(xsq_done, 1)

            def tokens_out(p):
                act.wait_ge(conv_done, p + 1)
                dst = ht[:, :].rearrange("p (b t) -> p t b", t=TOK)[:, 1 + p * NP:1 + (p + 1) * NP, :]
                nc.scalar.activation(dst, flat(conv_ps(p))[:, 0:N0].rearrange("p (j b) -> p j b", b=B),
                                     ACT.Copy).then_inc(tok_done, 1)

            squares1(0)
            for p in range(NP):
                squares1(p + 1)
                squares0(p)
                if p:
                    tokens_out(p - 1)
                prep_evac(p)
            tokens_out(NP - 1)
            act.wait_ge(pack_b_in, 16)
            nc.scalar.activation(ht[:, :].rearrange("p (b t) -> p t b", t=TOK)[:, 0, :],
                                 col(COL_CLS).broadcast_to([128, B]), ACT.Copy).then_inc(tok_done, 1)
            act.wait_ge(stat_step, 14)
            nc.scalar.activation(stat[:, 5 * B:6 * B], stat[:, 4 * B:5 * B], ACT.Sqrt, bias=eps[:, 0:1]).then_inc(act_stat, 1)

            def var_evac(g, kind, ready, n, scale, at):
                act.wait_ge(ready, g + 1)
                nc.scalar.activation(root_in[:, ROOTS[kind]], fr_ps[0:QC, 0, 0:n], ACT.Identity,
                                     bias=eps[0:QC, at:at + 1], scale=scale).then_inc(var_out[kind], 1)

            def early(g, step):
                if step == "tok_hi":
                    act.wait_ge(fixed, NB * (g + 1))
                    nc.scalar.activation(two(part_h), tokens(g), ACT.Copy).then_inc(tokh_ready, 1)
                if step == "sq":
                    act.wait_ge(dev_ready, g + 1)
                    nc.scalar.activation(sq, dev, ACT.Square).then_inc(sq_ready, 1)
                if step == "var":
                    var_evac(g, "ln1", var_ps, TILES, 1.0, 1)
                if step[:4] == "relu":
                    c = int(step[4])
                    act.wait_ge(g_ps, g + 1)
                    nc.scalar.activation(two(h1[:, c * T:(c + 1) * T]), halves(fr_ps), ACT.Relu,
                                         bias=scal[:, 4 + c:5 + c], scale=scal[:, c:c + 1]).then_inc(h1_ready, 1)

            def graph(g, step):
                if step == "sq2":
                    act.wait_ge(dev2_ready, g + 1)
                    nc.scalar.activation(sq, dev, ACT.Square).then_inc(sq2_ready, 1)
                if step == "var2":
                    var_evac(g, "ln2", var2_ps, TILES, 1.0 + EPS_LN, 2)

            def queries_keys(g, step):
                if step == "q":
                    act.wait_ge(q_ps, g + 1)
                    nc.scalar.activation(two(sqq), halves(fr_ps), ACT.Square, bias=att_b[:, 0:1]).then_inc(ss_ready, 1)
                    nc.scalar.activation(two(qs), halves(fr_ps), ACT.Identity, bias=att_b[:, 3:4],
                                         scale=gq[:, 1:2]).then_inc(q_ready, 1)
                if step == "k":
                    act.wait_ge(k_ps, g + 1)
                    nc.scalar.activation(two(sqk), halves(fr_ps), ACT.Square, bias=att_b[:, 1:2]).then_inc(ss_ready, 1)
                    nc.scalar.activation(two(kb), halves(fr_ps), ACT.Identity, bias=att_b[:, 1:2]).then_inc(k_ready, 1)
                if step == "sums":
                    var_evac(g, "qk", ss_ps, 4 * TILES, 1.0, 3)

            def values_evac(g, b, later):
                act.wait_ge(vp_ps, g * NB + b + 1)
                if b == 0 and later:
                    act.wait_ge(tmp_ready, g * E - 1)
                nc.scalar.activation(vp[:, b * 512:(b + 1) * 512], hid_ps[b // 2][0:QC, b % 2, :],
                                     ACT.Copy).then_inc(vp_ready, 1)

            def exps(g, b):
                act.wait_ge(nb_ready, g * (NB // 2) + b // 2 + 1)
                for c in range(2):
                    for h in range(H):
                        n = 4 * b + 2 * c + h
                        o0, w = score_at(h, c)
                        nc.scalar.activation(probs[:, b * SCORE + o0:b * SCORE + o0 + w],
                                             score_ps_at(b)[:, h, c * QC:c * QC + w], ACT.Exp,
                                             bias=nbias[:, n:n + 1], scale=rq[:, n:n + 1],
                                             accum_out=sm[:, n:n + 1]).then_inc(exp_ready, 1)

            def y_evac(g, j):
                act.wait_ge(pv_ps, NB * g + 2 * (j + 1))
                nc.scalar.activation(y32[:, j * TH:(j + 1) * TH], hid_ps[0][:, j, 0:TH], ACT.Identity,
                                     bias=att_b[:, 2:3]).then_inc(y_ready, 1)

            def attention(g, later, ahead):
                for b in range(NB):
                    values_evac(g, b, later)
                for b in range(NB):
                    exps(g, b)
                y_evac(g, 0)
                if ahead:
                    graph(g + 1, "sq2")
                y_evac(g, 1)
                if ahead:
                    graph(g + 1, "var2")
                act.wait_ge(lg_step, 3 * (g + 1))
                nc.scalar.activation(lge[:, :], lg[:, :], ACT.Exp).then_inc(lge_ready, 1)

            def experts(g, slot):
                n = g * SLOTS + slot
                act.wait_ge(hid_ps_ready, n + 1)
                if slot >= NHID:
                    act.wait_ge(hlo_ready, n - NHID + 1)
                nc.scalar.activation(two(hid[slot % NHID]), halves(hid_ps[slot % 2]), ACT.Gelu_apprx_tanh,
                                     bias=col(COL_B1 + slot)).then_inc(hid_ready, 1)
                if hi_on_act(slot):
                    if slot >= NPART:
                        act.wait_ge(chunk_used, n - NPART + 1)
                    nc.scalar.activation(two(hh[slot % NPART]), halves(hid_ps[slot % 2]), ACT.Gelu_apprx_tanh,
                                         bias=col(COL_B1 + slot)).then_inc(hhi_act, 1)

            def ffn(g, ahead):
                for slot in range(SLOTS):
                    experts(g, slot)
                    for step in steps_in(LN2_SLOTS, slot):
                        graph(g + 1, step)
                    for step in steps_in(QK_SLOTS, slot):
                        queries_keys(g + 1, step)
                    if ahead:
                        for step in steps_in(EARLY_SLOTS, slot):
                            early(g + 2, step)

            for step in EARLY_SLOTS:
                early(0, step)
            for step in ("sq2", "var2"):
                graph(0, step)
            for slot in range(SLOTS):
                for step in steps_in(QK_SLOTS, slot):
                    queries_keys(0, step)
                for step in steps_in(EARLY_SLOTS, slot):
                    early(1, step)
            act.wait_ge(wlo_done, 2 * E)
            attention(0, False, True)
            with act.Fori(1, G - 1) as g:
                ffn(g - 1, True)
                attention(g, True, True)
            ffn(G - 2, False)
            attention(G - 1, True, False)
            for slot in range(SLOTS):
                experts(G - 1, slot)

        @block.tensor
        def _(pe):
            mm, tr = nc.tensor.matmul, nc.tensor.transpose
            pe.wait_ge(pack_a_in, 16)

            def prepare(p):
                if p == 1:
                    pe.wait_ge(consts_ready, 1)
                    pe.wait_ge(pack_b_in, 16)
                    for n, src in enumerate((gam, beta)):
                        for s in range(SHIFTS):
                            last = mm(hid_ps[0][:, n, 0:NP * NP], conv_w[:, s * D:(s + 1) * D],
                                      src[:, s * NP * NP:(s + 1) * NP * NP], start=(s == 0), stop=(s == SHIFTS - 1))
                    last.then_inc(pe_prep, 1)
                    pe.wait_ge(oh_step, 1 + 2 * EK)
                    for k in range(EK):
                        mm(hid_ps[1][:, 0, 0:D], oh[:, (EK + k) * D:(EK + k + 1) * D], oh[:, k * D:(k + 1) * D],
                           start=(k == 0), stop=False)
                    mm(hid_ps[1][:, 0, 0:D], ident16[:, :], ident16[:, :], start=False, stop=True).then_inc(pe_prep, 1)
                if p == 2:
                    pe.wait_ge(dve_prep, 3)
                    tr(hid_ps[1][:, 1, 0:D], adj_n, ident[:, :]).then_inc(pe_prep, 1)
                if p == 3:
                    pe.wait_ge(dve_prep, 4)
                    tr(hid_ps[0][:, 0, 0:D], adj_t[:, :], ident[:, :]).then_inc(pe_prep, 1)
                if p == 4:
                    pe.wait_ge(act_prep, 4)
                    mm(hid_ps[1][:, 0, :], adj, wp_t[:, D:5 * D], start=True, stop=True).then_inc(pe_prep, 1)
                    for k in range(4):
                        mm(hid_ps[0][:, 0, D:D + 1], wp_t[:, (k + 1) * D:(k + 2) * D], scal[:, 24 + k:25 + k],
                           start=(k == 0), stop=(k == 3))
                    for h in range(H):
                        last = mm(hid_ps[h][:, 1, 0:D], wv_t[h * DH:(h + 1) * DH, :],
                                  wo_s[h * DH:(h + 1) * DH, :], start=True, stop=True)
                    last.then_inc(pe_prep, 1)
                if p == 5:
                    pe.wait_ge(act_prep, 7)
                    mm(hid_ps[0][:, 0, 2 * D:2 * D + 1], wqk_s[:, 0:D], col(COL_LNB), start=True, stop=True)
                    mm(hid_ps[0][:, 0, 2 * D + 1:2 * D + 2], wqk_s[:, D:2 * D], col(COL_LNB), start=True, stop=True).then_inc(pe_prep, 1)
                    for h in range(H):
                        last = mm(hid_ps[0][:, 0, 2 * D + 2:2 * D + 3], wvo[:, h * D:(h + 1) * D], col(COL_LNB),
                                  start=(h == 0), stop=(h == H - 1))
                    last.then_inc(pe_prep, 1)

            def conv(p):
                if p >= 2:
                    pe.wait_ge(tok_done, p - 1)
                for s in range(SHIFTS):
                    pe.wait_ge(mul_done, SHIFTS * p + s + 1)
                    for a, b in ((0, 512), (512, N0)):
                        last = mm(flat(conv_ps(p))[:, a:b], conv_w[:, s * D:(s + 1) * D], xg[p % 2][s][:, a:b],
                                  start=(s == 0), stop=(s == SHIFTS - 1))
                last.then_inc(conv_done, 1)

            for p in range(NP):
                conv(p)
                prepare(p)
            pe.wait_ge(stat_step, 10)
            mm(hid_ps[0][:, 0, 0:2 * B], count_m[:, :], stat[:, 0:2 * B], start=True, stop=True).then_inc(pe_stat, 1)
            pe.wait_ge(tok_done, NP + 1)

            def both(lhs, rhs, start=True, stop=True):
                for j in range(2):
                    last = mm(fr_ps[:, j, 0:TH], lhs, rhs[:, j, :], start=start, stop=stop)
                return last

            def of_xn(w_hi, w_lo, stop=True):
                both(w_hi, two(part_h), stop=False)
                both(w_hi, two(part_l), start=False, stop=False)
                return both(w_lo, two(part_h), start=False, stop=stop)

            def means(src):
                for t in range(TILES):
                    last = mm(fr_ps[0:QC, 0, t:t + 1], src[:, t * QC:(t + 1) * QC], mean_m[:, 0:1],
                              start=True, stop=True)
                return last

            def early(g, step, later=True):
                if step == "mean":
                    pe.wait_ge(tokl_ready, g + 1)
                    if later:
                        pe.wait_ge(k_ready, g)
                    both(mean_16[:, :], two(part_h), stop=False)
                    both(mean_16[:, :], two(part_l), start=False).then_inc(mean_ps, 1)
                if step == "var":
                    pe.wait_ge(sq_ready, g + 1)
                    if later:
                        pe.wait_ge(var_out["qk"], g)
                    means(sq).then_inc(var_ps, 1)
                if step == "edges":
                    pe.wait_ge(xnl_ready, g + 1)
                    of_xn(adj_h[:, :], adj_l[:, :]).then_inc(g_ps, 1)

            def graph(g, step):
                if step == "plain":
                    pe.wait_ge(h1_ready, 4 * (g + 1))
                    of_xn(plain_h[:, :], plain_l[:, :], stop=False)
                if step in range(4):
                    last = both(gcn_m[:, step * D:(step + 1) * D], two(h1[:, step * T:(step + 1) * T]),
                                start=False, stop=(step == 3))
                    if step == 3:
                        last.then_inc(gcn_ps, 1)
                if step == "mean2":
                    pe.wait_ge(h2_ready, g + 1)
                    both(mean_m[:, :], tokens(g)).then_inc(mean2_ps, 1)
                if step == "var2":
                    pe.wait_ge(sq2_ready, g + 1)
                    means(sq).then_inc(var2_ps, 1)

            def of_hx(c):
                both(wqk_h[:, c:c + D], two(xh_h), stop=False)
                both(wqk_h[:, c:c + D], two(xh_l), start=False, stop=False)
                return both(wqk_l[:, c:c + D], two(xh_h), start=False)

            def queries_keys(g, step, ahead=True):
                if step == "q":
                    pe.wait_ge(hxl_ready, g + 1)
                    of_hx(0).then_inc(q_ps, 1)
                if step == "k":
                    pe.wait_ge(q_ready, g + 1)
                    of_hx(D).then_inc(k_ps, 1)
                if step == "sums":
                    pe.wait_ge(k_ready, g + 1)
                    pe.wait_ge(ss_ready, 2 * (g + 1))
                    if ahead:
                        pe.wait_ge(dev_ready, g + 2)
                    for n, src in enumerate((sqq, sqk)):
                        for t in range(TILES):
                            c = 2 * (n * TILES + t)
                            last = mm(fr_ps[0:QC, 0, c:c + 2], src[:, t * QC:(t + 1) * QC],
                                      head_m[:, 0:DH + 1:DH], start=True, stop=True)
                    last.then_inc(ss_ps, 1)

            def values(g, b, later):
                if b == 0 and later:
                    pe.wait_ge(hhi_act, his(g, 0) - 1)
                if b == 2 and later:
                    pe.wait_ge(hhi_act, his(g, 0))
                for k in range(2):
                    t = 2 * b + k
                    for n, (x_part, w_part) in enumerate(((xh_h, wvo_h), (xh_l, wvo_h), (xh_h, wvo_l))):
                        last = mm(hid_ps[b // 2][0:QC, b % 2, k * H * D:(k + 1) * H * D],
                                  x_part[:, t * QC:(t + 1) * QC], w_part[:, :], start=(n == 0), stop=(n == 2))
                last.then_inc(vp_ps, 1)

            def scores(g, b):
                if b == 0:
                    pe.wait_ge(kn_ready, g + 1)
                pe.wait_ge(vp_ready, g * NB + 2 * (b // 2) + 2)
                ps = score_ps_at(b)
                for h in range(H):
                    p = slice(h * DH, (h + 1) * DH)
                    for c in range(2):
                        w = (c + 1) * QC
                        mm(ps[:, h, c * QC:c * QC + w], qs[p, (2 * b + c) * QC:(2 * b + c + 1) * QC],
                           kb[p, b * TOK:b * TOK + w], start=True, stop=False)
                        last = mm(ps[:, h, c * QC + w - QC:c * QC + w], identb[:, :], mask[:, :], start=False, stop=True)
                last.then_inc(score_ps, 1)

            def turn_probs(g, b, later):
                pe.wait_ge(p_ready, g * NB + b + 1)
                if b >= 2:
                    pe.wait_ge(pt_ready, g * NB + b - 1)
                elif later:
                    pe.wait_ge(tmp_ready, g * E)
                for n in range(3 * H):
                    last = tr(eo_ps[0:QC, b % 2, n * QC:(n + 1) * QC],
                              probs[:, b * SCORE + n * QC:b * SCORE + (n + 1) * QC], ident[0:QC, 0:QC])
                last.then_inc(pt_ps, 1)

            def weigh(g, b):
                pe.wait_ge(pt_ready, g * NB + b + 1)
                for k in range(2):
                    for h in range(H):
                        v0 = b * 512 + k * H * D + h * D
                        p0 = h * 3 * QC + k * TOK
                        y0 = (b % 2) * TOK
                        last = mm(hid_ps[0][:, b // 2, y0 + k * QC:y0 + TOK], vp[:, v0:v0 + D],
                                  pt[b % 2][0:QC, p0:p0 + TOK - k * QC],
                                  start=(k == 0 and h == 0), stop=(k == 1 and h == H - 1))
                last.then_inc(pv_ps, 1)

            def gates(g, step):
                if step == "turn":
                    pe.wait_ge(gate_step, 3 * (g + 1))
                    for t in range(TILES):
                        b, m = t // NB, t % NB
                        last = tr(eo_ps[0:E, b, m * QC:(m + 1) * QC], gts[:, t * E:(t + 1) * E], ident[0:QC, 0:QC])
                    last.then_inc(gt_ps, 1)

            def attention(g, later, ahead):
                def graph_of(*steps):
                    if ahead:
                        for step in steps:
                            graph(g + 1, step)

                for b in range(LAG if later else 0, NB):
                    values(g, b, later)
                scores(g, 0)
                scores(g, 1)
                graph_of("plain", 0)
                scores(g, 2)
                scores(g, 3)
                graph_of(1, 2)
                turn_probs(g, 0, later)
                turn_probs(g, 1, later)
                graph_of(3)
                weigh(g, 0)
                turn_probs(g, 2, later)
                weigh(g, 1)
                turn_probs(g, 3, later)
                graph_of("mean2")
                weigh(g, 2)
                weigh(g, 3)
                graph_of("var2")
                pe.wait_ge(y_ready, 2 * (g + 1))
                pe.wait_ge(pt_ready, NB * (g + 1))
                for t in range(TILES):
                    last = mm(eo_ps[0:QC, 0, t * E:(t + 1) * E], y32[:, t * QC:(t + 1) * QC], gate_ws,
                              start=True, stop=True)
                last.then_inc(logit_ps, 1)

            def experts_in(g, slot):
                n = g * SLOTS + slot
                if slot == 0:
                    pe.wait_ge(yl_ready, 2 * (g + 1))
                elif slot >= 2 and hi_on_act(slot - 2):
                    pe.wait_ge(hhi_act, his(g, slot - 1))
                elif slot >= 2:
                    pe.wait_ge(hid_ready, n - 1)
                w = slice(slot * D, (slot + 1) * D)
                for i, (lhs, rhs) in enumerate(((w1h, yh), (w1h, yl), (w1l, yh))):
                    for j in range(2):
                        last = mm(hid_ps[slot % 2][:, j, 0:TH], lhs[:, w], rhs[:, j * TH:(j + 1) * TH],
                                  start=(i == 0), stop=(i == 2))
                last.then_inc(hid_ps_ready, 1)

            def experts_out(g, m):
                n = g * SLOTS + m
                pe.wait_ge(hlo_ready, n + 1)
                if m == 0:
                    pe.wait_ge(gt_ready, g + 1)
                if m and m % CH == 0:
                    pe.wait_ge(tmp_ready, g * E + m // CH)
                w = slice(m * D, (m + 1) * D)
                for i, (lhs, rhs) in enumerate(((w2h, hh[m % NPART]), (w2h, hl[m % NPART]), (w2l, hh[m % NPART]))):
                    for j in range(2):
                        last = mm(eo_ps[:, j, 0:TH], lhs[:, w], rhs[:, j * TH:(j + 1) * TH],
                                  start=(m % CH == 0 and i == 0), stop=(m % CH == CH - 1 and i == 2))
                last.then_inc(chunk_used, 1)

            def ffn(g, ahead):
                for slot in range(SLOTS + LAG):
                    if slot < SLOTS:
                        experts_in(g, slot)
                        for step in steps_in(LN2_SLOTS, slot):
                            graph(g + 1, step)
                        for step in steps_in(GATE_SLOTS, slot):
                            gates(g, step)
                        for step in steps_in(QK_SLOTS, slot):
                            queries_keys(g + 1, step, ahead=ahead)
                        if ahead:
                            for step in steps_in(EARLY_SLOTS, slot):
                                early(g + 2, step)
                    else:
                        values(g + 1, slot - SLOTS, True)
                    if slot >= LAG:
                        experts_out(g, slot - LAG)

            pe.wait_ge(split_step, 8)
            for step in EARLY_SLOTS:
                early(0, step, later=False)
            for step in ("plain", 0, 1, 2, 3, "mean2", "var2"):
                graph(0, step)
            for slot in range(SLOTS):
                for step in steps_in(QK_SLOTS, slot):
                    queries_keys(0, step)
                for step in steps_in(EARLY_SLOTS, slot):
                    early(1, step)
            attention(0, False, True)
            pe.wait_ge(wlo_done, 2 * E)
            with pe.Fori(1, G - 1) as g:
                ffn(g - 1, True)
                attention(g, True, True)
            ffn(G - 2, False)
            attention(G - 1, True, False)
            for slot in range(SLOTS + LAG):
                if slot < SLOTS:
                    experts_in(G - 1, slot)
                    for step in steps_in(GATE_SLOTS, slot):
                        gates(G - 1, step)
                if slot >= LAG:
                    experts_out(G - 1, slot - LAG)

        @block.vector
        def _(dve):
            v = nc.vector
            def prepare(p):
                if p == 0:
                    dve.wait_ge(consts_ready, 1)
                    dve.wait_ge(edge_in, 16)
                    v.tensor_copy(edge_f[:, :], edge_i[:, :]).then_inc(oh_step, 1)
                    dve.wait_ge(oh_step, 1)
                    for k in range(2 * EK):
                        v.tensor_scalar(oh[:, k * D:(k + 1) * D], iota_f, edge_f[:, k:k + 1], None,
                                        ALU.is_equal).then_inc(oh_step, 1)
                if p == 2:
                    dve.wait_ge(pe_prep, 2)
                    v.tensor_reduce(deg[:, 0:1], hid_ps[1][:, 0, 0:D], AX.X, ALU.add).then_inc(dve_prep, 1)
                    dve.wait_ge(act_prep, 3)
                    v.reciprocal(deg[:, 2:3], deg[:, 1:2]).then_inc(dve_prep, 1)
                    dve.wait_ge(dve_prep, 2)
                    v.tensor_scalar(adj_n, hid_ps[1][:, 0, 0:D], deg[:, 2:3], None, ALU.mult).then_inc(dve_prep, 1)
                if p == 3:
                    dve.wait_ge(pe_prep, 3)
                    v.tensor_scalar(adj_t[:, :], hid_ps[1][:, 1, 0:D], deg[:, 2:3], None, ALU.mult).then_inc(dve_prep, 1)
                if p == 5:
                    dve.wait_ge(pe_prep, 5)
                    for k in range(4):
                        src = hid_ps[1][:, 0, k * D:(k + 1) * D]
                        for c in range(4):
                            dst, w = gcn_m[:, c * D:(c + 1) * D], scal[:, 8 + 4 * c + k:9 + 4 * c + k]
                            if k == 0:
                                v.tensor_scalar(dst, src, w, None, ALU.mult).then_inc(dve_prep, 1)
                            else:
                                dve.wait_ge(dve_prep, 4 + 4 * (k - 1) + c + 1)
                                v.scalar_tensor_tensor(dst, src, w, dst, ALU.mult, ALU.add).then_inc(dve_prep, 1)
                    dve.wait_ge(act_prep, 7)
                    for n, (src, hi, lo) in enumerate((
                            (wqk_s, wqk_h, wqk_l), (wvo[:, :], wvo_h, wvo_l), (adj_t[:, :], adj_h, adj_l),
                            (wp_t[:, 0:D], plain_h, plain_l))):
                        v.tensor_copy(hi[:, :], src).then_inc(split_step, 1)
                        dve.wait_ge(split_step, 2 * n + 1)
                        v.tensor_tensor(lo[:, :], src, hi[:, :], ALU.subtract).then_inc(split_step, 1)
                    v.tensor_scalar(gq[:, 0:1], col(COL_QN), float(DH) ** 0.5, None, ALU.mult).then_inc(dve_prep, 1)
                    dve.wait_ge(dve_prep, 21)
                    v.tensor_tensor(gq[:, 1:2], gq[:, 0:1], col(COL_KN), ALU.mult).then_inc(dve_prep, 1)

            dve.wait_ge(pack_a_in, 16)
            gam_v = gam.rearrange("p (s i j) -> p s i j", s=SHIFTS, i=NP)

            def square_sum(a):
                dve.wait_ge(xsq_done, order1(a) + 1)
                if a == 0:
                    v.tensor_scalar(as1, sq1[0], 0.5, None, ALU.mult).then_inc(sqsum1_done, 1)
                else:
                    dve.wait_ge(sqsum1_done, a)
                    v.scalar_tensor_tensor(as1, sq1[a % 2], 0.5 if a == NP else 1.0, as1,
                                           ALU.mult, ALU.add).then_inc(sqsum1_done, 1)

            for p in range(NP):
                dve.wait_ge(row0_in[p % R0], 16 * (p // R0 + 1))
                if p >= 2:
                    dve.wait_ge(conv_done, p - 1)
                upper, lower = row1[p % R1], row1[(p + 1) % R1]
                for s, (src, c0) in enumerate(((row0[p % R0], 0), (lower, 0), (lower, 1), (upper, 0), (upper, 1))):
                    if s == 1:
                        dve.wait_ge(row1_in[(p + 1) % R1], 16 * ((p + 1) // R1 + 1))
                    if s == 3 and p == 0:
                        dve.wait_ge(row1_in[0], 16)
                    gv = gam_v[:, s, p, :].unsqueeze(2).broadcast_to([128, NP, B])
                    v.tensor_tensor(xg[p % 2][s].rearrange("p (j b) -> p j b", b=B),
                                    src[:, c0 * B:(c0 + NP) * B].rearrange("p (j b) -> p j b", b=B),
                                    gv, ALU.mult).then_inc(mul_done, 1)
                if p == 0:
                    square_sum(0)
                square_sum(p + 1)
                if p == 2:
                    dve.wait_ge(pack_b_in, 16)
                prepare(p)
            dve.wait_ge(xsum_done, 2 * NP + 2)
            dve.wait_ge(sqsum0_done, NP)
            dve.wait_ge(sqsum1_done, NG1)
            for n, (a1, a0) in enumerate(((ax1, ax0), (as1, as0))):
                s1, s0, side = (stat[:, k * B:(k + 1) * B] for k in (2 + n, 4 + n, 6 + n))
                v.tensor_reduce(s1, a1.rearrange("p (c b) -> p b c", b=B), AX.X, ALU.add).then_inc(stat_step, 1)
                v.tensor_reduce(s0, a0.rearrange("p (c b) -> p b c", b=B), AX.X, ALU.add).then_inc(stat_step, 1)
                v.tensor_tensor(side, a1[:, 0:B], a1[:, N1 - B:N1], ALU.add).then_inc(stat_step, 1)
            dve.wait_ge(stat_step, 6)
            v.scalar_tensor_tensor(stat[:, 4 * B:6 * B], stat[:, 2 * B:4 * B], 4.0, stat[:, 4 * B:6 * B],
                                   ALU.mult, ALU.add).then_inc(stat_step, 3)
            dve.wait_ge(stat_step, 9)
            v.scalar_tensor_tensor(stat[:, 0:2 * B], stat[:, 6 * B:8 * B], -2.0, stat[:, 4 * B:6 * B],
                                   ALU.mult, ALU.add).then_inc(stat_step, 1)
            dve.wait_ge(pe_stat, 1)
            v.tensor_copy(stat[:, 2 * B:3 * B], hid_ps[0][:, 0, 0:B]).then_inc(stat_step, 1)
            dve.wait_ge(stat_step, 11)
            v.tensor_tensor(stat[:, 3 * B:4 * B], stat[:, 2 * B:3 * B], stat[:, 2 * B:3 * B], ALU.mult).then_inc(stat_step, 1)
            dve.wait_ge(stat_step, 12)
            v.tensor_tensor(stat[:, 4 * B:5 * B], hid_ps[0][:, 0, B:2 * B], stat[:, 3 * B:4 * B],
                            ALU.subtract).then_inc(stat_step, 2)
            dve.wait_ge(act_stat, 1)
            v.reciprocal(img[:, 0:B], stat[:, 5 * B:6 * B]).then_inc(stat_step, 1)
            dve.wait_ge(stat_step, 15)
            v.scalar_tensor_tensor(img[:, B:2 * B], stat[:, 2 * B:3 * B], -1.0, img[:, 0:B],
                                   ALU.mult, ALU.mult).then_inc(stat_step, 1)
            dve.wait_ge(stat_step, 16)
            dve.wait_ge(act_prep, PREP_ACT)
            dve.wait_ge(tok_done, NP + 1)
            dve.wait_ge(conv_done, NP)

            def roots(g, kind, n):
                x, y, t = (buf[:, ROOTS[kind]] for buf in (root_in, root, root_t))
                if n == 0:
                    dve.wait_ge(var_out[kind], g + 1)
                    v.tensor_scalar(y.bitcast(I32), x.bitcast(I32), -0.5, float(RSQRT_SEED),
                                    ALU.mult, ALU.add).then_inc(root_step[kind], 1)
                dve.wait_ge(root_step[kind], 9 * g + 3 * n + 1)
                v.scalar_tensor_tensor(t, y, -0.5, y, ALU.mult, ALU.mult).then_inc(root_step[kind], 1)
                dve.wait_ge(root_step[kind], 9 * g + 3 * n + 2)
                v.tensor_tensor(t, t, x, ALU.mult).then_inc(root_step[kind], 1)
                dve.wait_ge(root_step[kind], 9 * g + 3 * n + 3)
                v.scalar_tensor_tensor(y, t, 1.5, y, ALU.add, ALU.mult).then_inc(
                    root_step[kind] if n < 2 else root_ready[kind], 1)

            def early(g, step):
                if step[:3] == "fix":
                    b = int(step[3])
                    fix_b, h_b = fix[:, b * NP * NP:(b + 1) * NP * NP], ht[:, bass.ds(g * T + (b * TOK + 1), NP * NP)]
                    v.scalar_tensor_tensor(fix_b, conv_u[:, :], img[:, bass.ds(g * NB + (B + b), 1)], conv_b[:, :],
                                           ALU.mult, ALU.add).then_inc(fix_step, 1)
                    dve.wait_ge(fix_step, NB * g + (b + 1))
                    v.scalar_tensor_tensor(h_b, h_b, img[:, bass.ds(g * NB + b, 1)], fix_b,
                                           ALU.mult, ALU.add).then_inc(fixed, 1)
                if step == "dev":
                    dve.wait_ge(mean_ps, g + 1)
                    v.tensor_tensor(two(dev), tokens(g), halves(fr_ps), ALU.subtract).then_inc(dev_ready, 1)
                if step[:4] == "root":
                    roots(g, "ln1", int(step[4]))
                if step == "xn":
                    dve.wait_ge(root_cast["ln1"], 16 * (g + 1))
                    v.tensor_tensor(dev, dev, ln_fac, ALU.mult).then_inc(xn_ready, 1)
                    dve.wait_ge(xn_ready, g + 1)
                    v.tensor_copy(part_h, dev).then_inc(xnh_ready, 1)
                if step == "xn_lo":
                    dve.wait_ge(xnh_ready, g + 1)
                    v.tensor_tensor(part_l, dev, part_h, ALU.subtract).then_inc(xnl_ready, 1)

            def graph(g, step):
                if step == "h2":
                    dve.wait_ge(gcn_ps, g + 1)
                    v.scalar_tensor_tensor(tokens(g), halves(fr_ps), gcn_c[:, 0:1], tokens(g),
                                           ALU.add, ALU.add).then_inc(h2_ready, 1)
                if step == "dev2":
                    dve.wait_ge(mean2_ps, g + 1)
                    dve.wait_ge(h2_ready, g + 1)
                    v.tensor_tensor(two(dev), tokens(g), halves(fr_ps), ALU.subtract).then_inc(dev2_ready, 1)
                if step == "roots2":
                    for n in range(3):
                        roots(g, "ln2", n)
                if step == "hx":
                    dve.wait_ge(root_cast["ln2"], 16 * (g + 1))
                    v.scalar_tensor_tensor(xh, dev, col(COL_LNG), ln_fac, ALU.mult, ALU.mult).then_inc(hx_ready, 1)
                    dve.wait_ge(hx_ready, g + 1)
                    v.tensor_copy(xh_h, xh).then_inc(hxh_ready, 1)
                if step == "hx_lo":
                    dve.wait_ge(hxh_ready, g + 1)
                    v.tensor_tensor(xh_l, xh, xh_h, ALU.subtract).then_inc(hxl_ready, 1)

            def queries_keys(g, step):
                if step[:4] == "root":
                    roots(g, "qk", int(step[4]))
                if step == "kn":
                    dve.wait_ge(root_cast["qk"], 16 * H * (g + 1))
                    v.tensor_tensor(kb, kb, k_fac, ALU.mult).then_inc(kn_ready, 1)

            def maxima(g, m):
                dve.wait_ge(score_ps, (g * (NB // 2) + m + 1) * 2)
                mx4 = mx[:, 8 * m:8 * m + 8].rearrange("p (i c h) -> p c i h", c=2, h=H)
                ps = hid_ps[m][0:QC, :, 0:2 * 3 * QC].rearrange("p h (i n) -> p i h n", i=2)
                for c in range(2):
                    v.tensor_reduce(mx4[:, c], ps[:, :, :, c * QC:(2 * c + 1) * QC],
                                    AX.X, ALU.max).then_inc(max_ready, 1)
                dve.wait_ge(max_ready, 2 * (g * (NB // 2) + m + 1))
                v.scalar_tensor_tensor(nbias[:, 8 * m:8 * m + 8], mx[:, 8 * m:8 * m + 8], -1.0,
                                       rq[:, 8 * m:8 * m + 8], ALU.mult, ALU.mult).then_inc(nb_ready, 1)

            def normalise(g, b):
                dve.wait_ge(exp_ready, 4 * (g * NB + b + 1))
                v.reciprocal(rs[:, 4 * b:4 * b + 4], sm[:, 4 * b:4 * b + 4]).then_inc(rs_ready, 1)
                dve.wait_ge(rs_ready, g * NB + b + 1)
                for c in range(2):
                    for h in range(H):
                        o0, w = score_at(h, c)
                        p = probs[:, b * SCORE + o0:b * SCORE + o0 + w]
                        n = 4 * b + 2 * c + h
                        last = v.tensor_scalar(p, p, rs[:, n:n + 1], None, ALU.mult)
                last.then_inc(p_ready, 1)

            def turned(g, b):
                dve.wait_ge(pt_ps, g * NB + b + 1)
                if b >= 2:
                    dve.wait_ge(pv_ps, g * NB + b - 1)
                v.tensor_copy(pt[b % 2][0:QC, :], eo_ps[0:QC, b % 2, 0:SCORE]).then_inc(pt_ready, 1)

            def y_parts(g, j):
                half = slice(j * TH, (j + 1) * TH)
                dve.wait_ge(y_ready, 2 * g + j + 1)
                v.tensor_copy(yh[:, half], y32[:, half]).then_inc(yh_ready, 1)
                dve.wait_ge(yh_ready, 2 * g + j + 1)
                v.tensor_tensor(yl[:, half], y32[:, half], yh[:, half], ALU.subtract).then_inc(yl_ready, 1)

            def attention(g, later, ahead):
                maxima(g, 0)
                maxima(g, 1)
                normalise(g, 0)
                normalise(g, 1)
                turned(g, 0)
                normalise(g, 2)
                turned(g, 1)
                normalise(g, 3)
                if ahead:
                    graph(g + 1, "h2")
                turned(g, 2)
                turned(g, 3)
                y_parts(g, 0)
                if ahead:
                    graph(g + 1, "dev2")
                y_parts(g, 1)
                dve.wait_ge(logit_ps, g + 1)
                lg3 = lg[:, :].rearrange("p (t e) -> p t e", e=E)
                v.tensor_tensor(lg3, eo_ps[0:QC, 0, 0:TILES * E].rearrange("p (t e) -> p t e", e=E),
                                gate_bs.unsqueeze(1).broadcast_to([QC, TILES, E]), ALU.add).then_inc(lg_step, 1)
                dve.wait_ge(lg_step, 3 * g + 1)
                v.tensor_reduce(gm[:, 0:TILES], lg3, AX.X, ALU.max).then_inc(lg_step, 1)
                dve.wait_ge(lg_step, 3 * g + 2)
                v.tensor_tensor(lg3, lg3, gm[:, 0:TILES].unsqueeze(2).broadcast_to([QC, TILES, E]),
                                ALU.subtract).then_inc(lg_step, 1)
                if ahead:
                    roots(g + 1, "ln2", 0)
                dve.wait_ge(lge_ready, g + 1)
                lge3 = lge[:, :].rearrange("p (t e) -> p t e", e=E)
                v.tensor_reduce(gm[:, TILES:2 * TILES], lge3, AX.X, ALU.add).then_inc(gate_step, 1)
                dve.wait_ge(gate_step, 3 * g + 1)
                v.reciprocal(gm[:, 0:TILES], gm[:, TILES:2 * TILES]).then_inc(gate_step, 1)
                dve.wait_ge(gate_step, 3 * g + 2)
                v.tensor_tensor(gts[:, :].rearrange("p (t e) -> p t e", e=E), lge3,
                                gm[:, 0:TILES].unsqueeze(2).broadcast_to([QC, TILES, E]),
                                ALU.mult).then_inc(gate_step, 1)
                if ahead:
                    roots(g + 1, "ln2", 1)
                    roots(g + 1, "ln2", 2)

            def gates(g, step, later):
                if step == "turned":
                    dve.wait_ge(gt_ps, g + 1)
                    if later:
                        dve.wait_ge(gate_out, 16 * g)
                    v.tensor_copy(two(gt_t[:, :]), halves(eo_ps)[0:E]).then_inc(gt_ready, 1)

            def experts(g, slot):
                n = g * SLOTS + slot
                dve.wait_ge(hid_ready, n + 1)
                if slot >= NPART:
                    dve.wait_ge(chunk_used, n - NPART + 1)
                if hi_on_act(slot):
                    dve.wait_ge(hhi_act, his(g, slot + 1))
                else:
                    v.tensor_copy(hh[slot % NPART], hid[slot % NHID]).then_inc(hhi_dve, 1)
                    dve.wait_ge(hhi_dve, g * E + slot // CH + 1)
                v.tensor_tensor(hl[slot % NPART], hid[slot % NHID], hh[slot % NPART], ALU.subtract).then_inc(hlo_ready, 1)

            def weigh(g, e):
                dve.wait_ge(chunk_used, g * SLOTS + (e + 1) * CH)
                part = [n for n, (e0, e1) in enumerate(GATE_PARTS) if e0 <= e < e1][0]
                dve.wait_ge(gate_in[part], 16 * (g + 1))
                if e >= 2:
                    dve.wait_ge(acc_step, g * E + e - 1)
                v.scalar_tensor_tensor(two(tmp[e % 2]), halves(eo_ps), b2_s[:, e:e + 1],
                                       two(gbc[:, e * T:(e + 1) * T]), ALU.add, ALU.mult).then_inc(tmp_ready, 1)

            def expert_slot(g, slot):
                if slot >= LAG and (slot - LAG) % CH == CH - 1:
                    weigh(g, (slot - LAG) // CH)
                if slot < SLOTS:
                    experts(g, slot)

            def ffn(g, successor=True, ahead=True, later=True):
                for slot in range(SLOTS + LAG):
                    expert_slot(g, slot)
                    for step in steps_in(GATE_SLOTS, slot):
                        gates(g, step, later)
                    if successor:
                        for step in steps_in(LN2_SLOTS, slot):
                            graph(g + 1, step)
                        for step in steps_in(QK_SLOTS, slot):
                            queries_keys(g + 1, step)
                    if ahead:
                        for step in steps_in(EARLY_SLOTS, slot):
                            early(g + 2, step)

            for step in EARLY_SLOTS:
                early(0, step)
            for step in ("h2", "dev2", "roots2", "hx", "hx_lo"):
                graph(0, step)
            for slot in range(SLOTS):
                for step in steps_in(QK_SLOTS, slot):
                    queries_keys(0, step)
                for step in steps_in(EARLY_SLOTS, slot):
                    early(1, step)
            attention(0, False, True)
            ffn(0, later=False)
            attention(1, True, True)
            with dve.Fori(2, G - 1) as g:
                ffn(g - 1)
                attention(g, True, True)
            ffn(G - 2, ahead=False)
            attention(G - 1, True, False)
            ffn(G - 1, successor=False, ahead=False)


def kernel(**inputs):
    import numpy as np
    import concourse.bacc as bacc
    from concourse.bass_utils import run_bass_kernel_spmd

    def a(name):
        return np.asarray(inputs[name])

    def pack(layout, parts):
        for name, n in layout.items():
            assert parts[name].shape == (128, n), name
        return np.ascontiguousarray(np.concatenate([parts[name] for name in layout], axis=1))

    x = a("x")
    framed = np.pad(x, ((0, 0), (0, 0), (HP, HP), (HP, HP)))
    cells = [np.ascontiguousarray(v.reshape(B, C, n, PATCH, n, PATCH).transpose(2, 1, 3, 5, 4, 0).reshape(n, KP, n * B))
             for v, n in ((framed, NG1), (x, NP))]

    def patches(v):
        return v.reshape(SHIFTS, C, NP, PATCH, NP, PATCH).transpose(1, 3, 5, 0, 2, 4).reshape(KP, -1)

    vectors = [a("L0_ffn_b1").reshape(-1, D), a("L0_tok_b"), a("L0_attn_bp"), a("L0_ffn_ln_g"), a("L0_ffn_ln_b"),
               a("cls_tok").reshape(1, D), np.tile(a("L0_ffn_qn_g"), H), np.tile(a("L0_ffn_kn_g"), H)]
    scalars = [a("L0_attn_W1").ravel(), a("L0_attn_b1"), a("L0_attn_W2").ravel(), a("L0_attn_b2")]
    pack_a = pack(PACK_A, {
        "gamma": patches(a("L0_tok_gamma")),
        "conv_w": a("L0_tok_W").reshape(D, SHIFTS, KP).transpose(2, 1, 0).reshape(KP, -1)})
    pack_b = pack(PACK_B, {
        "beta": patches(a("L0_tok_beta")),
        "cols": np.concatenate([v.reshape(-1, D) for v in vectors]).T,
        "scal": np.tile(np.concatenate(scalars), (128, 1)),
        "wp": a("L0_attn_Wp").reshape(D, D, 5).transpose(1, 2, 0).reshape(D, -1),
        "wv_t": a("L0_ffn_Wv").T, "wo": a("L0_ffn_Wo"), "wqk": np.concatenate([a("L0_ffn_Wq"), a("L0_ffn_Wk")], axis=1),
        "gate_w": a("L0_ffn_gate_W"), "gate_b": np.tile(a("L0_ffn_gate_b"), (128, 1)),
        "b2": a("L0_ffn_b2").T})
    arrays = {
        "cells1": cells[0], "cells0": cells[1], "pack_a": pack_a, "pack_b": pack_b,
        "edge": np.ascontiguousarray(a("L0_attn_edge_index").reshape(2, 128, EK).transpose(1, 0, 2).reshape(128, -1)),
        "w1": np.ascontiguousarray(a("L0_ffn_W1").transpose(1, 0, 2).reshape(D, -1)),
        "w2": np.ascontiguousarray(a("L0_ffn_W2").reshape(SLOTS, D, D).transpose(1, 0, 2).reshape(D, -1))}

    nc = bacc.Bacc("TRN2", target_bir_lowering=False, num_devices=1)
    args = [nc.dram_tensor(n, v.shape, mybir.dt.from_np(v.dtype), kind="ExternalInput").ap() for n, v in arrays.items()]
    args.append(nc.dram_tensor("tower_out", (D, B * TOK), F32, kind="ExternalOutput").ap())
    vit_tower(nc, *args)
    r = run_bass_kernel_spmd(nc, [arrays], core_ids=[0])
    return np.ascontiguousarray(r.results[0]["tower_out"].reshape(D, B, TOK).transpose(1, 2, 0))
```
